# Optimizing a Trainium2 kernel written in Bass

```python
import numpy as np
import jax
import jax.numpy as jnp

def _softmax(x, axis=-1):
    return jax.nn.softmax(x, axis=axis)

def _gelu(x):
    return jax.nn.gelu(x, approximate=True)

def _silu(x):
    return jax.nn.silu(x)

def _sigmoid(x):
    return jax.nn.sigmoid(x)

def _layernorm(x, axis=-1, eps=1e-05):
    m = jnp.mean(x, axis=axis, keepdims=True)
    v = jnp.var(x, axis=axis, keepdims=True)
    return (x - m) / jnp.sqrt(v + eps)

def _scatter_add(tgt, idx, src, axis=0):
    return tgt.at[idx].add(src)

def _segment_sum(src, seg, n):
    return jax.ops.segment_sum(src, seg, n)
kernel_name = 'mk_gnn_ffn_d2_gnn_r32_bd0fae'

def setup_inputs(seed: int=0):
    np.random.seed(seed)
    _w = jnp.asarray

    def _rec_inputs():
        import jax
        import jax.numpy as jnp
        _gk = jax.random.key(seed)
        x = -0.0003713 + 1 * jax.random.normal(jax.random.fold_in(_gk, 1), (3125, 256), jnp.float32)
        _s = jax.random.randint(jax.random.fold_in(_gk, 2), (25000,), 0, 3125, jnp.int32)
        _d = jax.random.randint(jax.random.fold_in(_gk, 3), (25000,), 0, 3125, jnp.int32)
        _loop = jnp.arange(3125, dtype=jnp.int32)
        src = jnp.concatenate([_s, _d, _loop])
        dst = jnp.concatenate([_d, _s, _loop])
        _o = jnp.argsort(dst, stable=True)
        src = src[_o]
        dst = dst[_o]
        edge_weight = jax.random.uniform(jax.random.fold_in(_gk, 13), (53125,), jnp.float32, 0.0, 1)
        return (x, src, dst, edge_weight)
    x, src, dst, edge_weight = _rec_inputs()

    def _L0_gnn_setup():
        import jax, jax.numpy as jnp
        import numpy as np
        N_NODES = 50000
        EMB = 256
        HEADS = 8
        NEG_SLOPE = 0.2

        def gat_conv(x, src, dst, W, a_src, a_dst, b, num_nodes):
            h = jnp.einsum('nd,dhf->nhf', x, W)
            al_s = jnp.sum(h * a_src, axis=-1)
            al_d = jnp.sum(h * a_dst, axis=-1)
            logits = jax.nn.leaky_relu(al_s[src] + al_d[dst], NEG_SLOPE)
            m = jax.ops.segment_max(logits, dst, num_segments=num_nodes)
            e = jnp.exp(logits - m[dst])
            z = jax.ops.segment_sum(e, dst, num_segments=num_nodes)
            alpha = e / (z[dst] + 1e-16)
            msg = h[src] * alpha[..., None]
            out = jax.ops.segment_sum(msg, dst, num_segments=num_nodes)
            return out.reshape(num_nodes, -1) + b
        key = jax.random.key(seed)
        ks = jax.random.split(key, 10)
        F1 = EMB // HEADS
        x = jax.random.normal(ks[0], (N_NODES, EMB), dtype=jnp.float32)
        edge_index = jax.random.randint(ks[1], (2, 25000), 0, N_NODES, dtype=jnp.int64)
        s1 = 1.0 / np.sqrt(EMB)
        W1 = jax.random.normal(ks[2], (EMB, HEADS, F1), dtype=jnp.float32) * s1
        a_src1 = jax.random.normal(ks[3], (HEADS, F1), dtype=jnp.float32) * s1
        a_dst1 = jax.random.normal(ks[4], (HEADS, F1), dtype=jnp.float32) * s1
        b1 = jnp.zeros((HEADS * F1,), dtype=jnp.float32)
        W2 = jax.random.normal(ks[5], (EMB, 1, EMB), dtype=jnp.float32) * s1
        a_src2 = jax.random.normal(ks[6], (1, EMB), dtype=jnp.float32) * s1
        a_dst2 = jax.random.normal(ks[7], (1, EMB), dtype=jnp.float32) * s1
        b2 = jnp.zeros((EMB,), dtype=jnp.float32)
        return {'x': x, 'edge_index': edge_index, 'W1': W1, 'a_src1': a_src1, 'a_dst1': a_dst1, 'b1': b1, 'W2': W2, 'a_src2': a_src2, 'a_dst2': a_dst2, 'b2': b2}
    _L0_gnn_all = _L0_gnn_setup()
    _L0_gnn_in = {k: v for k, v in _L0_gnn_all.items() if k in ('W1', 'a_src1', 'a_dst1', 'b1', 'W2', 'a_src2', 'a_dst2', 'b2')}
    del _L0_gnn_all

    def _L0_ffn_setup():
        import jax, jax.numpy as jnp
        import numpy as np
        B, T, D, H, E = (16, 128, 256, 512, 8)
        key = jax.random.key(seed)
        ks = jax.random.split(key, 5)
        x = jax.random.normal(ks[0], (B, T, D), dtype=jnp.float32)
        gate_w = jax.random.normal(ks[1], (D, E), dtype=jnp.float32) * 0.02
        gate_b = jnp.zeros((E,), dtype=jnp.float32)
        W1 = jax.random.normal(ks[2], (E, D, H), dtype=jnp.float32) * 0.02
        b1 = jnp.zeros((E, H), dtype=jnp.float32)
        W2 = jax.random.normal(ks[3], (E, H, D), dtype=jnp.float32) * 0.02
        b2 = jnp.zeros((E, D), dtype=jnp.float32)
        return {'x': x, 'gate_w': gate_w, 'gate_b': gate_b, 'W1': W1, 'b1': b1, 'W2': W2, 'b2': b2}
    _L0_ffn_all = _L0_ffn_setup()
    _L0_ffn_in = {k: v for k, v in _L0_ffn_all.items() if k in ('gate_w', 'gate_b', 'W1', 'b1', 'W2', 'b2')}
    del _L0_ffn_all

    def _L1_gnn_setup():
        import jax, jax.numpy as jnp
        import numpy as np
        N_NODES = 3125
        N_EDGES = 100000
        D_IN = 256
        D_OUT = 256
        key = jax.random.key(seed)
        k1, k2, k3, k4, k5, k6 = jax.random.split(key, 6)
        x = jax.random.normal(k1, (N_NODES, D_IN), dtype=jnp.float32)
        edge_val = jax.random.uniform(k2, (N_EDGES,), dtype=jnp.float32)
        stdv = 1.0 / np.sqrt(D_OUT)
        W = jax.random.uniform(k3, (D_IN, D_OUT), dtype=jnp.float32, minval=-stdv, maxval=stdv)
        b = jax.random.uniform(k4, (D_OUT,), dtype=jnp.float32, minval=-stdv, maxval=stdv)
        edge_row = jax.random.randint(k5, (N_EDGES,), 0, N_NODES, dtype=jnp.int32)
        edge_col = jax.random.randint(k6, (N_EDGES,), 0, N_NODES, dtype=jnp.int32)
        return {'x': x, 'edge_val': edge_val, 'W': W, 'b': b, 'edge_row': edge_row, 'edge_col': edge_col}
    _L1_gnn_all = _L1_gnn_setup()
    _L1_gnn_in = {k: v for k, v in _L1_gnn_all.items() if k in ('W', 'b')}
    del _L1_gnn_all

    def _L1_ffn_setup():
        import math
        import jax, jax.numpy as jnp
        import numpy as np
        CAPACITY_FACTOR = 1.25
        key = jax.random.key(seed)
        ks = jax.random.split(key, 5)
        B, L, D, F, E = (8, 256, 256, 1024, 8)
        h = jax.random.normal(ks[0], (B, L, D), dtype=jnp.float32)
        gate_w = jax.random.normal(ks[1], (D, E), dtype=jnp.float32) * 0.02
        gate_b = jnp.zeros((E,), dtype=jnp.float32)
        w1 = jax.random.normal(ks[2], (E, D, F), dtype=jnp.float32) * (1.0 / math.sqrt(D))
        b1 = jnp.zeros((E, F), dtype=jnp.float32)
        w2 = jax.random.normal(ks[3], (E, F, D), dtype=jnp.float32) * (1.0 / math.sqrt(F))
        b2 = jnp.zeros((E, D), dtype=jnp.float32)
        return {'h': h, 'gate_w': gate_w, 'gate_b': gate_b, 'w1': w1, 'b1': b1, 'w2': w2, 'b2': b2}
    _L1_ffn_all = _L1_ffn_setup()
    _L1_ffn_in = {k: v for k, v in _L1_ffn_all.items() if k in ('gate_w', 'gate_b', 'w1', 'b1', 'w2', 'b2')}
    del _L1_ffn_all
    return {'x': x, 'src': src, 'dst': dst, 'edge_weight': edge_weight, 'L0_gnn_W1': _L0_gnn_in['W1'], 'L0_gnn_a_src1': _L0_gnn_in['a_src1'], 'L0_gnn_a_dst1': _L0_gnn_in['a_dst1'], 'L0_gnn_b1': _L0_gnn_in['b1'], 'L0_gnn_W2': _L0_gnn_in['W2'], 'L0_gnn_a_src2': _L0_gnn_in['a_src2'], 'L0_gnn_a_dst2': _L0_gnn_in['a_dst2'], 'L0_gnn_b2': _L0_gnn_in['b2'], 'L0_ffn_gate_w': _L0_ffn_in['gate_w'], 'L0_ffn_gate_b': _L0_ffn_in['gate_b'], 'L0_ffn_W1': _L0_ffn_in['W1'], 'L0_ffn_b1': _L0_ffn_in['b1'], 'L0_ffn_W2': _L0_ffn_in['W2'], 'L0_ffn_b2': _L0_ffn_in['b2'], 'L1_gnn_W': _L1_gnn_in['W'], 'L1_gnn_b': _L1_gnn_in['b'], 'L1_ffn_gate_w': _L1_ffn_in['gate_w'], 'L1_ffn_gate_b': _L1_ffn_in['gate_b'], 'L1_ffn_w1': _L1_ffn_in['w1'], 'L1_ffn_b1': _L1_ffn_in['b1'], 'L1_ffn_w2': _L1_ffn_in['w2'], 'L1_ffn_b2': _L1_ffn_in['b2']}

def reference(x, src, dst, edge_weight, L0_gnn_W1, L0_gnn_a_src1, L0_gnn_a_dst1, L0_gnn_b1, L0_gnn_W2, L0_gnn_a_src2, L0_gnn_a_dst2, L0_gnn_b2, L0_ffn_gate_w, L0_ffn_gate_b, L0_ffn_W1, L0_ffn_b1, L0_ffn_W2, L0_ffn_b2, L1_gnn_W, L1_gnn_b, L1_ffn_gate_w, L1_ffn_gate_b, L1_ffn_w1, L1_ffn_b1, L1_ffn_w2, L1_ffn_b2):
    import jax
    import jax.numpy as jnp

    def _L0_gnn_ref(x, edge_index, W1, a_src1, a_dst1, b1, W2, a_src2, a_dst2, b2):
        import jax, jax.numpy as jnp
        import numpy as np
        N_NODES = 50000
        EMB = 256
        HEADS = 8
        NEG_SLOPE = 0.2

        def gat_conv(x, src, dst, W, a_src, a_dst, b, num_nodes):
            h = jnp.einsum('nd,dhf->nhf', x, W)
            al_s = jnp.sum(h * a_src, axis=-1)
            al_d = jnp.sum(h * a_dst, axis=-1)
            logits = jax.nn.leaky_relu(al_s[src] + al_d[dst], NEG_SLOPE)
            m = jax.ops.segment_max(logits, dst, num_segments=num_nodes)
            e = jnp.exp(logits - m[dst])
            z = jax.ops.segment_sum(e, dst, num_segments=num_nodes)
            alpha = e / (z[dst] + 1e-16)
            msg = h[src] * alpha[..., None]
            out = jax.ops.segment_sum(msg, dst, num_segments=num_nodes)
            return out.reshape(num_nodes, -1) + b
        n = x.shape[0]
        loops = jnp.arange(n, dtype=edge_index.dtype)
        src = jnp.concatenate([edge_index[0], loops])
        dst = jnp.concatenate([edge_index[1], loops])
        h = gat_conv(x, src, dst, W1, a_src1, a_dst1, b1, n)
        out = gat_conv(h, src, dst, W2, a_src2, a_dst2, b2, n)
        return out

    def _L0_ffn_ref(x, gate_w, gate_b, W1, b1, W2, b2):
        import jax, jax.numpy as jnp
        import numpy as np
        B, T, D, H, E = (16, 128, 256, 512, 8)
        Bb, Tt, Dd = x.shape
        Ee = gate_w.shape[1]
        xf = x.reshape(-1, Dd)
        N = xf.shape[0]
        logits = xf @ gate_w + gate_b
        probs = jax.nn.softmax(logits, axis=-1)
        top2_vals, top2_idx = jax.lax.top_k(probs, 2)
        cw = jnp.zeros((N, Ee), dtype=xf.dtype).at[jnp.arange(N)[:, None], top2_idx].add(top2_vals)

        def step(acc, params):
            w1, bb1, w2, bb2, we = params
            h = jax.nn.gelu(xf @ w1 + bb1, approximate=False)
            y = h @ w2 + bb2
            return (acc + we[:, None] * y, None)
        out, _ = jax.lax.scan(step, jnp.zeros_like(xf), (W1, b1, W2, b2, cw.T))
        return out.reshape(Bb, Tt, Dd)

    def _L1_gnn_ref(x, edge_val, W, b, edge_row, edge_col):
        import jax, jax.numpy as jnp
        import numpy as np
        N_NODES = 3125
        N_EDGES = 100000
        D_IN = 256
        D_OUT = 256
        support = jnp.matmul(x, W)
        gathered = support[edge_col] * edge_val[:, None]
        out = jax.ops.segment_sum(gathered, edge_row, num_segments=x.shape[0])
        return out + b

    def _L1_ffn_ref(h, gate_w, gate_b, w1, b1, w2, b2):
        import math
        import jax, jax.numpy as jnp
        import numpy as np
        CAPACITY_FACTOR = 1.25
        B, L, D = h.shape
        E = gate_w.shape[1]
        T = B * L
        C = max(1, math.ceil(CAPACITY_FACTOR * T / E))
        x = h.reshape(T, D)
        logits = x @ gate_w + gate_b
        probs = jax.nn.softmax(logits, axis=-1)
        idx = jnp.argmax(probs, axis=-1)
        prb = jnp.take_along_axis(probs, idx[:, None], axis=1)[:, 0]
        one_hot = jax.nn.one_hot(idx, E, dtype=jnp.float32)
        pos = (jnp.cumsum(one_hot, axis=0) * one_hot).sum(-1).astype(jnp.int32) - 1
        kept = pos < C
        pos_safe = jnp.where(kept, pos, C)
        buf = jnp.zeros((E, C, D), dtype=h.dtype).at[idx, pos_safe].set(x, mode='drop')
        hmid = jax.nn.relu(jnp.einsum('ecd,edf->ecf', buf, w1) + b1[:, None, :])
        ybuf = jnp.einsum('ecf,efd->ecd', hmid, w2) + b2[:, None, :]
        pos_g = jnp.minimum(pos, C - 1)
        y_tok = ybuf[idx, pos_g] * (prb * kept)[:, None]
        y = y_tok.reshape(B, L, D)
        y = jnp.nan_to_num(y, nan=0.0, posinf=10000.0, neginf=-10000.0)
        return y
    edge_index = jnp.stack([src, dst])
    x = x + _L0_gnn_ref(_layernorm(x, axis=-1), edge_index, L0_gnn_W1, L0_gnn_a_src1, L0_gnn_a_dst1, L0_gnn_b1, L0_gnn_W2, L0_gnn_a_src2, L0_gnn_a_dst2, L0_gnn_b2)
    x = x + _L0_ffn_ref(_layernorm(x, axis=-1)[None], L0_ffn_gate_w, L0_ffn_gate_b, L0_ffn_W1, L0_ffn_b1, L0_ffn_W2, L0_ffn_b2)[0]
    x = x + _L1_gnn_ref(_layernorm(x, axis=-1), edge_weight, L1_gnn_W, L1_gnn_b, src, dst)
    x = x + _L1_ffn_ref(_layernorm(x, axis=-1)[None], L1_ffn_gate_w, L1_ffn_gate_b, L1_ffn_w1, L1_ffn_b1, L1_ffn_w2, L1_ffn_b2)[0]
    return x

_drawn_inputs = setup_inputs


def setup_inputs(seed=0):
    import zlib

    import numpy as np

    out = dict(_drawn_inputs(seed))
    spreads = {'L0_gnn_b1': (0.0, 0.1),
     'L0_gnn_b2': (0.0, 0.1),
     'L0_ffn_gate_b': (0.0, 0.298),
     'L0_ffn_b1': (0.0, 0.651),
     'L0_ffn_b2': (0.0, 0.1),
     'L1_ffn_gate_b': (0.0, 0.1),
     'L1_ffn_b1': (0.0, 0.8),
     'L1_ffn_b2': (0.0, 0.79)}
    factors = {'L0_gnn_a_dst1': 5.874,
     'L0_gnn_a_src2': 2.715,
     'L0_gnn_a_dst2': 7.861,
     'L0_ffn_W1': 2.747,
     'L1_gnn_b': 2.835}
    for name, (base, spread) in spreads.items():
        noise = np.random.default_rng([zlib.crc32(name.encode()), seed]).standard_normal(out[name].shape)
        drawn = base * np.exp(spread * noise) if base else spread * noise
        out[name] = jnp.asarray(drawn.astype(out[name].dtype))
    for name, factor in factors.items():
        out[name] = (out[name] * factor).astype(out[name].dtype)
    return out
```

```python
from contextlib import ExitStack

import numpy as np
import concourse.bass as bass
from concourse import mybir

F32 = mybir.dt.float32
BF16 = mybir.dt.bfloat16
I32 = mybir.dt.int32
U8 = mybir.dt.uint8
ALU = mybir.AluOpType
ACT = mybir.ActivationFunctionType
AX = mybir.AxisListType

P = 128
N, D = 3125, 256
NT = -(-N // P)
NP = NT * P
E = 53125
ET = 416
EP = ET * P
CH, CI = 16, 26
CL = CI * P
SLOTS = 8
V = 440
DUMMY = NT
HEADS, HF = 8, 32
NEG = 0.2
EXPERTS = 8
F1 = 512
F2 = 1024
CAP = int(np.ceil(1.25 * N / EXPERTS))
CAPP = 512
BIG = 1e30
PAD_KEY = NP
EPS = 1e-5
KC = D // P
RG = -(-ET // P)
assert ET >= -(-E // P) and V >= ET + NT - 1 and V % SLOTS == 0 and CH * CI == ET


class Chain:

    def __init__(self, engine, sem):
        self.engine, self.sem, self.count = engine, sem, 0

    def link(self, instruction):
        self.count += 1
        instruction.then_inc(self.sem, 1)
        self.engine.wait_ge(self.sem, self.count)


def load_rows(sp, dst, src, count, sem):
    full = count // P
    whole = full // P
    n = 0
    if whole:
        sp.dma_start(dst[:, 0:whole, :], src[0:whole * P * P].rearrange("(g k e) -> k g e", k=P, e=P)).then_inc(sem, 16)
        n += 1
    left = full - whole * P
    if left:
        sp.dma_start(dst[0:left, whole, :], src[whole * P * P:full * P].rearrange("(k e) -> k e", e=P)).then_inc(sem, 16)
        n += 1
    rest = count - full * P
    if rest:
        sp.dma_start(dst[left:left + 1, whole, 0:rest], src[full * P:count].rearrange("(k e) -> k e", k=1)).then_inc(sem, 16)
        n += 1
    return n


class Graph:

    def __init__(self, nc):
        self.nc, self.numbers, self.at = nc, list(nc.free_semaphores), 0

    def semaphores(self, c):
        taken = []

        def sem(name):
            number = self.numbers[self.at % len(self.numbers)]
            taken.append(self.nc.alloc_semaphore(f"{name}_{self.at}", num=number))
            self.at += 1
            return taken[-1]

        c.callback(lambda: self.nc.clear_and_free_semaphores(taken))
        return sem


def constants(nc, g, ctx):
    sb = lambda n, s, d=F32: ctx.enter_context(nc.sbuf_tensor(n, s, d, allow_name_mangling=True))
    g.ident = sb("ident", [P, P])
    g.iota_row = sb("iota_row", [P, P])
    g.iota_col = sb("iota_col", [P, 1])
    g.iota25 = sb("iota25", [P, 32])
    g.falling = sb("falling", [P, EXPERTS])
    g.before = sb("before", [P, P])
    g.ones = sb("ones", [P, P])
    with ExitStack() as c:
        s_iota = g.semaphores(c)("s_iota")
        with nc.Block() as block:
            @block.gpsimd
            def _(pool):
                pool.iota(g.iota_row[:], [[1, P]], base=0, channel_multiplier=0, allow_small_or_imprecise_dtypes=True).then_inc(s_iota, 1)
                pool.iota(g.iota_col[:], [[0, 1]], base=0, channel_multiplier=1, allow_small_or_imprecise_dtypes=True).then_inc(s_iota, 1)
                pool.iota(g.iota25[:], [[1, 32]], base=0, channel_multiplier=0, allow_small_or_imprecise_dtypes=True).then_inc(s_iota, 1)

            @block.vector
            def _(dve):
                dve.memset(g.ones[:], 1.0)
                dve.wait_ge(s_iota, 3)
                dve.tensor_scalar(g.falling[:], g.iota25[:, 0:EXPERTS], -1.0, float(EXPERTS), ALU.mult, ALU.add)
                dve.tensor_scalar(g.ident[:], g.iota_row[:], g.iota_col[:, 0:1], None, ALU.is_equal)
                dve.tensor_scalar(g.before[:], g.iota_row[:], g.iota_col[:, 0:1], None, ALU.is_gt)


def graph_tables(nc, g, src, dst, w, ctx):
    sb = lambda n, s, d=F32: ctx.enter_context(nc.sbuf_tensor(n, s, d, allow_name_mangling=True))
    g.src_key = sb("src_key", [P, ET])
    g.dst_key = sb("dst_key", [P, ET])
    g.weight = sb("weight", [P, ET])
    g.is_last = sb("is_last", [P, ET])
    g.src_idx = sb("src_idx", [P, ET], I32)
    g.lo_dram = [nc.dram_tensor(f"lo_{n}", (EP,), BF16, kind="Internal").ap() for n in ("src", "dst")]
    with ExitStack() as c:
        rows = c.enter_context(nc.sbuf_tensor("rows", [P, 4, RG, P], I32, allow_name_mangling=True))
        rows_f = c.enter_context(nc.sbuf_tensor("rows_f", [P, 4, RG, P], F32, allow_name_mangling=True))
        lo = c.enter_context(nc.sbuf_tensor("lo", [P, 2, RG, P], I32, allow_name_mangling=True))
        lo_bf = c.enter_context(nc.sbuf_tensor("lo_bf", [P, 2, RG, P], BF16, allow_name_mangling=True))
        turned = c.enter_context(nc.psum_tensor("turned", [P, 4, 512], F32, allow_name_mangling=True))
        sem = g.semaphores(c)
        s_padded, s_rows, s_float, s_turned, s_low, s_out, s_chain = map(
            sem, ("s_padded", "s_rows", "s_float", "s_turned", "s_low", "s_out", "s_chain"))
        loads = [0]
        lists = ((src, E), (dst, E), (dst[1:E], E - 1), (w, E))
        with nc.Block() as block:
            @block.sync
            def _(sp):
                sp.wait_ge(s_padded, 4)
                for i, (a, count) in enumerate(lists):
                    into = rows[:, i] if i < 3 else rows_f[:, 3]
                    loads[0] += load_rows(sp, into, a, count, s_rows)
                sp.wait_ge(s_low, 2)
                for i in range(2):
                    o = g.lo_dram[i]
                    sp.dma_start(o[0:3 * P * P].rearrange("(g k e) -> k g e", k=P, e=P), lo_bf[:, i, 0:3, :]).then_inc(s_out, 16)
                    sp.dma_start(o[3 * P * P:EP].rearrange("(k e) -> k e", e=P), lo_bf[0:ET - 3 * P, i, 3, :]).then_inc(s_out, 16)
                sp.wait_ge(s_out, 64)

            @block.vector
            def _(dve):
                ch = Chain(dve, s_chain)
                dve.memset(rows[:, 0], PAD_KEY).then_inc(s_padded, 1)
                dve.memset(rows[:, 1], PAD_KEY).then_inc(s_padded, 1)
                dve.memset(rows[:, 2], PAD_KEY + 1).then_inc(s_padded, 1)
                dve.memset(rows_f[:, 3], 0.0).then_inc(s_padded, 1)
                dve.wait_ge(s_padded, 4)
                dve.wait_ge(s_rows, 16 * loads[0])
                dve.tensor_copy(rows_f[:, 0:3], rows[:, 0:3]).then_inc(s_float, 1)
                ch.link(dve.tensor_scalar(lo[:], rows[:, 0:2], P - 1, None, ALU.bitwise_and))
                dve.tensor_copy(lo_bf[:], lo[:]).then_inc(s_low, 2)
                dve.wait_ge(s_turned, 1)
                dve.tensor_copy(g.src_key[:], turned[:, 0, 0:ET])
                dve.tensor_copy(g.dst_key[:], turned[:, 1, 0:ET]).then_inc(s_chain, 1)
                dve.tensor_copy(g.weight[:], turned[:, 3, 0:ET])
                dve.tensor_scalar(g.src_idx[:], turned[:, 0, 0:ET], float(N - 1), None, ALU.min)
                dve.wait_ge(s_chain, 2)
                dve.tensor_tensor(g.is_last[:], turned[:, 2, 0:ET], g.dst_key[:], ALU.not_equal)

            @block.tensor
            def _(pe):
                pe.wait_ge(s_float, 1)
                for i in range(4):
                    for r in range(RG):
                        k = min(P, ET - r * P)
                        mm = pe.transpose(turned[:, i, r * P:r * P + k], rows_f[0:k, i, r, :], g.ident[0:k, 0:k])
                mm.then_inc(s_turned, 1)


def high_parts(nc, name, g, key, ctx):
    hot = ctx.enter_context(nc.sbuf_tensor(name, [P, ET, NT], U8))
    with ExitStack() as c:
        ki = c.enter_context(nc.sbuf_tensor("ki", [P, ET], I32, allow_name_mangling=True))
        hi = c.enter_context(nc.sbuf_tensor("hi", [P, ET], F32, allow_name_mangling=True))
        s = g.semaphores(c)("s_hi")
        with nc.Block() as block:
            @block.vector
            def _(dve):
                ch = Chain(dve, s)
                ch.link(dve.tensor_copy(ki[:], key[:]))
                ch.link(dve.tensor_scalar(ki[:], ki[:], 7, None, ALU.logical_shift_right))
                ch.link(dve.tensor_copy(hi[:], ki[:]))
                dve.tensor_tensor(hot[:], hi[:].unsqueeze(2).to_broadcast([P, ET, NT]),
                                  g.iota25[:, 0:NT].unsqueeze(1).to_broadcast([P, ET, NT]), ALU.is_equal)
    return hot


def visit_tables(nc, name, g, key, ctx):
    sb = lambda n, s, d=F32: ctx.enter_context(nc.sbuf_tensor(n, s, d, allow_name_mangling=True))
    table = sb(name + "_table", [1, 2, V], I32)
    minus = sb(name + "_minus", [P, V])
    ends = sb(name + "_ends", [P, NT])
    with ExitStack() as c:
        tb = lambda n, s, d=F32: c.enter_context(nc.sbuf_tensor(n, s, d, allow_name_mangling=True))
        part = tb("part", [P, NT])
        junk = tb("junk", [P, 2, ET], BF16)
        work = tb("work", [P, 8, NT])
        work_i = tb("work_i", [P, 2, NT], I32)
        past = tb("past", [P, V, NT])
        prod = tb("prod", [P, V, NT])
        vi = tb("vi", [P, V])
        tv = tb("tv", [P, V])
        kv = tb("kv", [P, V])
        total = c.enter_context(nc.psum_tensor("total", [P, NT], F32, allow_name_mangling=True))
        sem = g.semaphores(c)
        s_part, s_total, s_vi, s_chain = map(sem, ("s_part", "s_total", "s_vi", "s_chain"))
        with nc.Block() as block:
            @block.gpsimd
            def _(pool):
                pool.iota(vi[:], [[1, V]], base=0, channel_multiplier=0, allow_small_or_imprecise_dtypes=True).then_inc(s_vi, 1)

            @block.tensor
            def _(pe):
                pe.wait_ge(s_part, NT)
                pe.matmul(total[:], g.ones[:], part[:], start=True, stop=True).then_inc(s_total, 1)

            @block.vector
            def _(dve):
                ch = Chain(dve, s_chain)
                for t in range(NT):
                    if t >= 2:
                        dve.wait_ge(s_part, t - 1)
                    dve.tensor_scalar(junk[:, t % 2, :], key[:], float(P * (t + 1)), None, ALU.is_lt, ALU.add,
                                      accum_out=part[:, t:t + 1]).then_inc(s_part, 1)
                dve.wait_ge(s_total, 1)
                ch.link(dve.tensor_copy(ends[:], total[:]))
                ch.link(dve.memset(work[:], 0.0))
                start, first, last, nvis, vend, off, step = (work[:, i, :] for i in range(7))
                ch.link(dve.tensor_copy(start[:, 1:NT], ends[:, 0:NT - 1]))
                ch.link(dve.tensor_copy(work_i[:, 0, :], start))
                ch.link(dve.tensor_scalar(work_i[:, 1, :], ends[:], -1.0, 0.0, ALU.add, ALU.max))
                ch.link(dve.tensor_scalar(work_i[:], work_i[:], 7, None, ALU.logical_shift_right))
                ch.link(dve.tensor_copy(work[:, 1:3, :], work_i[:]))
                ch.link(dve.tensor_tensor(nvis, last, first, ALU.subtract))
                ch.link(dve.tensor_scalar(nvis, nvis, 1.0, None, ALU.add))
                ch.link(dve.tensor_tensor(off, ends[:], start, ALU.is_gt))
                ch.link(dve.tensor_tensor(nvis, nvis, off, ALU.mult))
                ch.link(dve.tensor_tensor_scan(vend, g.ones[:, 0:NT], nvis, 0.0, ALU.mult, ALU.add))
                ch.link(dve.tensor_tensor(off, first, vend, ALU.subtract))
                ch.link(dve.tensor_tensor(off, off, nvis, ALU.add))
                ch.link(dve.tensor_tensor(step[:, 0:NT - 1], off[:, 1:NT], off[:, 0:NT - 1], ALU.subtract))
                dve.wait_ge(s_vi, 1)
                shape = [P, V, NT]
                ch.link(dve.tensor_tensor(past[:], vi[:].unsqueeze(2).to_broadcast(shape),
                                          vend.unsqueeze(1).to_broadcast(shape), ALU.is_ge))
                ch.link(dve.tensor_reduce(tv[:], past[:], AX.X, ALU.add))
                ch.link(dve.tensor_tensor(prod[:], past[:], step.unsqueeze(1).to_broadcast(shape), ALU.mult))
                ch.link(dve.tensor_reduce(kv[:], prod[:], AX.X, ALU.add))
                ch.link(dve.tensor_tensor(kv[:], kv[:], vi[:], ALU.add))
                ch.link(dve.tensor_scalar(kv[:], kv[:], off[:, 0:1], 0.0, ALU.add, ALU.max))
                ch.link(dve.tensor_scalar(table[:, 0, :], kv[0:1, :], float(ET - 1), None, ALU.min))
                dve.tensor_copy(table[:, 1, :], tv[0:1, :])
                dve.tensor_scalar(minus[:], tv[:], -float(P), None, ALU.mult)
    return table, minus, ends


def normalise(nc, g, x, out, turned_out):
    with ExitStack() as c:
        tb = lambda n, s, d=F32: c.enter_context(nc.sbuf_tensor(n, s, d, allow_name_mangling=True))
        stats = tb("stats", [P, NT, 6])
        mv = tb("mv", [P, NT, 2])
        std = tb("std", [P, NT])
        rstd = tb("rstd", [P, NT])
        turn = [c.enter_context(nc.psum_tensor(f"turn{i}", [P, KC * P], F32, allow_name_mangling=True)) for i in range(4)]
        sem = g.semaphores(c)
        s_var, s_eps, s_std, s_norm, s_turn, s_copied, s_chain = map(
            sem, ("s_var", "s_eps", "s_std", "s_norm", "s_turn", "s_copied", "s_chain"))
        norm = x if out is None else out
        with nc.Block() as block:
            @block.vector
            def _(dve):
                if out is None:
                    dve.sem_inc(s_norm, NT)
                    return
                ch = Chain(dve, s_chain)
                for t in range(NT):
                    dve.bn_stats(stats[:, t, :], x[:, t, :]).then_inc(s_chain, 1)
                dve.wait_ge(s_chain, NT)
                for t in range(NT):
                    dve.bn_aggr(mv[:, t, :], stats[:, t, :]).then_inc(s_chain, 1)
                dve.wait_ge(s_chain, 2 * NT)
                dve.tensor_scalar(std[:], mv[:, :, 1], EPS, None, ALU.add).then_inc(s_var, 1)
                dve.wait_ge(s_std, 1)
                ch.count = 2 * NT
                ch.link(dve.reciprocal(rstd[:], std[:]))
                ch.link(dve.tensor_tensor(std[:], rstd[:], rstd[:], ALU.mult))
                ch.link(dve.scalar_tensor_tensor(std[:], mv[:, :, 1], EPS, std[:], ALU.add, ALU.mult))
                ch.link(dve.tensor_scalar(std[:], std[:], -0.5, 1.5, ALU.mult, ALU.add))
                ch.link(dve.tensor_tensor(rstd[:], rstd[:], std[:], ALU.mult))
                for t in range(NT):
                    dve.tensor_scalar(out[:, t, :], x[:, t, :], mv[:, t, 0:1], rstd[:, t:t + 1],
                                      ALU.subtract, ALU.mult).then_inc(s_norm, 1)

            @block.scalar
            def _(act):
                if out is not None:
                    act.wait_ge(s_var, 1)
                    act.activation(std[:], std[:], ACT.Sqrt).then_inc(s_std, 1)
                for t in range(NT):
                    act.wait_ge(s_turn, t + 1)
                    act.activation(turned_out[:, :, t * P:(t + 1) * P],
                                   turn[t % 4][:].rearrange("p (k n) -> p k n", k=KC), ACT.Copy).then_inc(s_copied, 1)

            @block.tensor
            def _(pe):
                for t in range(NT):
                    pe.wait_ge(s_norm, t + 1)
                    if t >= 4:
                        pe.wait_ge(s_copied, t - 3)
                    for k in range(KC):
                        mm = pe.transpose(turn[t % 4][:, k * P:(k + 1) * P], norm[:, t, k * P:(k + 1) * P], g.ident[:])
                    mm.then_inc(s_turn, 1)


def project(nc, g, name, turned, W, attention, heads, ctx):
    C = heads if attention else 0
    h = ctx.enter_context(nc.sbuf_tensor(name + "_h", [P, NT, D], F32, side="right"))
    al = ctx.enter_context(nc.sbuf_tensor(name + "_al", [P, NT, 2, max(C, 1)], F32, side="right"))
    table = nc.dram_tensor(name + "_table_dram", (NP, D), F32, kind="Internal").ap()
    with ExitStack() as c:
        tb = lambda n, s, d=F32: c.enter_context(nc.sbuf_tensor(n, s, d, allow_name_mangling=True))
        wcat = tb("wcat", [P, KC, D + 2 * C])
        wraw = tb("wraw", [P, KC, D])
        avec = tb("avec", [P, 2, D])
        prod = tb("prod_wa", [P, 2, KC, D])
        ps = [c.enter_context(nc.psum_tensor(f"proj{i}", [P, D + 2 * C], F32, allow_name_mangling=True)) for i in range(4)]
        sem = g.semaphores(c)
        s_w, s_chain, s_wcat, s_mm, s_h, s_out = map(sem, ("s_w", "s_chain", "s_wcat", "s_mm", "s_h", "s_out"))
        CHUNK = 5
        with nc.Block() as block:
            @block.sync
            def _(sp):
                flat_w = W.rearrange("(k p) h f -> p k (h f)", p=P) if len(W.shape) == 3 else W.rearrange("(k p) n -> p k n", p=P)
                sp.dma_start(wraw[:], flat_w).then_inc(s_w, 16)
                for i, a in enumerate(attention or ()):
                    sp.dma_start(avec[:, i, :], a.rearrange("(o h) f -> o (h f)", o=1).to_broadcast([P, D])).then_inc(s_w, 16)
                for j in range(0, NT, CHUNK):
                    sp.wait_ge(s_h, j + CHUNK)
                    sp.dma_start(table[j * P:(j + CHUNK) * P].rearrange("(t p) d -> p t d", p=P), h[:, j:j + CHUNK, :]).then_inc(s_out, 16)
                sp.wait_ge(s_out, 16 * (NT // CHUNK))

            @block.vector
            def _(dve):
                ch = Chain(dve, s_chain)
                dve.wait_ge(s_w, 48 if C else 16)
                dve.tensor_copy(wcat[:, :, 0:D], wraw[:]).then_inc(s_wcat, 1)
                for i in range(2 if C else 0):
                    ch.link(dve.tensor_tensor(prod[:, i], wraw[:], avec[:, i, :].unsqueeze(1).to_broadcast([P, KC, D]), ALU.mult))
                    for k in range(KC):
                        dve.tensor_reduce(wcat[:, k, D + i * C:D + (i + 1) * C],
                                          prod[:, i, k, :].rearrange("p (h f) -> p h f", h=C), AX.X, ALU.add).then_inc(s_wcat, 1)

            @block.tensor
            def _(pe):
                pe.wait_ge(s_wcat, 1 + 2 * KC if C else 1)
                for t in range(NT):
                    if t >= 4:
                        pe.wait_ge(s_h, t - 3)
                    for k in range(KC):
                        mm = pe.matmul(ps[t % 4][:], turned[:, k, t * P:(t + 1) * P], wcat[:, k, :], start=(k == 0), stop=(k == KC - 1))
                    mm.then_inc(s_mm, 1)

            @block.scalar
            def _(act):
                for t in range(NT):
                    act.wait_ge(s_mm, t + 1)
                    if C:
                        act.activation(al[:, t].rearrange("p s c -> p (s c)"), ps[t % 4][:, D:], ACT.Copy)
                    act.activation(h[:, t, :], ps[t % 4][:, 0:D], ACT.Copy).then_inc(s_h, 1)
    return h, al, table


def expand(nc, g, name, al, hots, heads, ctx):
    C = heads
    BT = 16
    TB = 2 if C > 1 else BT
    NB = BT // TB
    RING = 4
    ae = [ctx.enter_context(nc.sbuf_tensor(f"{name}_ae{s}", [P, ET, C], F32)) for s in range(2)]
    with ExitStack() as c:
        tb = lambda n, s, d=F32: c.enter_context(nc.sbuf_tensor(n, s, d, allow_name_mangling=True))
        rest = tb("rest", [P, 2, C, NT])
        part = [tb(f"part{j}", [P, 2, C, NT], BF16) for j in range(3)]
        lo_rows = [tb(f"lo_rows{s}", [P, BT * P], BF16) for s in range(2)]
        hot_lo = [tb(f"hot_lo{s}", [P, BT * P], BF16) for s in range(2)]
        sel = [tb(f"sel{r}", [P, TB, C, NT]) for r in range(RING)]
        ps = [c.enter_context(nc.psum_tensor(f"picked{r}", [P, TB, C, NT], F32, allow_name_mangling=True)) for r in range(RING)]
        sem = g.semaphores(c)
        s_chain, s_parts, s_hot, s_bank, s_sel, s_red = map(sem, ("s_chain", "s_parts", "s_hot", "s_bank", "s_sel", "s_red"))
        s_lo = [sem("s_lo0"), sem("s_lo1")]
        BLOCKS = ET // BT
        with nc.Block() as block:
            @block.sync
            def _(sp):
                with sp.Fori(0, BLOCKS) as i:
                    for s in range(2):
                        sp.wait_ge(s_hot, 2 * i)
                        sp.dma_start(lo_rows[s][:], g.lo_dram[s].rearrange("(o n) -> o n", o=1)[:, bass.ds(i * (BT * P), BT * P)]
                                     .to_broadcast([P, BT * P])).then_inc(s_lo[s], 16)

            @block.vector
            def _(dve):
                ch = Chain(dve, s_chain)
                ch.link(dve.tensor_copy(rest[:], al[:].rearrange("p t s c -> p s c t")))
                for j in range(3):
                    ch.link(dve.tensor_copy(part[j][:], rest[:]))
                    if j < 2:
                        ch.link(dve.tensor_tensor(rest[:], rest[:], part[j][:], ALU.subtract))
                dve.sem_inc(s_parts, 1)
                with dve.Fori(0, BLOCKS) as i:
                    for s in range(2):
                        dve.wait_ge(s_lo[s], 16 * i + 16)
                        dve.wait_ge(s_bank, 2 * NB * i)
                        dve.tensor_scalar(hot_lo[s][:], lo_rows[s][:], g.iota_col[:, 0:1], None, ALU.is_equal).then_inc(s_hot, 1)
                    for b in range(2 * NB + 1):
                        if b < 2 * NB:
                            s, r = b // NB, b % RING
                            dve.wait_ge(s_bank, 2 * NB * i + (b + 1))
                            dve.wait_ge(s_red, 2 * NB * i + max(0, b - RING + 1))
                            dve.tensor_tensor(sel[r][:], ps[r][:],
                                              hots[s][:, bass.ds(i * BT + (b % NB) * TB, TB), :].unsqueeze(2).to_broadcast([P, TB, C, NT]),
                                              ALU.mult).then_inc(s_sel, 1)
                        if b >= 1:
                            s, r = (b - 1) // NB, (b - 1) % RING
                            dve.wait_ge(s_sel, 2 * NB * i + b)
                            dve.tensor_reduce(ae[s][:, bass.ds(i * BT + ((b - 1) % NB) * TB, TB), :], sel[r][:], AX.X, ALU.add).then_inc(s_red, 1)

            @block.tensor
            def _(pe):
                pe.wait_ge(s_parts, 1)
                with pe.Fori(0, BLOCKS) as i:
                    for b in range(2 * NB):
                        s, r = b // NB, b % RING
                        if b % NB == 0:
                            pe.wait_ge(s_hot, 2 * i + s + 1)
                        pe.wait_ge(s_sel, 2 * NB * i + max(0, b - RING + 1))
                        for k in range(TB):
                            tile = (b % NB) * TB + k
                            for j in range(3):
                                mm = pe.matmul(ps[r][:, k].rearrange("p c t -> p (c t)"), hot_lo[s][:, tile * P:(tile + 1) * P],
                                               part[j][:, s].rearrange("p c t -> p (c t)"), start=(j == 0), stop=(j == 2))
                        mm.then_inc(s_bank, 1)
    return ae


def edge_softmax(nc, g, name, ae, dst, heads, ctx):
    C = heads
    R = CH * C
    ext = ctx.enter_context(nc.sbuf_tensor(name + "_ext", [P, ET, 2 * C + 1], F32, side="right"))
    with ExitStack() as c:
        tb = lambda n, s, d=F32: c.enter_context(nc.sbuf_tensor(n, s, d, allow_name_mangling=True))
        run = tb("run", [P, CL])
        d_i = run[0:R, :].bitcast(I32)
        d_all = tb("d_all", [P, CL])
        d_f = d_all[0:R, :]
        run = run[0:R, :]
        brk = tb("brk", [R, CL + 1])
        val = tb("val", [R, CL])
        most = d_all[:, 0:ET * C].rearrange("p (k c) -> p k c", c=C)
        ends = tb("ends_c", [R, 4])
        row = tb("row", [1, 4, R])
        hc = tb("hc", [1, 6, C, CH])
        back = tb("back", [R, 4])
        ps = [c.enter_context(nc.psum_tensor(f"sx{r}", [P, 4, P], F32, allow_name_mangling=True)) for r in range(4)]
        small = c.enter_context(nc.psum_tensor("small", [P, 512], F32, allow_name_mangling=True))
        sem = g.semaphores(c)
        s_pad, s_d, s_in, s_val, s_ends, s_row, s_back_row, s_back, s_run, s_out, s_most, s_logit, s_p, s_chain = map(sem, (
            "s_pad", "s_d", "s_in", "s_val", "s_ends", "s_row", "s_back_row", "s_back", "s_run", "s_out", "s_most", "s_logit", "s_p", "s_chain"))
        s_step = sem("s_step")
        by_step = ext[:].rearrange("p k x -> p (k x)")[:, 0:ET * C]
        G4 = -(-CI // 4)
        tail = E - (CH - 1) * CL
        ids = g.ident
        with nc.Block() as block:
            @block.sync
            def _(sp):
                sp.wait_ge(s_pad, 1)
                sp.dma_start(d_i[0:R - C, :], dst[0:(CH - 1) * CL].rearrange("(c n) -> c n", n=CL).unsqueeze(1).to_broadcast([CH - 1, C, CL])).then_inc(s_d, 16)
                sp.dma_start(d_i[R - C:R, 0:tail], dst[(CH - 1) * CL:E].rearrange("(o n) -> o n", o=1).to_broadcast([C, tail])).then_inc(s_d, 16)

            @block.tensor
            def _(pe):
                pe.wait_ge(s_step, 1)
                for q in range(G4):
                    if q >= 4:
                        pe.wait_ge(s_val, q - 3)
                    for i in range(4 * q, min(CI, 4 * q + 4)):
                        mm = pe.transpose(ps[q % 4][0:R, i % 4, :], by_step[:, i * R:(i + 1) * R], ids[:])
                    mm.then_inc(s_in, 1)
                pe.wait_ge(s_ends, 1)
                for i in range(4):
                    mm = pe.transpose(small[0:1, i * R:(i + 1) * R], ends[:, i:i + 1], ids[0:R, 0:R])
                mm.then_inc(s_row, 1)
                pe.wait_ge(s_back_row, 1)
                for i in range(4):
                    mm = pe.transpose(small[0:R, i:i + 1], row[0:1, i, :], ids[0:1, 0:1])
                mm.then_inc(s_back, 1)
                pe.wait_ge(s_run, 1)
                for q in range(G4):
                    if q >= 4:
                        pe.wait_ge(s_most, q - 3)
                    for i in range(4 * q, min(CI, 4 * q + 4)):
                        mm = pe.transpose(ps[q % 4][:, i % 4, 0:R], val[:, i * P:(i + 1) * P], ids[0:R, 0:R])
                    mm.then_inc(s_out, 1)

            @block.scalar
            def _(act):
                act.activation(by_step.rearrange("p (i c h) -> p i c h", c=CH, h=C),
                               ae[0][:].rearrange("p (c i) h -> p i c h", i=CI), ACT.Copy).then_inc(s_step, 1)
                for q in range(G4):
                    n = min(CI, 4 * q + 4) - 4 * q
                    act.wait_ge(s_in, q + 1)
                    act.activation(val[:, 4 * q * P:(4 * q + n) * P].rearrange("r (a b) -> r a b", b=P), ps[q % 4][0:R, 0:n, :], ACT.Copy).then_inc(s_val, 1)
                for q in range(G4):
                    n = min(CI, 4 * q + 4) - 4 * q
                    act.wait_ge(s_out, q + 1)
                    act.activation(most[:].rearrange("p (c i) h -> p i c h", i=CI)[:, 4 * q:4 * q + n],
                                   ps[q % 4][:, 0:n, 0:R].rearrange("p i (c h) -> p i c h", h=C), ACT.Copy).then_inc(s_most, 1)
                act.wait_ge(s_logit, 1)
                act.activation(ext[:, :, 0:C], ae[0][:], ACT.Exp).then_inc(s_p, 1)

            @block.vector
            def _(dve):
                ch = Chain(dve, s_chain)
                dve.memset(d_i[:], PAD_KEY).then_inc(s_pad, 1)
                ch.link(dve.memset(brk[:], -BIG))
                dve.wait_ge(s_d, 32)
                ch.link(dve.tensor_copy(d_f[:], d_i[:]))
                ch.link(dve.tensor_tensor(brk[:, 1:CL], d_f[:, 1:CL], d_f[:, 0:CL - 1], ALU.not_equal))
                ch.link(dve.tensor_scalar(brk[:, 1:CL], brk[:, 1:CL], -BIG, None, ALU.mult))
                dve.wait_ge(s_val, G4)
                ch.link(dve.tensor_tensor_scan(run[:], brk[:, 0:CL], val[:], 0.0, ALU.add, ALU.max))
                ch.link(dve.tensor_copy(ends[:, 0:1], run[:, CL - 1:CL]))
                ch.link(dve.tensor_tensor_scan(val[:, ::-1], brk[:, 1:CL + 1][:, ::-1], run[:, ::-1], 0.0, ALU.add, ALU.max))
                dve.tensor_copy(ends[:, 1:2], val[:, 0:1])
                dve.tensor_copy(ends[:, 2:3], d_f[:, CL - 1:CL])
                ch.link(dve.tensor_copy(ends[:, 3:4], d_f[:, 0:1]))
                dve.sem_inc(s_ends, 1)
                dve.wait_ge(s_row, 1)
                fend, mbeg, dlast, dfirst, wf, wb = (hc[:, i] for i in range(6))
                for i in range(4):
                    last = dve.tensor_copy(hc[:, i], small[0:1, i * R:(i + 1) * R].rearrange("o (c h) -> o h c", h=C))
                ch.link(last)
                dve.memset(wf[:, :, 0:1], 1.0)
                dve.memset(wb[:, :, CH - 1:CH], 1.0)
                dve.tensor_tensor(wf[:, :, 1:CH], dlast[:, :, 1:CH], dlast[:, :, 0:CH - 1], ALU.not_equal)
                ch.link(dve.tensor_tensor(wb[:, :, 0:CH - 1], dfirst[:, :, 1:CH], dfirst[:, :, 0:CH - 1], ALU.not_equal))
                ch.link(dve.tensor_scalar(hc[:, 4:6], hc[:, 4:6], -BIG, None, ALU.mult))
                one = lambda a: a.rearrange("o h c -> o (h c)")
                ch.link(dve.tensor_tensor_scan(one(fend), one(wf), one(fend), 0.0, ALU.add, ALU.max))
                ch.link(dve.tensor_tensor_scan(one(mbeg)[:, ::-1], one(wb)[:, ::-1], one(mbeg)[:, ::-1], 0.0, ALU.add, ALU.max))
                ch.link(dve.memset(row[:], -BIG))
                r4 = row[:].rearrange("o f (c h) -> o f c h", h=C)
                sw = lambda a: a.rearrange("o h c -> o c h")
                dve.tensor_copy(r4[:, 0, 1:CH], sw(fend)[:, 0:CH - 1])
                dve.tensor_copy(r4[:, 1, 0:CH - 1], sw(mbeg)[:, 1:CH])
                dve.tensor_copy(r4[:, 2, 1:CH], sw(dlast)[:, 0:CH - 1])
                ch.link(dve.tensor_copy(r4[:, 3, 0:CH - 1], sw(dfirst)[:, 1:CH]))
                dve.sem_inc(s_back_row, 1)
                dve.wait_ge(s_back, 1)
                ch.link(dve.tensor_copy(back[:], small[0:R, 0:4]))
                for j in range(2):
                    ch.link(dve.tensor_scalar(run[:], d_f[:], back[:, 2 + j:3 + j], -BIG, ALU.not_equal, ALU.mult))
                    ch.link(dve.scalar_tensor_tensor(val[:], run[:], back[:, j:j + 1], val[:], ALU.add, ALU.max))
                dve.sem_inc(s_run, 1)
                lo = ae[0][:]
                ch.link(dve.tensor_tensor(lo, ae[0][:], ae[1][:], ALU.add))
                ch.link(dve.scalar_tensor_tensor(lo, lo, NEG, lo, ALU.mult, ALU.max))
                dve.wait_ge(s_most, G4)
                dve.tensor_copy(ext[:, :, 2 * C:2 * C + 1], g.is_last[:].unsqueeze(2))
                dve.tensor_tensor(ext[:, :, C:2 * C], most[:], g.is_last[:].unsqueeze(2).to_broadcast([P, ET, C]), ALU.mult)
                ch.link(dve.tensor_tensor(ae[1][:], most[:], ae[1][:], ALU.add))
                ch.link(dve.scalar_tensor_tensor(ae[1][:], ae[1][:], NEG, ae[1][:], ALU.mult, ALU.max))
                ch.link(dve.tensor_tensor(lo, lo, ae[1][:], ALU.subtract))
                dve.sem_inc(s_logit, 1)
    return ext


def aggregate(nc, g, name, table, idx, key, visits, scale, heads, ext, acc):
    vt, minus = visits
    X = ext.shape[2] if ext is not None else 0
    W = D + X
    with ExitStack() as c:
        tb = lambda n, s, d=F32: c.enter_context(nc.sbuf_tensor(n, s, d, allow_name_mangling=True))
        idx_now = [tb(f"idx_now{u}", [P, 1], I32) for u in range(SLOTS)]
        rows = [tb(f"rows{u}", [P, D]) for u in range(SLOTS)]
        msg = [tb(f"msg{u}", [P, D]) for u in range(SLOTS)]
        hot = [tb(f"hot{u}", [P, P]) for u in range(SLOTS)]
        ps = [c.enter_context(nc.psum_tensor(f"sum{u}", [P, W], F32, allow_name_mangling=True)) for u in range(SLOTS)]
        sem = g.semaphores(c)
        s_go, s_act, s_idx, s_msg, s_sum, s_acc, s_hot = map(sem, ("s_go", "s_act", "s_idx", "s_msg", "s_sum", "s_acc", "s_hot"))
        s_rows = [sem(f"s_rows{u}") for u in range(SLOTS)]
        ROUNDS = V // SLOTS
        eng = mybir.EngineType
        def of_round(which, row, i):
            _, values = nc.values_load_multi_w_load_instructions(
                vt[0:1, row, bass.ds(i * SLOTS, SLOTS)], engines=(which,), min_val=0, max_val=(ET - 1, DUMMY)[row],
                skip_runtime_bounds_check_because="the table's values are clamped where it is made")
            return values
        with nc.Block() as block:
            @block.gpsimd
            def _(pool):
                with pool.Fori(0, ROUNDS) as i:
                    for u in range(SLOTS):
                        pool.wait_ge(s_idx, SLOTS * i + (u + 1))
                        pool.wait_ge(s_msg, SLOTS * i + (u + 1))
                        pool.sem_inc(s_go, 1)
                        pool.indirect_dma_start(out=rows[u][:], out_offset=None, in_=table,
                                                in_offset=bass.IndirectOffsetOnAxis(ap=idx_now[u][:], axis=0)).then_inc(s_rows[u], 16)

            @block.scalar
            def _(act):
                with act.Fori(0, ROUNDS) as i:
                    ks = of_round(eng.Activation, 0, i)
                    for u in range(SLOTS):
                        act.wait_ge(s_rows[u], 16 * i)
                        act.sem_inc(s_act, 1)
                        act.activation(idx_now[u][:], idx[:, bass.ds(ks[u], 1)], ACT.Copy).then_inc(s_idx, 1)

            @block.vector
            def _(dve):
                dve.memset(acc[:], 0.0).then_inc(s_acc, 1)
                dve.sem_inc(s_msg, SLOTS)
                def add(i, u, ts):
                    dve.wait_ge(s_sum, SLOTS * i + (u + 1))
                    dve.wait_ge(s_acc, SLOTS * i + (u + 1))
                    into = acc[:, bass.ds(ts[u], 1), :].rearrange("p o w -> p (o w)")
                    dve.tensor_tensor(into, ps[u][:], into, ALU.add).then_inc(s_acc, 1)
                with dve.Fori(0, ROUNDS) as i:
                    ks, ts = of_round(eng.DVE, 0, i), of_round(eng.DVE, 1, i)
                    for u in range(SLOTS):
                        if u == 0:
                            dve.wait_ge(s_sum, SLOTS * i)
                        dve.tensor_scalar(hot[u][:], g.iota_row[:], key[:, bass.ds(ks[u], 1)], minus[:, bass.ds(SLOTS * i + u, 1)],
                                          ALU.subtract, ALU.is_equal).then_inc(s_hot, 1)
                        dve.wait_ge(s_rows[u], 16 * i + 16)
                        if heads == 1:
                            dve.tensor_scalar(msg[u][:], rows[u][:], scale(ks[u]), None, ALU.mult).then_inc(s_msg, 1)
                        else:
                            dve.tensor_tensor(msg[u][:].rearrange("p (h f) -> p h f", h=heads), rows[u][:].rearrange("p (h f) -> p h f", h=heads),
                                              scale(ks[u]), ALU.mult).then_inc(s_msg, 1)
                        if u >= 2:
                            add(i, u - 2, ts)
                    add(i, SLOTS - 2, ts)
                    add(i, SLOTS - 1, ts)

            @block.tensor
            def _(pe):
                with pe.Fori(0, ROUNDS) as i:
                    if ext is not None:
                        ks = of_round(eng.PE, 0, i)
                    for u in range(SLOTS):
                        pe.wait_ge(s_msg, SLOTS * i + (u + 1 + SLOTS))
                        pe.wait_ge(s_hot, SLOTS * i + (u + 1))
                        if u == 0:
                            pe.wait_ge(s_acc, SLOTS * i + 1)
                        mm = pe.matmul(ps[u][:, 0:D], hot[u][:], msg[u][:], start=True, stop=True)
                        if ext is not None:
                            mm = pe.matmul(ps[u][:, D:W], hot[u][:], ext[:, bass.ds(ks[u], 1), :].rearrange("p o x -> p (o x)"),
                                           start=False, stop=True, skip_group_check=True)
                        mm.then_inc(s_sum, 1)


def finish_attention(nc, g, acc, h, al, bias, heads, x):
    C = heads
    with ExitStack() as c:
        tb = lambda n, s, d=F32: c.enter_context(nc.sbuf_tensor(n, s, d, allow_name_mangling=True))
        b_row = tb("b_row", [P, D])
        w = tb("w_fin", [P, 7, NT, C])
        sem = g.semaphores(c)
        s_b, s_chain, s_logit, s_exp, s_coef, s_own, s_num = map(sem, ("s_b", "s_chain", "s_logit", "s_exp", "s_coef", "s_own", "s_num"))
        own, near, top, den, c_near, c_own, spare = (w[:, i] for i in range(7))
        heads_of = lambda a: a.rearrange("p t (h f) -> p t h f", h=C)
        over = lambda a: a.unsqueeze(3).to_broadcast([P, NT, C, D // C])
        sums = acc[:, 0:NT, 0:D]
        with nc.Block() as block:
            @block.sync
            def _(sp):
                sp.dma_start(b_row[:], bias.rearrange("(o d) -> o d", o=1).to_broadcast([P, D])).then_inc(s_b, 16)

            @block.vector
            def _(dve):
                ch = Chain(dve, s_chain)
                ch.link(dve.tensor_scalar(spare, acc[:, 0:NT, D + 2 * C:].to_broadcast([P, NT, C]), -1.0, BIG, ALU.add, ALU.mult))
                ch.link(dve.tensor_tensor(near, acc[:, 0:NT, D + C:D + 2 * C], spare, ALU.add))
                ch.link(dve.tensor_tensor(near, near, al[:, :, 1, :], ALU.add))
                ch.link(dve.tensor_tensor(own, al[:, :, 0, :], al[:, :, 1, :], ALU.add))
                ch.link(dve.scalar_tensor_tensor(w[:, 0:2], w[:, 0:2], NEG, w[:, 0:2], ALU.mult, ALU.max))
                ch.link(dve.tensor_tensor(top, own, near, ALU.max))
                ch.link(dve.tensor_tensor(w[:, 0:2], w[:, 0:2], top.unsqueeze(1).to_broadcast([P, 2, NT, C]), ALU.subtract))
                dve.sem_inc(s_logit, 1)
                dve.wait_ge(s_exp, 1)
                ch.link(dve.tensor_tensor(den, acc[:, 0:NT, D:D + C], near, ALU.mult))
                ch.link(dve.tensor_tensor(den, den, own, ALU.add))
                ch.link(dve.tensor_scalar(den, den, 1e-16, None, ALU.add))
                ch.link(dve.reciprocal(spare, den))
                ch.link(dve.tensor_tensor(c_own, own, spare, ALU.mult))
                dve.sem_inc(s_coef, 1)
                ch.link(dve.tensor_tensor(c_near, near, spare, ALU.mult))
                ch.link(dve.tensor_tensor(heads_of(sums), heads_of(sums), over(c_near), ALU.mult))
                if x is not None:
                    ch.link(dve.tensor_tensor(x[:], x[:], sums, ALU.add))
                dve.wait_ge(s_own, 2)
                into = x[:] if x is not None else sums
                dve.tensor_tensor(into, into, h[:], ALU.add)

            @block.scalar
            def _(act):
                act.wait_ge(s_logit, 1)
                act.activation(w[:, 0:2], w[:, 0:2], ACT.Exp).then_inc(s_exp, 1)

            @block.gpsimd
            def _(pool):
                pool.wait_ge(s_coef, 1)
                pool.tensor_tensor(heads_of(h[:]), heads_of(h[:]), over(c_own), ALU.mult).then_inc(s_own, 1)
                pool.wait_ge(s_own, 1)
                pool.wait_ge(s_b, 16)
                pool.tensor_tensor(h[:], h[:], b_row[:].unsqueeze(1).to_broadcast([P, NT, D]), ALU.add).then_inc(s_own, 1)


def by_source(nc, g, hot, ends, ctx):
    sb = lambda n, s, d=F32: ctx.enter_context(nc.sbuf_tensor(n, s, d, allow_name_mangling=True))
    g.spot = sb("spot", [P, ET], I32)
    g.list_dram = nc.dram_tensor("list_dram", (EP, 4), F32, kind="Internal").ap()
    with ExitStack() as c:
        tb = lambda n, s, d=F32: c.enter_context(nc.sbuf_tensor(n, s, d, allow_name_mangling=True))
        rank = tb("rank", [P, NT, ET])
        total = tb("total", [P, NT])
        base = tb("base", [P, NT])
        place = tb("place", [P, ET])
        number = tb("number", [P, ET])
        ps = c.enter_context(nc.psum_tensor("base_ps", [P, NT], F32, allow_name_mangling=True))
        sem = g.semaphores(c)
        s_number, s_scan, s_total, s_base, s_chain = map(sem, ("s_number", "s_scan", "s_total", "s_base", "s_chain"))
        with nc.Block() as block:
            @block.gpsimd
            def _(pool):
                pool.iota(number[:], [[P, ET]], base=0, channel_multiplier=1, allow_small_or_imprecise_dtypes=True).then_inc(s_number, 1)

            @block.tensor
            def _(pe):
                pe.wait_ge(s_total, 1)
                pe.matmul(ps[:], g.before[:], total[:], start=True, stop=True).then_inc(s_base, 1)

            @block.vector
            def _(dve):
                ch = Chain(dve, s_chain)
                for t in range(NT):
                    dve.tensor_tensor_scan(rank[:, t, :], g.ones[:, 0:1].to_broadcast([P, ET]), hot[:, :, t], 0.0,
                                           ALU.mult, ALU.add).then_inc(s_scan, 1)
                dve.wait_ge(s_scan, NT)
                dve.tensor_copy(total[:], rank[:, :, ET - 1]).then_inc(s_total, 1)
                dve.wait_ge(s_base, 1)
                ch.link(dve.tensor_scalar(base[:], ps[:], -1.0, None, ALU.add))
                ch.link(dve.tensor_tensor(base[:, 1:NT], base[:, 1:NT], ends[:, 0:NT - 1], ALU.add))
                ch.link(dve.tensor_tensor(rank[:], rank[:], base[:].unsqueeze(2).to_broadcast([P, NT, ET]), ALU.add))
                ch.link(dve.tensor_tensor(rank[:], rank[:], hot[:].rearrange("p k t -> p t k"), ALU.mult))
                ch.link(dve.tensor_reduce(place[:], rank[:].rearrange("p t k -> p k t"), AX.X, ALU.add))
                dve.wait_ge(s_number, 1)
                ch.link(dve.scalar_tensor_tensor(number[:], g.src_key[:], float(NP), number[:], ALU.is_ge, ALU.mult))
                ch.link(dve.tensor_tensor(g.spot[:], place[:], number[:], ALU.add))


def read_list(nc, g, ctx):
    sb = lambda n, s, d=F32: ctx.enter_context(nc.sbuf_tensor(n, s, d, allow_name_mangling=True))
    idx = sb("l_idx", [P, ET], I32)
    key = sb("l_key", [P, ET])
    weight = sb("l_weight", [P, ET])
    with ExitStack() as c:
        rows = c.enter_context(nc.sbuf_tensor("l_rows", [P, RG, P, 4], F32, allow_name_mangling=True))
        ps = c.enter_context(nc.psum_tensor("l_turned", [P, 3, 512], F32, allow_name_mangling=True))
        s_rows, s_turned = map(g.semaphores(c), ("s_rows", "s_turned"))
        with nc.Block() as block:
            @block.sync
            def _(sp):
                o = g.list_dram
                sp.dma_start(rows[:, 0:3], o[0:3 * P * P].rearrange("(g k e) f -> k g e f", k=P, e=P)).then_inc(s_rows, 16)
                sp.dma_start(rows[0:ET - 3 * P, 3], o[3 * P * P:EP].rearrange("(k e) f -> k e f", e=P)).then_inc(s_rows, 16)

            @block.tensor
            def _(pe):
                pe.wait_ge(s_rows, 32)
                for f in range(3):
                    for r in range(RG):
                        k = min(P, ET - r * P)
                        mm = pe.transpose(ps[:, f, r * P:r * P + k], rows[0:k, r, :, f], g.ident[0:k, 0:k])
                mm.then_inc(s_turned, 1)

            @block.vector
            def _(dve):
                dve.wait_ge(s_turned, 1)
                dve.tensor_scalar(idx[:], ps[:, 0, 0:ET], float(N - 1), None, ALU.min)
                dve.tensor_copy(key[:], ps[:, 1, 0:ET])
                dve.tensor_copy(weight[:], ps[:, 2, 0:ET])
    return idx, key, weight


def gate(nc, g, name, turned, gate_w, gate_b, ctx):
    probs = ctx.enter_context(nc.sbuf_tensor(name + "_probs", [P, NT, EXPERTS], F32))
    with ExitStack() as c:
        tb = lambda n, s, d=F32: c.enter_context(nc.sbuf_tensor(n, s, d, allow_name_mangling=True))
        w = tb("gate_w", [P, KC, EXPERTS])
        b = tb("gate_b", [P, EXPERTS])
        top = tb("gate_top", [P, 2, NT])
        ps = c.enter_context(nc.psum_tensor("gate_ps", [P, NT, EXPERTS], F32, allow_name_mangling=True))
        sem = g.semaphores(c)
        s_w, s_mm, s_logit, s_exp, s_chain = map(sem, ("s_w", "s_mm", "s_logit", "s_exp", "s_chain"))
        shape = [P, NT, EXPERTS]
        with nc.Block() as block:
            @block.sync
            def _(sp):
                sp.dma_start(w[:], gate_w.rearrange("(k p) e -> p k e", p=P)).then_inc(s_w, 16)
                sp.dma_start(b[:], gate_b.rearrange("(o e) -> o e", o=1).to_broadcast([P, EXPERTS])).then_inc(s_w, 16)

            @block.tensor
            def _(pe):
                pe.wait_ge(s_w, 32)
                for t in range(NT):
                    for k in range(KC):
                        mm = pe.matmul(ps[:, t, :], turned[:, k, t * P:(t + 1) * P], w[:, k, :], start=(k == 0), stop=(k == KC - 1))
                mm.then_inc(s_mm, 1)

            @block.scalar
            def _(act):
                act.wait_ge(s_logit, 1)
                act.activation(probs[:], probs[:], ACT.Exp).then_inc(s_exp, 1)

            @block.vector
            def _(dve):
                ch = Chain(dve, s_chain)
                dve.wait_ge(s_w, 32)
                dve.wait_ge(s_mm, 1)
                ch.link(dve.tensor_tensor(probs[:], ps[:], b[:].unsqueeze(1).to_broadcast(shape), ALU.add))
                ch.link(dve.tensor_reduce(top[:, 0], probs[:], AX.X, ALU.max))
                ch.link(dve.tensor_tensor(probs[:], probs[:], top[:, 0].unsqueeze(2).to_broadcast(shape), ALU.subtract))
                dve.sem_inc(s_logit, 1)
                dve.wait_ge(s_exp, 1)
                ch.link(dve.tensor_reduce(top[:, 0], probs[:], AX.X, ALU.add))
                ch.link(dve.reciprocal(top[:, 1], top[:, 0]))
                ch.link(dve.tensor_tensor(probs[:], probs[:], top[:, 1].unsqueeze(2).to_broadcast(shape), ALU.mult))
    return probs


def bias_columns(nc, g, b, parts, ctx):
    cols = ctx.enter_context(nc.sbuf_tensor("b1_cols", [P, EXPERTS, parts], F32, allow_name_mangling=True))
    with ExitStack() as c:
        rows = c.enter_context(nc.sbuf_tensor("b1_rows", [EXPERTS * parts, P], F32, allow_name_mangling=True))
        ps = c.enter_context(nc.psum_tensor("b1_ps", [P, EXPERTS * parts], F32, allow_name_mangling=True))
        s_rows, s_turned = map(g.semaphores(c), ("s_rows", "s_turned"))
        with nc.Block() as block:
            @block.sync
            def _(sp):
                sp.dma_start(rows[:], b.rearrange("e (k p) -> (e k) p", p=P)).then_inc(s_rows, 16)

            @block.tensor
            def _(pe):
                pe.wait_ge(s_rows, 16)
                pe.transpose(ps[:], rows[:], g.ident[0:EXPERTS * parts, 0:EXPERTS * parts]).then_inc(s_turned, 1)

            @block.vector
            def _(dve):
                dve.wait_ge(s_turned, 1)
                dve.tensor_copy(cols[:].rearrange("p e k -> p (e k)"), ps[:])
    return cols


def first_largest(dve, ch, g, values, best, hot, work):
    shape = [P, NT, EXPERTS]
    ch.link(dve.tensor_reduce(best, values, AX.X, ALU.max))
    ch.link(dve.tensor_tensor(hot, values, best.unsqueeze(2).to_broadcast(shape), ALU.is_equal))
    ch.link(dve.tensor_tensor(hot, hot, g.falling[:].unsqueeze(1).to_broadcast(shape), ALU.mult))
    ch.link(dve.tensor_reduce(work, hot, AX.X, ALU.max))
    ch.link(dve.tensor_tensor(hot, hot, work.unsqueeze(2).to_broadcast(shape), ALU.is_equal))


def mixture_top2(nc, g, x, turned, probs, W1, b1, W2, b2, zero_dram):
    FC = F1 // P
    BT = 5
    BLOCKS = NT // BT
    HALF = BT * P // 2
    STEPS = 2 * BLOCKS
    GROUP = 8
    with ExitStack() as c:
        tb = lambda n, s, d=F32: c.enter_context(nc.sbuf_tensor(n, s, d, allow_name_mangling=True))
        w1 = [tb(f"w1_{j}", [P, KC, F1]) for j in range(2)]
        w2 = [tb(f"w2_{j}", [P, FC, D]) for j in range(2)]
        b1_all = bias_columns(nc, g, b1, FC, c)
        b2_all = tb("b2_all", [EXPERTS, D])
        cw = tb("cw", [P, NT, EXPERTS])
        hot = tb("hot_e", [P, NT, EXPERTS])
        best = tb("best", [P, 2, NT])
        cw_turned = tb("cw_turned", [EXPERTS, NT, P])
        hid = [tb(f"hid{j}", [P, FC, BT * P]) for j in range(2)]
        zeros = tb("zeros", [P, 2048])
        spot_now = [tb(f"spot_now{j}", [P, GROUP], I32) for j in range(2)]
        load_now = [tb(f"load_now{j}", [P, GROUP, 4]) for j in range(2)]
        ps_h = [c.enter_context(nc.psum_tensor(f"ps_h{j}", [P, 2, 512], F32, allow_name_mangling=True)) for j in range(2)]
        ps_y = [c.enter_context(nc.psum_tensor(f"ps_y{j}", [P, 512], F32, allow_name_mangling=True)) for j in range(4)]
        sem = g.semaphores(c)
        s_b, s_zero, s_zeroed, s_chain, s_cw, s_turn, s_turned, s_bias, s_bias_in, s_h, s_hid, s_y, s_x, s_staged, s_go, s_act = map(sem, (
            "s_b", "s_zero", "s_zeroed", "s_chain", "s_cw", "s_turn", "s_turned", "s_bias", "s_bias_in", "s_h", "s_hid", "s_y", "s_x", "s_staged", "s_go", "s_act"))
        s_w = [sem("s_w0"), sem("s_w1")]
        s_sent = [sem("s_sent0"), sem("s_sent1")]
        TG = -(-NT // 4)
        with nc.Block() as block:
            @block.sync
            def _(sp):
                sp.dma_start(b2_all[:], b2).then_inc(s_b, 16)
                with sp.Fori(0, EXPERTS // 2) as i:
                    for j in range(2):
                        sp.wait_ge(s_y, STEPS * BT * i)
                        sp.dma_start(w1[j][:], W1[bass.ds(2 * i + j, 1)].rearrange("o (k p) f -> p (o k) f", p=P)).then_inc(s_w[j], 16)
                        sp.dma_start(w2[j][:], W2[bass.ds(2 * i + j, 1)].rearrange("o (k p) f -> p (o k) f", p=P)).then_inc(s_w[j], 16)
                sp.wait_ge(s_zero, 1)
                for r in range(0, EXPERTS * CAPP, 2048 * P // D):
                    sp.dma_start(zero_dram[r:r + 2048 * P // D].rearrange("(p a) d -> p (a d)", p=P), zeros[:]).then_inc(s_zeroed, 16)
                sp.wait_ge(s_zeroed, 16 * (EXPERTS * CAPP * D // (2048 * P)))

            @block.gpsimd
            def _(pool):
                pool.memset(zeros[:], 0.0).then_inc(s_zero, 1)
                for j in range(2):
                    pool.memset(load_now[j][:], 0.0).then_inc(s_staged, 1)
                pool.wait_ge(s_staged, 2)
                with pool.Fori(0, ET // (2 * GROUP)) as i:
                    for j in range(2):
                        pool.wait_ge(s_sent[j], 16 * GROUP * i)
                        pool.tensor_copy(spot_now[j][:], g.spot[:, bass.ds((2 * i + j) * GROUP, GROUP)]).then_inc(s_staged, 1)
                        for f, values in enumerate((g.dst_key, g.src_key, g.weight)):
                            pool.tensor_copy(load_now[j][:, :, f], values[:, bass.ds((2 * i + j) * GROUP, GROUP)]).then_inc(s_staged, 1)
                        pool.wait_ge(s_staged, 8 * i + 4 * j + 6)
                        pool.sem_inc(s_go, 1)
                        for u in range(GROUP):
                            pool.indirect_dma_start(out=g.list_dram, out_offset=bass.IndirectOffsetOnAxis(ap=spot_now[j][:, u:u + 1], axis=0),
                                                    in_=load_now[j][:, u, :], in_offset=None).then_inc(s_sent[j], 16)
                for j in range(2):
                    pool.wait_ge(s_sent[j], 16 * GROUP * (ET // (2 * GROUP)))

            @block.tensor
            def _(pe):
                pe.wait_ge(s_cw, 1)
                for q in range(TG):
                    if q >= 4:
                        pe.wait_ge(s_turned, q - 3)
                    for t in range(4 * q, min(NT, 4 * q + 4)):
                        mm = pe.transpose(ps_y[q % 4][0:EXPERTS, (t % 4) * P:(t % 4 + 1) * P], cw[:, t, :], g.ident[:])
                    mm.then_inc(s_turn, 1)
                pe.wait_ge(s_turned, TG)
                pe.wait_ge(s_b, 16)
                for t in range(NT):
                    if t >= 4:
                        pe.wait_ge(s_bias_in, t - 3)
                    pe.matmul(ps_y[t % 4][:, 0:D], cw_turned[:, t, :], b2_all[:], start=True, stop=True).then_inc(s_bias, 1)
                pe.wait_ge(s_bias_in, NT)

                def up(i, s):
                    j, b = s // BLOCKS, s % BLOCKS
                    if b == 0:
                        pe.wait_ge(s_w[j], 32 * i + 32)
                    for f in range(FC):
                        pe.wait_ge(s_hid, STEPS * FC * i + max(0, s * FC + f - 1))
                        for half in range(2):
                            for k in range(KC):
                                mm = pe.matmul(ps_h[f % 2][:, half, 0:HALF], w1[j][:, k, f * P:(f + 1) * P],
                                               turned[:, k, b * BT * P + half * HALF:b * BT * P + (half + 1) * HALF],
                                               start=(k == 0), stop=(k == KC - 1))
                        mm.then_inc(s_h, 1)

                def down(i, s):
                    j = s // BLOCKS
                    pe.wait_ge(s_hid, STEPS * FC * i + (s + 1) * FC)
                    for t in range(BT):
                        m = s * BT + t
                        pe.wait_ge(s_x, STEPS * BT * i + max(0, m - 3))
                        for f in range(FC):
                            mm = pe.matmul(ps_y[m % 4][:, 0:D], hid[s % 2][:, f, t * P:(t + 1) * P], w2[j][:, f, :],
                                           start=(f == 0), stop=(f == FC - 1))
                        mm.then_inc(s_y, 1)

                with pe.Fori(0, EXPERTS // 2) as i:
                    for s in range(STEPS + 1):
                        if s < STEPS:
                            up(i, s)
                        if s >= 1:
                            down(i, s - 1)

            @block.scalar
            def _(act):
                for q in range(TG):
                    n = min(NT, 4 * q + 4) - 4 * q
                    act.wait_ge(s_turn, q + 1)
                    act.activation(cw_turned[:, 4 * q:4 * q + n, :].rearrange("e t n -> e (t n)"), ps_y[q % 4][0:EXPERTS, 0:n * P], ACT.Copy).then_inc(s_turned, 1)
                with act.Fori(0, EXPERTS // 2) as i:
                    for s in range(STEPS):
                        act.wait_ge(s_y, STEPS * BT * i + max(0, s - 1) * BT)
                        for f in range(FC):
                            act.wait_ge(s_h, STEPS * FC * i + (s * FC + f + 1))
                            act.sem_inc(s_act, 1)
                            act.activation(hid[s % 2][:, f, :].rearrange("p (a b) -> p a b", a=2), ps_h[f % 2][:, :, 0:HALF], ACT.Gelu,
                                           bias=b1_all[:, bass.ds(2 * i + s // BLOCKS, 1), f:f + 1].rearrange("p o f -> p (o f)")).then_inc(s_hid, 1)

            @block.vector
            def _(dve):
                ch = Chain(dve, s_chain)
                first_largest(dve, ch, g, probs[:], best[:, 0], hot[:], best[:, 1])
                ch.link(dve.tensor_tensor(cw[:], probs[:], hot[:], ALU.mult))
                ch.link(dve.scalar_tensor_tensor(probs[:], hot[:], -2.0, probs[:], ALU.mult, ALU.add))
                first_largest(dve, ch, g, probs[:], best[:, 0], hot[:], best[:, 1])
                ch.link(dve.tensor_tensor(hot[:], probs[:], hot[:], ALU.mult))
                ch.link(dve.tensor_tensor(cw[:], cw[:], hot[:], ALU.add))
                dve.sem_inc(s_cw, 1)
                for t in range(NT):
                    dve.wait_ge(s_bias, t + 1)
                    dve.tensor_tensor(x[:, t, :], ps_y[t % 4][:, 0:D], x[:, t, :], ALU.add).then_inc(s_bias_in, 1)
                dve.wait_ge(s_bias_in, NT)
                with dve.Fori(0, EXPERTS // 2) as i:
                    for s in range(STEPS):
                        for t in range(BT):
                            m, tile = s * BT + t, (s % BLOCKS) * BT + t
                            dve.wait_ge(s_y, STEPS * BT * i + (m + 1))
                            dve.wait_ge(s_x, STEPS * BT * i + max(0, m - NT + 1))
                            dve.scalar_tensor_tensor(x[:, tile, :], ps_y[m % 4][:, 0:D], cw[:, tile, bass.ds(2 * i + s // BLOCKS, 1)],
                                                     x[:, tile, :], ALU.mult, ALU.add).then_inc(s_x, 1)


def add_sums(nc, g, x, acc, bias):
    with ExitStack() as c:
        b_row = c.enter_context(nc.sbuf_tensor("b_row2", [P, D], F32, allow_name_mangling=True))
        s_b, s_sum = map(g.semaphores(c), ("s_b", "s_sum"))
        with nc.Block() as block:
            @block.sync
            def _(sp):
                sp.dma_start(b_row[:], bias.rearrange("(o d) -> o d", o=1).to_broadcast([P, D])).then_inc(s_b, 16)

            @block.gpsimd
            def _(pool):
                pool.wait_ge(s_b, 16)
                pool.tensor_tensor(acc[:, 0:NT, :], acc[:, 0:NT, :], b_row[:].unsqueeze(1).to_broadcast([P, NT, D]), ALU.add).then_inc(s_sum, 1)

            @block.vector
            def _(dve):
                dve.wait_ge(s_sum, 1)
                dve.tensor_tensor(x[:], x[:], acc[:, 0:NT, :], ALU.add)


def route(nc, g, probs, xn, rows_dram, ctx):
    sb = lambda n, s, d=F32: ctx.enter_context(nc.sbuf_tensor(n, s, d, allow_name_mangling=True))
    take = sb("take", [P, NT], I32)
    factor = sb("factor", [P, NT])
    with ExitStack() as c:
        tb = lambda n, s, d=F32: c.enter_context(nc.sbuf_tensor(n, s, d, allow_name_mangling=True))
        hot = tb("hot_r", [P, NT, EXPERTS])
        w = tb("w_route", [P, 8, NT])
        tot = tb("tot", [P, EXPERTS, NT])
        run = tb("run_r", [P, EXPERTS, NT])
        rank = tb("rank_r", [P, NT, EXPERTS])
        put = tb("put", [P, NT], I32)
        ps = c.enter_context(nc.psum_tensor("route_ps", [P, 2, 512], F32, allow_name_mangling=True))
        sem = g.semaphores(c)
        s_number, s_chain, s_hot, s_ranks, s_put, s_sent = map(sem, ("s_number", "s_chain", "s_hot", "s_ranks", "s_put", "s_sent"))
        best, spare, number, valid, place, expert, kept, spot = (w[:, i] for i in range(8))
        shape = [P, NT, EXPERTS]
        with nc.Block() as block:
            @block.gpsimd
            def _(pool):
                pool.iota(number, [[P, NT]], base=0, channel_multiplier=1, allow_small_or_imprecise_dtypes=True).then_inc(s_number, 1)
                pool.wait_ge(s_put, 1)
                for t in range(NT):
                    pool.indirect_dma_start(out=rows_dram, out_offset=bass.IndirectOffsetOnAxis(ap=put[:, t:t + 1], axis=0),
                                            in_=xn[:, t, :], in_offset=None).then_inc(s_sent, 16)
                pool.wait_ge(s_sent, 16 * NT)

            @block.tensor
            def _(pe):
                pe.wait_ge(s_hot, 1)
                rows = hot[:].rearrange("p t e -> p (t e)")
                pe.matmul(ps[:, 0, 0:NT * EXPERTS], g.before[:], rows, start=True, stop=True)
                pe.matmul(ps[:, 1, 0:NT * EXPERTS], g.ones[:], rows, start=True, stop=True).then_inc(s_ranks, 1)

            @block.vector
            def _(dve):
                ch = Chain(dve, s_chain)
                first_largest(dve, ch, g, probs[:], best, hot[:], spare)
                dve.wait_ge(s_number, 1)
                ch.link(dve.tensor_scalar(valid, number, float(N), None, ALU.is_lt))
                ch.link(dve.tensor_tensor(hot[:], hot[:], valid.unsqueeze(2).to_broadcast(shape), ALU.mult))
                dve.sem_inc(s_hot, 1)
                dve.wait_ge(s_ranks, 1)
                ch.link(dve.tensor_copy(tot[:], ps[:, 1, 0:NT * EXPERTS].rearrange("p (t e) -> p e t", e=EXPERTS)))
                for e in range(EXPERTS):
                    last = dve.tensor_tensor_scan(run[:, e, :], g.ones[:, 0:NT], tot[:, e, :], 0.0, ALU.mult, ALU.add)
                ch.link(last)
                ch.link(dve.tensor_tensor(run[:], run[:], tot[:], ALU.subtract))
                ch.link(dve.tensor_tensor(rank[:], ps[:, 0, 0:NT * EXPERTS].rearrange("p (t e) -> p t e", e=EXPERTS),
                                          run[:].rearrange("p e t -> p t e"), ALU.add))
                ch.link(dve.tensor_tensor(rank[:], rank[:], hot[:], ALU.mult))
                ch.link(dve.tensor_reduce(place, rank[:], AX.X, ALU.add))
                ch.link(dve.tensor_tensor(rank[:], hot[:], g.iota25[:, 0:EXPERTS].unsqueeze(1).to_broadcast(shape), ALU.mult))
                ch.link(dve.tensor_reduce(expert, rank[:], AX.X, ALU.add))
                ch.link(dve.tensor_scalar(kept, place, float(CAP), None, ALU.is_lt))
                ch.link(dve.tensor_tensor(kept, kept, valid, ALU.mult))
                ch.link(dve.tensor_tensor(factor[:], best, kept, ALU.mult))
                ch.link(dve.tensor_scalar(expert, expert, float(CAPP), None, ALU.mult))
                ch.link(dve.tensor_scalar(spare, place, float(CAP - 1), None, ALU.min))
                ch.link(dve.tensor_tensor(take[:], spare, expert, ALU.add))
                ch.link(dve.tensor_tensor(spot, place, expert, ALU.add))
                ch.link(dve.tensor_scalar(number, number, float(EXPERTS * CAPP), None, ALU.add))
                ch.link(dve.tensor_tensor(spot, spot, number, ALU.subtract))
                ch.link(dve.tensor_tensor(spot, spot, kept, ALU.mult))
                ch.link(dve.tensor_tensor(put[:], spot, number, ALU.add))
                dve.sem_inc(s_put, 1)
    return take, factor


def expert_layers(nc, g, rows_dram, y_dram, w1, b1, w2, b2):
    FC = F2 // P
    RT = CAPP // P
    with ExitStack() as c:
        tb = lambda n, s, d=F32: c.enter_context(nc.sbuf_tensor(n, s, d, allow_name_mangling=True))
        up_w = [tb(f"up_w{j}", [P, KC, F2]) for j in range(2)]
        down_w = [tb(f"down_w{j}", [P, FC, D]) for j in range(2)]
        b1_all = bias_columns(nc, g, b1, FC, c)
        b2_row = [tb(f"b2_row{j}", [1, D]) for j in range(2)]
        xin = [tb(f"xin{j}", [P, RT, D]) for j in range(2)]
        xt = [tb(f"xt{j}", [P, KC, CAPP]) for j in range(2)]
        hid = [tb(f"hidden{j}", [P, FC, CAPP]) for j in range(2)]
        y = [tb(f"y{j}", [P, RT, D]) for j in range(2)]
        bank = lambda n: c.enter_context(nc.psum_tensor(n, [P, 512], F32, allow_name_mangling=True))
        ps_t = [bank(f"ps_t{k}") for k in range(KC)]
        ps_h = [bank(f"ps_u{k}") for k in range(3)]
        ps_y = [bank(f"ps_v{k}") for k in range(3)]
        sem = g.semaphores(c)
        s_act, s_turn, s_turned, s_h, s_hid, s_y, s_out_y = map(sem, ("s_act", "s_turn", "s_turned", "s_h", "s_hid", "s_y", "s_out_y"))
        s_w = [sem("s_w0"), sem("s_w1")]
        s_st = [sem("s_st0"), sem("s_st1")]
        PAIRS = EXPERTS // 2
        with nc.Block() as block:
            @block.sync
            def _(sp):
                with sp.Fori(0, PAIRS) as i:
                    for j in range(2):
                        e = 2 * i + j
                        sp.wait_ge(s_y, 2 * RT * i)
                        sp.dma_start(xin[j][:], rows_dram[bass.ds(e * CAPP, CAPP)].rearrange("(t p) d -> p t d", p=P)).then_inc(s_w[j], 16)
                        sp.dma_start(up_w[j][:], w1[bass.ds(e, 1)].rearrange("o (k p) f -> p (o k) f", p=P)).then_inc(s_w[j], 16)
                        sp.dma_start(down_w[j][:], w2[bass.ds(e, 1)].rearrange("o (k p) f -> p (o k) f", p=P)).then_inc(s_w[j], 16)
                        sp.dma_start(b2_row[j][:], b2[bass.ds(e, 1)]).then_inc(s_w[j], 16)

            @block.tensor
            def _(pe):
                with pe.Fori(0, PAIRS) as i:
                    for j in range(2):
                        pe.wait_ge(s_w[j], 64 * i + 64)
                        pe.wait_ge(s_turned, 2 * KC * i + KC * j)
                        for k in range(KC):
                            for t in range(RT):
                                mm = pe.transpose(ps_t[k][:, t * P:(t + 1) * P], xin[j][:, t, k * P:(k + 1) * P], g.ident[:])
                            mm.then_inc(s_turn, 1)
                        pe.wait_ge(s_turned, 2 * KC * i + KC * (j + 1))
                        for f in range(FC):
                            n = j * FC + f
                            pe.wait_ge(s_hid, 2 * FC * i + max(0, n - 2))
                            for k in range(KC):
                                mm = pe.matmul(ps_h[f % 3][:], up_w[j][:, k, f * P:(f + 1) * P], xt[j][:, k, :], start=(k == 0), stop=(k == KC - 1))
                            mm.then_inc(s_h, 1)
                        for t in range(RT):
                            m = j * RT + t
                            pe.wait_ge(s_out_y, 2 * RT * i + max(0, m - 2))
                            pe.matmul(ps_y[m % 3][:, 0:D], g.ones[0:1, :], b2_row[j][:], start=True, stop=False)
                            for f in range(FC):
                                if t == 0:
                                    pe.wait_ge(s_hid, 2 * FC * i + (j * FC + f + 1))
                                mm = pe.matmul(ps_y[m % 3][:, 0:D], hid[j][:, f, t * P:(t + 1) * P], down_w[j][:, f, :], start=False, stop=(f == FC - 1))
                            mm.then_inc(s_y, 1)

            @block.scalar
            def _(act):
                with act.Fori(0, PAIRS) as i:
                    for j in range(2):
                        act.wait_ge(s_y, 2 * RT * i)
                        for f in range(FC):
                            act.wait_ge(s_h, 2 * FC * i + (j * FC + f + 1))
                            act.sem_inc(s_act, 1)
                            act.activation(hid[j][:, f, :], ps_h[f % 3][:], ACT.Relu,
                                           bias=b1_all[:, bass.ds(2 * i + j, 1), f:f + 1].rearrange("p o f -> p (o f)")).then_inc(s_hid, 1)
                        act.wait_ge(s_out_y, 2 * RT * i + RT * (j + 1))
                        act.dma_start(y_dram[bass.ds((2 * i + j) * CAPP, CAPP)].rearrange("(t p) d -> p t d", p=P), y[j][:]).then_inc(s_st[j], 16)
                for j in range(2):
                    act.wait_ge(s_st[j], 16 * PAIRS)

            @block.vector
            def _(dve):
                with dve.Fori(0, PAIRS) as i:
                    for j in range(2):
                        dve.wait_ge(s_y, 2 * RT * i)
                        for k in range(KC):
                            dve.wait_ge(s_turn, 2 * KC * i + (KC * j + k + 1))
                            dve.tensor_copy(xt[j][:, k, :], ps_t[k][:]).then_inc(s_turned, 1)
                        dve.wait_ge(s_st[j], 16 * i)
                        for t in range(RT):
                            m = j * RT + t
                            dve.wait_ge(s_y, 2 * RT * i + (m + 1))
                            dve.tensor_copy(y[j][:, t, :], ps_y[m % 3][:, 0:D]).then_inc(s_out_y, 1)


def combine(nc, g, x, y_dram, take, factor, out):
    RING = 8
    TOP = 3.4028234e38
    with ExitStack() as c:
        tb = lambda n, s, d=F32: c.enter_context(nc.sbuf_tensor(n, s, d, allow_name_mangling=True))
        rows = [tb(f"rows_c{u}", [P, D]) for u in range(RING)]
        odd = [tb(f"odd{u}", [P, 3, D], U8) for u in range(2)]
        fill = tb("fill", [P, 3, D])
        sem = g.semaphores(c)
        s_fill, s_chain, s_x, s_out = map(sem, ("s_fill", "s_chain", "s_x", "s_out"))
        s_rows = [sem(f"s_rows{u}") for u in range(RING)]
        with nc.Block() as block:
            @block.gpsimd
            def _(pool):
                for t in range(NT):
                    if t >= RING:
                        pool.wait_ge(s_x, t - RING + 1)
                    pool.indirect_dma_start(out=rows[t % RING][:], out_offset=None, in_=y_dram,
                                            in_offset=bass.IndirectOffsetOnAxis(ap=take[:, t:t + 1], axis=0)).then_inc(s_rows[t % RING], 16)

            @block.vector
            def _(dve):
                ch = Chain(dve, s_chain)
                for i, v in enumerate((0.0, 1e4, -1e4)):
                    dve.memset(fill[:, i, :], v).then_inc(s_fill, 1)
                dve.wait_ge(s_fill, 3)
                for t in range(NT):
                    r, m = rows[t % RING], odd[t % 2]
                    dve.wait_ge(s_rows[t % RING], 16 * (t // RING + 1))
                    ch.link(dve.tensor_scalar(r[:], r[:], factor[:, t:t + 1], None, ALU.mult))
                    dve.tensor_tensor(m[:, 0], r[:], r[:], ALU.not_equal)
                    dve.tensor_scalar(m[:, 1], r[:], TOP, None, ALU.is_gt)
                    ch.link(dve.tensor_scalar(m[:, 2], r[:], -TOP, None, ALU.is_lt))
                    for i in range(3):
                        ch.link(dve.copy_predicated(r[:], m[:, i], fill[:, i, :]))
                    dve.tensor_tensor(x[:, t, :], x[:, t, :], r[:], ALU.add).then_inc(s_x, 1)

            @block.sync
            def _(sp):
                for t in range(NT):
                    n = min(P, N - t * P)
                    sp.wait_ge(s_x, t + 1)
                    sp.dma_start(out[t * P:t * P + n], x[0:n, t, :]).then_inc(s_out, 16)
                sp.wait_ge(s_out, 16 * NT)


def load_nodes(nc, g, x, x_dram):
    with ExitStack() as c:
        s_pad, s_x = map(g.semaphores(c), ("s_pad", "s_x"))
        with nc.Block() as block:
            @block.vector
            def _(dve):
                dve.memset(x[:, NT - 1, :], 0.0).then_inc(s_pad, 1)

            @block.sync
            def _(sp):
                full = (NT - 1) * P
                sp.dma_start(x[:, 0:NT - 1, :], x_dram[0:full].rearrange("(t p) d -> p t d", p=P)).then_inc(s_x, 16)
                sp.wait_ge(s_pad, 1)
                sp.dma_start(x[0:N - full, NT - 1, :], x_dram[full:N]).then_inc(s_x, 16)
                sp.wait_ge(s_x, 32)


def attention_layer(nc, g, name, turned_from, x_in, weights, heads, dst, hots, visits, x_out, ctx):
    W, a_src, a_dst, bias = weights
    C = heads
    with ExitStack() as left:
        turned = left.enter_context(nc.sbuf_tensor(name + "_turned", [P, KC, NP], F32))
        if turned_from == "norm":
            with nc.sbuf_tensor(name + "_xn", [P, NT, D], F32) as xn:
                normalise(nc, g, x_in, xn, turned)
        else:
            normalise(nc, g, x_in, None, turned)
        if turned_from != "norm":
            ctx.close()
        h, al, table = project(nc, g, name, turned, W, (a_src, a_dst), C, ctx)
    with ExitStack() as left:
        ae = expand(nc, g, name, al, hots, C, left)
        ext = edge_softmax(nc, g, name, ae, dst, C, ctx)
    acc = ctx.enter_context(nc.sbuf_tensor(name + "_acc", [P, NT + 1, D + 2 * C + 1], F32, side="right"))
    if C > 1:
        scale = lambda k: ext[:, bass.ds(k, 1), 0:C].rearrange("p o c -> p (o c)").unsqueeze(2).to_broadcast([P, C, D // C])
    else:
        scale = lambda k: ext[:, bass.ds(k, 1), 0:1].rearrange("p o c -> p (o c)")
    aggregate(nc, g, name, table, g.src_idx, g.dst_key, visits, scale, C, ext, acc)
    finish_attention(nc, g, acc, h, al, bias, C, x_out)
    return acc


def build(nc, x, src, dst, edge_weight, L0_gnn_W1, L0_gnn_a_src1, L0_gnn_a_dst1, L0_gnn_b1, L0_gnn_W2, L0_gnn_a_src2,
          L0_gnn_a_dst2, L0_gnn_b2, L0_ffn_gate_w, L0_ffn_gate_b, L0_ffn_W1, L0_ffn_b1, L0_ffn_W2, L0_ffn_b2, L1_gnn_W,
          L1_gnn_b, L1_ffn_gate_w, L1_ffn_gate_b, L1_ffn_w1, L1_ffn_b1, L1_ffn_w2, L1_ffn_b2, out, stop=99, probe=None):
    g = Graph(nc)
    rows_dram = nc.dram_tensor("rows_dram", (EXPERTS * CAPP + NP, D), F32, kind="Internal").ap()
    y_dram = nc.dram_tensor("y_dram", (EXPERTS * CAPP, D), F32, kind="Internal").ap()
    with ExitStack() as keep:
        constants(nc, g, keep)
        xs = keep.enter_context(nc.sbuf_tensor("x_nodes", [P, NT, D], F32))
        load_nodes(nc, g, xs, x)
        graph_tables(nc, g, src, dst, edge_weight, keep)
        to_dst, minus_dst, _ = visit_tables(nc, "by_dst", g, g.dst_key, keep)
        to_src, minus_src, ends = visit_tables(nc, "by_src", g, g.src_key, keep)
        with ExitStack() as graph:
            hot_src = high_parts(nc, "hot_src", g, g.src_key, graph)
            by_source(nc, g, hot_src, ends, graph)
            hot_dst = high_parts(nc, "hot_dst", g, g.dst_key, graph)
            right = ExitStack()
            acc = attention_layer(nc, g, "gat1", "norm", xs, (L0_gnn_W1, L0_gnn_a_src1, L0_gnn_a_dst1, L0_gnn_b1), HEADS,
                                  dst, (hot_src, hot_dst), (to_dst, minus_dst), None, right)
            if stop == 1:
                probe(nc, acc[:, 0:NT, 0:D]); right.close(); return
            attention_layer(nc, g, "gat2", "sums", acc[:, 0:NT, 0:D], (L0_gnn_W2, L0_gnn_a_src2, L0_gnn_a_dst2, L0_gnn_b2), 1,
                            dst, (hot_src, hot_dst), (to_dst, minus_dst), xs, right)
            right.close()
            if stop == 2:
                probe(nc, xs[:]); return
            with ExitStack() as left:
                turned = left.enter_context(nc.sbuf_tensor("ffn0_turned", [P, KC, NP], F32))
                with nc.sbuf_tensor("ffn0_xn", [P, NT, D], F32) as xn:
                    normalise(nc, g, xs, xn, turned)
                probs = gate(nc, g, "ffn0", turned, L0_ffn_gate_w, L0_ffn_gate_b, left)
                mixture_top2(nc, g, xs, turned, probs, L0_ffn_W1, L0_ffn_b1, L0_ffn_W2, L0_ffn_b2, rows_dram)
            if stop == 3:
                probe(nc, xs[:]); return
        with ExitStack() as left:
            l_idx, l_key, l_weight = read_list(nc, g, left)
            with ExitStack() as right:
                with ExitStack() as inner:
                    turned = inner.enter_context(nc.sbuf_tensor("gcn_turned", [P, KC, NP], F32))
                    with nc.sbuf_tensor("gcn_xn", [P, NT, D], F32) as xn:
                        normalise(nc, g, xs, xn, turned)
                    _, _, table = project(nc, g, "gcn", turned, L1_gnn_W, None, 1, right)
                acc = right.enter_context(nc.sbuf_tensor("gcn_acc", [P, NT + 1, D], F32, side="right"))
                aggregate(nc, g, "gcn", table, l_idx, l_key, (to_src, minus_src), lambda k: l_weight[:, bass.ds(k, 1)], 1, None, acc)
                add_sums(nc, g, xs, acc, L1_gnn_b)
        if stop == 4:
            probe(nc, xs[:]); return
        with ExitStack() as left:
            xn = left.enter_context(nc.sbuf_tensor("ffn1_xn", [P, NT, D], F32))
            turned = left.enter_context(nc.sbuf_tensor("ffn1_turned", [P, KC, NP], F32))
            normalise(nc, g, xs, xn, turned)
            probs = gate(nc, g, "ffn1", turned, L1_ffn_gate_w, L1_ffn_gate_b, left)
            take, factor = route(nc, g, probs, xn, rows_dram, left)
            expert_layers(nc, g, rows_dram, y_dram, L1_ffn_w1, L1_ffn_b1, L1_ffn_w2, L1_ffn_b2)
            combine(nc, g, xs, y_dram, take, factor, out)


_INS = ["x", "src", "dst", "edge_weight", "L0_gnn_W1", "L0_gnn_a_src1", "L0_gnn_a_dst1", "L0_gnn_b1", "L0_gnn_W2", "L0_gnn_a_src2",
        "L0_gnn_a_dst2", "L0_gnn_b2", "L0_ffn_gate_w", "L0_ffn_gate_b", "L0_ffn_W1", "L0_ffn_b1", "L0_ffn_W2", "L0_ffn_b2", "L1_gnn_W",
        "L1_gnn_b", "L1_ffn_gate_w", "L1_ffn_gate_b", "L1_ffn_w1", "L1_ffn_b1", "L1_ffn_w2", "L1_ffn_b2"]
_OUTS = [((N, D), "float32")]


def kernel(**inputs):
    import numpy as _np
    import concourse.bacc as _bacc
    from concourse import mybir as _mybir
    from concourse.bass_utils import run_bass_kernel_spmd as _run

    nc = _bacc.Bacc("TRN2", target_bir_lowering=False, num_devices=1)
    arrays, args = {}, []
    for name in _INS:
        a = _np.ascontiguousarray(inputs[name])
        arrays[f"in_{name}_dram"] = a
        args.append(nc.dram_tensor(f"in_{name}_dram", a.shape, _mybir.dt.from_np(a.dtype), kind="ExternalInput").ap())
    for i, (shape, dtype) in enumerate(_OUTS):
        dt = _mybir.dt.from_np(_np.dtype(dtype))
        args.append(nc.dram_tensor(f"out_{i}_dram", shape, dt, kind="ExternalOutput").ap())
    build(nc, *args)
    r = _run(nc, [arrays], core_ids=[0])
    return r.results[0]["out_0_dram"]
```

```python
from contextlib import ExitStack

import numpy as np
import concourse.bass as bass
from concourse import mybir

F32 = mybir.dt.float32
BF16 = mybir.dt.bfloat16
I32 = mybir.dt.int32
U8 = mybir.dt.uint8
ALU = mybir.AluOpType
ACT = mybir.ActivationFunctionType
AX = mybir.AxisListType

P = 128
N, D = 3125, 256
NT = -(-N // P)
NP = NT * P
E = 53125
ET = 416
EP = ET * P
CH, CI = 16, 26
CL = CI * P
SLOTS = 8
VG, VQ = 110, 4
V = VG * VQ
LAG = 2
DUMMY = NT
HEADS, HF = 8, 32
NEG = 0.2
EXPERTS = 8
F1 = 512
F2 = 1024
CAP = int(np.ceil(1.25 * N / EXPERTS))
CAPP = 512
ST = (2 * N - EXPERTS) // P + EXPERTS
BIG = 1e30
PAD_KEY = NP
EPS = 1e-5
KC = D // P
RG = -(-ET // P)
assert ST % SLOTS == 0
assert ET >= -(-E // P) and V >= ET + NT - 1 and V % SLOTS == 0 and CH * CI == ET


class Chain:

    def __init__(self, engine, sem):
        self.engine, self.sem, self.count = engine, sem, 0

    def link(self, instruction):
        self.count += 1
        instruction.then_inc(self.sem, 1)
        self.engine.wait_ge(self.sem, self.count)


def load_rows(sp, dst, src, count, sem):
    full = count // P
    whole = full // P
    n = 0
    if whole:
        sp.dma_start(dst[:, 0:whole, :], src[0:whole * P * P].rearrange("(g k e) -> k g e", k=P, e=P)).then_inc(sem, 16)
        n += 1
    left = full - whole * P
    if left:
        sp.dma_start(dst[0:left, whole, :], src[whole * P * P:full * P].rearrange("(k e) -> k e", e=P)).then_inc(sem, 16)
        n += 1
    rest = count - full * P
    if rest:
        sp.dma_start(dst[left:left + 1, whole, 0:rest], src[full * P:count].rearrange("(k e) -> k e", k=1)).then_inc(sem, 16)
        n += 1
    return n


class Graph:

    def __init__(self, nc):
        self.nc, self.numbers, self.at = nc, list(nc.free_semaphores), 0

    def semaphores(self, c):
        taken = []

        def sem(name):
            number = self.numbers[self.at % len(self.numbers)]
            taken.append(self.nc.alloc_semaphore(f"{name}_{self.at}", num=number))
            self.at += 1
            return taken[-1]

        c.callback(lambda: self.nc.clear_and_free_semaphores(taken))
        return sem


def constants(nc, g, ctx):
    sb = lambda n, s, d=F32: ctx.enter_context(nc.sbuf_tensor(n, s, d, allow_name_mangling=True))
    g.ident = sb("ident", [P, P])
    g.iota_row = sb("iota_row", [P, P])
    g.iota_col = sb("iota_col", [P, 1])
    g.iota25 = sb("iota25", [P, 32])
    g.falling = sb("falling", [P, EXPERTS])
    g.before = sb("before", [P, P])
    g.ones = sb("ones", [P, P])
    with ExitStack() as c:
        s_iota = g.semaphores(c)("s_iota")
        with nc.Block() as block:
            @block.gpsimd
            def _(pool):
                pool.iota(g.iota_row[:], [[1, P]], base=0, channel_multiplier=0, allow_small_or_imprecise_dtypes=True).then_inc(s_iota, 1)
                pool.iota(g.iota_col[:], [[0, 1]], base=0, channel_multiplier=1, allow_small_or_imprecise_dtypes=True).then_inc(s_iota, 1)
                pool.iota(g.iota25[:], [[1, 32]], base=0, channel_multiplier=0, allow_small_or_imprecise_dtypes=True).then_inc(s_iota, 1)

            @block.vector
            def _(dve):
                dve.memset(g.ones[:], 1.0)
                dve.wait_ge(s_iota, 3)
                dve.tensor_scalar(g.falling[:], g.iota25[:, 0:EXPERTS], -1.0, float(EXPERTS), ALU.mult, ALU.add)
                dve.tensor_scalar(g.ident[:], g.iota_row[:], g.iota_col[:, 0:1], None, ALU.is_equal)
                dve.tensor_scalar(g.before[:], g.iota_row[:], g.iota_col[:, 0:1], None, ALU.is_gt)


def graph_tables(nc, g, src, dst, w, ctx):
    sb = lambda n, s, d=F32: ctx.enter_context(nc.sbuf_tensor(n, s, d, allow_name_mangling=True))
    g.src_key = sb("src_key", [P, ET])
    g.dst_key = sb("dst_key", [P, ET])
    g.weight = sb("weight", [P, ET])
    g.is_last = sb("is_last", [P, ET])
    g.src_idx = sb("src_idx", [P, ET], I32)
    g.lo_dram = [nc.dram_tensor(f"lo_{n}", (EP,), BF16, kind="Internal").ap() for n in ("src", "dst")]
    with ExitStack() as c:
        rows = c.enter_context(nc.sbuf_tensor("rows", [P, 4, RG, P], I32, allow_name_mangling=True))
        rows_f = c.enter_context(nc.sbuf_tensor("rows_f", [P, 4, RG, P], F32, allow_name_mangling=True))
        lo = c.enter_context(nc.sbuf_tensor("lo", [P, 2, RG, P], I32, allow_name_mangling=True))
        lo_bf = c.enter_context(nc.sbuf_tensor("lo_bf", [P, 2, RG, P], BF16, allow_name_mangling=True))
        turned = c.enter_context(nc.psum_tensor("turned", [P, 4, 512], F32, allow_name_mangling=True))
        sem = g.semaphores(c)
        s_padded, s_rows, s_float, s_turned, s_low, s_out, s_chain = map(
            sem, ("s_padded", "s_rows", "s_float", "s_turned", "s_low", "s_out", "s_chain"))
        loads = [0]
        lists = ((src, E), (dst, E), (dst[1:E], E - 1), (w, E))
        with nc.Block() as block:
            @block.sync
            def _(sp):
                sp.wait_ge(s_padded, 4)
                for i, (a, count) in enumerate(lists):
                    into = rows[:, i] if i < 3 else rows_f[:, 3]
                    loads[0] += load_rows(sp, into, a, count, s_rows)
                sp.wait_ge(s_low, 2)
                for i in range(2):
                    o = g.lo_dram[i]
                    sp.dma_start(o[0:3 * P * P].rearrange("(g k e) -> k g e", k=P, e=P), lo_bf[:, i, 0:3, :]).then_inc(s_out, 16)
                    sp.dma_start(o[3 * P * P:EP].rearrange("(k e) -> k e", e=P), lo_bf[0:ET - 3 * P, i, 3, :]).then_inc(s_out, 16)
                sp.wait_ge(s_out, 64)

            @block.vector
            def _(dve):
                ch = Chain(dve, s_chain)
                dve.memset(rows[:, 0], PAD_KEY).then_inc(s_padded, 1)
                dve.memset(rows[:, 1], PAD_KEY).then_inc(s_padded, 1)
                dve.memset(rows[:, 2], PAD_KEY + 1).then_inc(s_padded, 1)
                dve.memset(rows_f[:, 3], 0.0).then_inc(s_padded, 1)
                dve.wait_ge(s_padded, 4)
                dve.wait_ge(s_rows, 16 * loads[0])
                dve.tensor_copy(rows_f[:, 0:3], rows[:, 0:3]).then_inc(s_float, 1)
                ch.link(dve.tensor_scalar(lo[:], rows[:, 0:2], P - 1, None, ALU.bitwise_and))
                dve.tensor_copy(lo_bf[:], lo[:]).then_inc(s_low, 2)
                dve.wait_ge(s_turned, 1)
                dve.tensor_copy(g.src_key[:], turned[:, 0, 0:ET])
                dve.tensor_copy(g.dst_key[:], turned[:, 1, 0:ET]).then_inc(s_chain, 1)
                dve.tensor_copy(g.weight[:], turned[:, 3, 0:ET])
                dve.tensor_scalar(g.src_idx[:], turned[:, 0, 0:ET], float(N - 1), None, ALU.min)
                dve.wait_ge(s_chain, 2)
                dve.tensor_tensor(g.is_last[:], turned[:, 2, 0:ET], g.dst_key[:], ALU.not_equal)

            @block.tensor
            def _(pe):
                pe.wait_ge(s_float, 1)
                for i in range(4):
                    for r in range(RG):
                        k = min(P, ET - r * P)
                        mm = pe.transpose(turned[:, i, r * P:r * P + k], rows_f[0:k, i, r, :], g.ident[0:k, 0:k])
                mm.then_inc(s_turned, 1)


def high_parts(nc, name, g, key, ctx):
    hot = ctx.enter_context(nc.sbuf_tensor(name, [P, ET, NT], U8))
    with ExitStack() as c:
        ki = c.enter_context(nc.sbuf_tensor("ki", [P, ET], I32, allow_name_mangling=True))
        hi = c.enter_context(nc.sbuf_tensor("hi", [P, ET], F32, allow_name_mangling=True))
        s = g.semaphores(c)("s_hi")
        with nc.Block() as block:
            @block.vector
            def _(dve):
                ch = Chain(dve, s)
                ch.link(dve.tensor_copy(ki[:], key[:]))
                ch.link(dve.tensor_scalar(ki[:], ki[:], 7, None, ALU.logical_shift_right))
                ch.link(dve.tensor_copy(hi[:], ki[:]))
                dve.tensor_tensor(hot[:], hi[:].unsqueeze(2).to_broadcast([P, ET, NT]),
                                  g.iota25[:, 0:NT].unsqueeze(1).to_broadcast([P, ET, NT]), ALU.is_equal)
    return hot


def visit_tables(nc, name, g, key, ctx):
    sb = lambda n, s, d=F32: ctx.enter_context(nc.sbuf_tensor(n, s, d, allow_name_mangling=True))
    table = sb(name + "_table", [1, 2, V + SLOTS], I32)
    minus = sb(name + "_minus", [P, V])
    ends = sb(name + "_ends", [P, NT])
    with ExitStack() as c:
        tb = lambda n, s, d=F32: c.enter_context(nc.sbuf_tensor(n, s, d, allow_name_mangling=True))
        part = tb("part", [P, NT])
        junk = tb("junk", [P, 2, ET], BF16)
        work = tb("work", [P, 8, NT])
        work_i = tb("work_i", [P, 2, NT], I32)
        past = tb("past", [VG, VQ, NT])
        prod = tb("prod", [VG, VQ, NT])
        vi = tb("vi", [VG, VQ])
        both = tb("both_v", [VG, 2, VQ])
        spread = tb("spread", [VG, 2, VQ, VG])
        everywhere = c.enter_context(nc.psum_tensor("everywhere", [P, 2, 512], F32, allow_name_mangling=True))
        total = c.enter_context(nc.psum_tensor("total", [P, NT], F32, allow_name_mangling=True))
        sem = g.semaphores(c)
        s_part, s_total, s_vi, s_chain, s_spread, s_every = map(sem, ("s_part", "s_total", "s_vi", "s_chain", "s_spread", "s_every"))
        with nc.Block() as block:
            @block.gpsimd
            def _(pool):
                pool.iota(vi[:], [[VG, VQ]], base=0, channel_multiplier=1, allow_small_or_imprecise_dtypes=True).then_inc(s_vi, 1)

            @block.tensor
            def _(pe):
                pe.wait_ge(s_part, NT)
                pe.matmul(total[:], g.ones[:], part[:], start=True, stop=True).then_inc(s_total, 1)
                pe.wait_ge(s_spread, 1)
                for i in range(2):
                    mm = pe.matmul(everywhere[:, i, 0:V], g.ones[0:VG, :], spread[:, i].rearrange("p q v -> p (q v)"), start=True, stop=True)
                mm.then_inc(s_every, 1)

            @block.vector
            def _(dve):
                ch = Chain(dve, s_chain)
                for t in range(NT):
                    if t >= 2:
                        dve.wait_ge(s_part, t - 1)
                    dve.tensor_scalar(junk[:, t % 2, :], key[:], float(P * (t + 1)), None, ALU.is_lt, ALU.add,
                                      accum_out=part[:, t:t + 1]).then_inc(s_part, 1)
                dve.wait_ge(s_total, 1)
                ch.link(dve.tensor_copy(ends[:], total[:]))
                ch.link(dve.memset(work[:], 0.0))
                start, first, last, nvis, vend, off, step = (work[:, i, :] for i in range(7))
                ch.link(dve.tensor_copy(start[:, 1:NT], ends[:, 0:NT - 1]))
                ch.link(dve.tensor_copy(work_i[:, 0, :], start))
                ch.link(dve.tensor_scalar(work_i[:, 1, :], ends[:], -1.0, 0.0, ALU.add, ALU.max))
                ch.link(dve.tensor_scalar(work_i[:], work_i[:], 7, None, ALU.logical_shift_right))
                ch.link(dve.tensor_copy(work[:, 1:3, :], work_i[:]))
                ch.link(dve.tensor_tensor(nvis, last, first, ALU.subtract))
                ch.link(dve.tensor_scalar(nvis, nvis, 1.0, None, ALU.add))
                ch.link(dve.tensor_tensor(off, ends[:], start, ALU.is_gt))
                ch.link(dve.tensor_tensor(nvis, nvis, off, ALU.mult))
                ch.link(dve.tensor_tensor_scan(vend, g.ones[:, 0:NT], nvis, 0.0, ALU.mult, ALU.add))
                ch.link(dve.tensor_tensor(off, first, vend, ALU.subtract))
                ch.link(dve.tensor_tensor(off, off, nvis, ALU.add))
                ch.link(dve.tensor_tensor(step[:, 0:NT - 1], off[:, 1:NT], off[:, 0:NT - 1], ALU.subtract))
                dve.wait_ge(s_vi, 1)
                shape = [VG, VQ, NT]
                tv, kv = both[:, 0, :], both[:, 1, :]
                ch.link(dve.tensor_tensor(past[:], vi[:].unsqueeze(2).to_broadcast(shape),
                                          work[0:VG, 4, :].unsqueeze(1).to_broadcast(shape), ALU.is_ge))
                ch.link(dve.tensor_reduce(tv, past[:], AX.X, ALU.add))
                ch.link(dve.tensor_tensor(prod[:], past[:], work[0:VG, 6, :].unsqueeze(1).to_broadcast(shape), ALU.mult))
                ch.link(dve.tensor_reduce(kv, prod[:], AX.X, ALU.add))
                ch.link(dve.tensor_tensor(kv, kv, vi[:], ALU.add))
                ch.link(dve.tensor_scalar(kv, kv, work[0:VG, 5, 0:1], 0.0, ALU.add, ALU.max))
                ch.link(dve.tensor_tensor(spread[:], both[:].unsqueeze(3).to_broadcast([VG, 2, VQ, VG]),
                                          g.ident[0:VG, 0:VG].unsqueeze(1).unsqueeze(1).to_broadcast([VG, 2, VQ, VG]), ALU.mult))
                dve.sem_inc(s_spread, 1)
                ch.link(dve.memset(table[:], DUMMY))
                dve.wait_ge(s_every, 1)
                dve.tensor_scalar(table[:, 0, 0:V], everywhere[0:1, 1, 0:V], float(ET - 1), None, ALU.min)
                dve.tensor_copy(table[:, 1, LAG:LAG + V], everywhere[0:1, 0, 0:V])
                dve.tensor_scalar(minus[:], everywhere[:, 0, 0:V], -float(P), None, ALU.mult)
    return table, minus, ends


def normalise(nc, g, x, out, turned_out):
    with ExitStack() as c:
        tb = lambda n, s, d=F32: c.enter_context(nc.sbuf_tensor(n, s, d, allow_name_mangling=True))
        stats = tb("stats", [P, NT, 6])
        mv = tb("mv", [P, NT, 2])
        std = tb("std", [P, NT])
        rstd = tb("rstd", [P, NT])
        turn = [c.enter_context(nc.psum_tensor(f"turn{i}", [P, KC * P], F32, allow_name_mangling=True)) for i in range(4)]
        sem = g.semaphores(c)
        s_var, s_eps, s_std, s_norm, s_turn, s_copied, s_chain = map(
            sem, ("s_var", "s_eps", "s_std", "s_norm", "s_turn", "s_copied", "s_chain"))
        norm = x if out is None else out
        with nc.Block() as block:
            @block.vector
            def _(dve):
                if out is None:
                    dve.sem_inc(s_norm, NT)
                    return
                ch = Chain(dve, s_chain)
                for t in range(NT):
                    dve.bn_stats(stats[:, t, :], x[:, t, :]).then_inc(s_chain, 1)
                dve.wait_ge(s_chain, NT)
                for t in range(NT):
                    dve.bn_aggr(mv[:, t, :], stats[:, t, :]).then_inc(s_chain, 1)
                dve.wait_ge(s_chain, 2 * NT)
                dve.tensor_scalar(std[:], mv[:, :, 1], EPS, None, ALU.add).then_inc(s_var, 1)
                dve.wait_ge(s_std, 1)
                ch.count = 2 * NT
                ch.link(dve.reciprocal(rstd[:], std[:]))
                ch.link(dve.tensor_tensor(std[:], rstd[:], rstd[:], ALU.mult))
                ch.link(dve.scalar_tensor_tensor(std[:], mv[:, :, 1], EPS, std[:], ALU.add, ALU.mult))
                ch.link(dve.tensor_scalar(std[:], std[:], -0.5, 1.5, ALU.mult, ALU.add))
                ch.link(dve.tensor_tensor(rstd[:], rstd[:], std[:], ALU.mult))
                for t in range(NT):
                    dve.tensor_scalar(out[:, t, :], x[:, t, :], mv[:, t, 0:1], rstd[:, t:t + 1],
                                      ALU.subtract, ALU.mult).then_inc(s_norm, 1)

            @block.scalar
            def _(act):
                if out is not None:
                    act.wait_ge(s_var, 1)
                    act.activation(std[:], std[:], ACT.Sqrt).then_inc(s_std, 1)
                for t in range(NT):
                    act.wait_ge(s_turn, t + 1)
                    act.activation(turned_out[:, :, t * P:(t + 1) * P],
                                   turn[t % 4][:].rearrange("p (k n) -> p k n", k=KC), ACT.Copy).then_inc(s_copied, 1)

            @block.tensor
            def _(pe):
                for t in range(NT):
                    pe.wait_ge(s_norm, t + 1)
                    if t >= 4:
                        pe.wait_ge(s_copied, t - 3)
                    for k in range(KC):
                        mm = pe.transpose(turn[t % 4][:, k * P:(k + 1) * P], norm[:, t, k * P:(k + 1) * P], g.ident[:])
                    mm.then_inc(s_turn, 1)


def project(nc, g, name, turned, W, attention, heads, ctx):
    C = heads if attention else 0
    h = ctx.enter_context(nc.sbuf_tensor(name + "_h", [P, NT, D], F32, side="right"))
    al = ctx.enter_context(nc.sbuf_tensor(name + "_al", [P, NT, 2, max(C, 1)], F32, side="right"))
    table = nc.dram_tensor(name + "_table_dram", (NP, D), F32, kind="Internal").ap()
    with ExitStack() as c:
        tb = lambda n, s, d=F32: c.enter_context(nc.sbuf_tensor(n, s, d, allow_name_mangling=True))
        wcat = tb("wcat", [P, KC, D + 2 * C])
        wraw = tb("wraw", [P, KC, D])
        avec = tb("avec", [P, 2, D])
        prod = tb("prod_wa", [P, 2, KC, D])
        ps = [c.enter_context(nc.psum_tensor(f"proj{i}", [P, D + 2 * C], F32, allow_name_mangling=True)) for i in range(4)]
        sem = g.semaphores(c)
        s_w, s_chain, s_wcat, s_mm, s_h, s_out = map(sem, ("s_w", "s_chain", "s_wcat", "s_mm", "s_h", "s_out"))
        CHUNK = 5
        with nc.Block() as block:
            @block.sync
            def _(sp):
                flat_w = W.rearrange("(k p) h f -> p k (h f)", p=P) if len(W.shape) == 3 else W.rearrange("(k p) n -> p k n", p=P)
                sp.dma_start(wraw[:], flat_w).then_inc(s_w, 16)
                for i, a in enumerate(attention or ()):
                    sp.dma_start(avec[:, i, :], a.rearrange("(o h) f -> o (h f)", o=1).to_broadcast([P, D])).then_inc(s_w, 16)
                for j in range(0, NT, CHUNK):
                    sp.wait_ge(s_h, j + CHUNK)
                    sp.dma_start(table[j * P:(j + CHUNK) * P].rearrange("(t p) d -> p t d", p=P), h[:, j:j + CHUNK, :]).then_inc(s_out, 16)
                sp.wait_ge(s_out, 16 * (NT // CHUNK))

            @block.vector
            def _(dve):
                ch = Chain(dve, s_chain)
                dve.wait_ge(s_w, 48 if C else 16)
                dve.tensor_copy(wcat[:, :, 0:D], wraw[:]).then_inc(s_wcat, 1)
                for i in range(2 if C else 0):
                    ch.link(dve.tensor_tensor(prod[:, i], wraw[:], avec[:, i, :].unsqueeze(1).to_broadcast([P, KC, D]), ALU.mult))
                    for k in range(KC):
                        dve.tensor_reduce(wcat[:, k, D + i * C:D + (i + 1) * C],
                                          prod[:, i, k, :].rearrange("p (h f) -> p h f", h=C), AX.X, ALU.add).then_inc(s_wcat, 1)

            @block.tensor
            def _(pe):
                pe.wait_ge(s_wcat, 1 + 2 * KC if C else 1)
                for t in range(NT):
                    if t >= 4:
                        pe.wait_ge(s_h, t - 3)
                    for k in range(KC):
                        mm = pe.matmul(ps[t % 4][:], turned[:, k, t * P:(t + 1) * P], wcat[:, k, :], start=(k == 0), stop=(k == KC - 1))
                    mm.then_inc(s_mm, 1)

            @block.scalar
            def _(act):
                for t in range(NT):
                    act.wait_ge(s_mm, t + 1)
                    if C:
                        act.activation(al[:, t].rearrange("p s c -> p (s c)"), ps[t % 4][:, D:], ACT.Copy)
                    act.activation(h[:, t, :], ps[t % 4][:, 0:D], ACT.Copy).then_inc(s_h, 1)
    return h, al, table


def expand(nc, g, name, al, hots, heads, send_list, ctx):
    GROUP = 8
    C = heads
    BT = 16
    TB = 2 if C > 1 else BT
    NB = BT // TB
    RING = 4
    ae = [ctx.enter_context(nc.sbuf_tensor(f"{name}_ae{s}", [P, ET, C], F32)) for s in range(2)]
    with ExitStack() as c:
        tb = lambda n, s, d=F32: c.enter_context(nc.sbuf_tensor(n, s, d, allow_name_mangling=True))
        rest = tb("rest", [P, 2, C, NT])
        part = [tb(f"part{j}", [P, 2, C, NT], BF16) for j in range(3)]
        lo_rows = [[tb(f"lo_rows{s}{j}", [P, BT * P], BF16) for j in range(2)] for s in range(2)]
        hot_lo = [[tb(f"hot_lo{s}{j}", [P, BT * P], BF16) for j in range(2)] for s in range(2)]
        sel = [tb(f"sel{r}", [P, TB, C, NT]) for r in range(RING)]
        ps = [c.enter_context(nc.psum_tensor(f"picked{r}", [P, TB, C, NT], F32, allow_name_mangling=True)) for r in range(RING)]
        sem = g.semaphores(c)
        s_chain, s_parts, s_hot, s_bank, s_sel, s_red = map(sem, ("s_chain", "s_parts", "s_hot", "s_bank", "s_sel", "s_red"))
        s_lo = [[sem(f"s_lo{s}{j}") for j in range(2)] for s in range(2)]
        BLOCKS = ET // BT
        if send_list:
            spot_now = [tb(f"spot_now{j}", [P, GROUP], I32) for j in range(2)]
            load_now = [tb(f"load_now{j}", [P, GROUP, 4]) for j in range(2)]
            s_staged, s_go = map(sem, ("s_staged", "s_go"))
            s_sent = [sem("s_sent0"), sem("s_sent1")]
        with nc.Block() as block:
            @block.gpsimd
            def _(pool):
                if not send_list:
                    return
                for j in range(2):
                    pool.memset(load_now[j][:], 0.0).then_inc(s_staged, 1)
                pool.wait_ge(s_staged, 2)

                def send(i, peeled):
                    for j in range(2):
                        if not peeled:
                            pool.wait_ge(s_sent[j], 16 * GROUP * i)
                        pool.tensor_copy(spot_now[j][:], g.spot[:, bass.ds((2 * i + j) * GROUP, GROUP)]).then_inc(s_staged, 1)
                        for f, values in enumerate((g.dst_key, g.src_key, g.weight)):
                            pool.tensor_copy(load_now[j][:, :, f], values[:, bass.ds((2 * i + j) * GROUP, GROUP)]).then_inc(s_staged, 1)
                        pool.wait_ge(s_staged, 8 * i + (4 * j + 6))
                        pool.sem_inc(s_go, 1)
                        for u in range(GROUP):
                            pool.indirect_dma_start(out=g.list_dram, out_offset=bass.IndirectOffsetOnAxis(ap=spot_now[j][:, u:u + 1], axis=0),
                                                    in_=load_now[j][:, u, :], in_offset=None).then_inc(s_sent[j], 16)

                send(0, True)
                with pool.Fori(1, ET // (2 * GROUP)) as i:
                    send(i, False)
                for j in range(2):
                    pool.wait_ge(s_sent[j], 16 * GROUP * (ET // (2 * GROUP)))

            @block.sync
            def _(sp):
                with sp.Fori(0, BLOCKS // 2) as i:
                    for j in range(2):
                        for s in range(2):
                            n = 2 * i + j
                            sp.wait_ge(s_hot, 4 * i + (2 * j + s + 1))
                            sp.dma_start(lo_rows[s][j][:], g.lo_dram[s].rearrange("(o n) -> o n", o=1)[:, bass.ds(n * (BT * P), BT * P)]
                                         .to_broadcast([P, BT * P])).then_inc(s_lo[s][j], 16)

            @block.vector
            def _(dve):
                ch = Chain(dve, s_chain)
                ch.link(dve.tensor_copy(rest[:], al[:].rearrange("p t s c -> p s c t")))
                for j in range(3):
                    ch.link(dve.tensor_copy(part[j][:], rest[:]))
                    if j < 2:
                        ch.link(dve.tensor_tensor(rest[:], rest[:], part[j][:], ALU.subtract))
                dve.sem_inc(s_parts, 1)
                dve.sem_inc(s_hot, 4)
                dve.sem_inc(s_bank, 4 * NB)
                dve.sem_inc(s_sel, RING)
                dve.sem_inc(s_red, RING)

                def compare(i, j):
                    for s in range(2):
                        dve.wait_ge(s_lo[s][j], 16 * i + 16)
                        dve.wait_ge(s_bank, 4 * NB * i + (2 * NB * j + NB * (s + 1)))
                        dve.tensor_scalar(hot_lo[s][j][:], lo_rows[s][j][:], g.iota_col[:, 0:1], None, ALU.is_equal).then_inc(s_hot, 1)

                def select(i, j):
                    tile = lambda b: bass.ds((2 * i + j) * BT + (b % NB) * TB, TB)
                    for b in range(2 * NB + 1):
                        at = 2 * NB * j + b
                        if b < 2 * NB:
                            dve.wait_ge(s_bank, 4 * NB * i + (at + 1 + 4 * NB))
                            dve.wait_ge(s_red, 4 * NB * i + (at + 1))
                            dve.tensor_tensor(sel[at % RING][:], ps[at % RING][:],
                                              hots[b // NB][:, tile(b), :].unsqueeze(2).to_broadcast([P, TB, C, NT]),
                                              ALU.mult).then_inc(s_sel, 1)
                        if b >= 1:
                            dve.wait_ge(s_sel, 4 * NB * i + (at + RING))
                            dve.tensor_reduce(ae[(b - 1) // NB][:, tile(b - 1), :], sel[(at - 1) % RING][:], AX.X, ALU.add).then_inc(s_red, 1)

                compare(0, 0)
                with dve.Fori(0, BLOCKS // 2 - 1) as i:
                    compare(i, 1)
                    select(i, 0)
                    compare(i + 1, 0)
                    select(i, 1)
                compare(BLOCKS // 2 - 1, 1)
                select(BLOCKS // 2 - 1, 0)
                select(BLOCKS // 2 - 1, 1)

            @block.tensor
            def _(pe):
                pe.wait_ge(s_parts, 1)
                with pe.Fori(0, BLOCKS // 2) as i:
                    for at in range(4 * NB):
                        j, b = at // (2 * NB), at % (2 * NB)
                        s, r = b // NB, at % RING
                        if b % NB == 0:
                            pe.wait_ge(s_hot, 4 * i + (2 * j + s + 5))
                        pe.wait_ge(s_sel, 4 * NB * i + (at + 1))
                        for k in range(TB):
                            tile = (b % NB) * TB + k
                            for n in range(3):
                                mm = pe.matmul(ps[r][:, k].rearrange("p c t -> p (c t)"), hot_lo[s][j][:, tile * P:(tile + 1) * P],
                                               part[n][:, s].rearrange("p c t -> p (c t)"), start=(n == 0), stop=(n == 2))
                        mm.then_inc(s_bank, 1)
    return ae


def edge_softmax(nc, g, name, ae, dst, heads, ctx):
    C = heads
    R = CH * C
    ext = ctx.enter_context(nc.sbuf_tensor(name + "_ext", [P, ET, 2 * C + 2], F32, side="right"))
    with ExitStack() as c:
        tb = lambda n, s, d=F32: c.enter_context(nc.sbuf_tensor(n, s, d, allow_name_mangling=True))
        run = tb("run", [P, CL])
        d_i = run[0:R, :].bitcast(I32)
        d_all = tb("d_all", [P, CL])
        d_f = d_all[0:R, :]
        run = run[0:R, :]
        brk = tb("brk", [R, CL + 1])
        val = tb("val", [R, CL])
        most = d_all[:, 0:ET * C].rearrange("p (k c) -> p k c", c=C)
        ends = tb("ends_c", [R, 4])
        row = tb("row", [1, 4, R])
        hc = tb("hc", [1, 6, C, CH])
        back = tb("back", [R, 4])
        ps = [c.enter_context(nc.psum_tensor(f"sx{r}", [P, 4, P], F32, allow_name_mangling=True)) for r in range(4)]
        small = c.enter_context(nc.psum_tensor("small", [P, 512], F32, allow_name_mangling=True))
        sem = g.semaphores(c)
        s_pad, s_d, s_in, s_val, s_ends, s_row, s_back_row, s_back, s_run, s_out, s_most, s_logit, s_p, s_chain = map(sem, (
            "s_pad", "s_d", "s_in", "s_val", "s_ends", "s_row", "s_back_row", "s_back", "s_run", "s_out", "s_most", "s_logit", "s_p", "s_chain"))
        s_step = sem("s_step")
        by_step = ext[:].rearrange("p k x -> p (k x)")[:, 0:ET * C]
        G4 = -(-CI // 4)
        tail = E - (CH - 1) * CL
        ids = g.ident
        with nc.Block() as block:
            @block.sync
            def _(sp):
                sp.wait_ge(s_pad, 1)
                sp.dma_start(d_i[0:R - C, :], dst[0:(CH - 1) * CL].rearrange("(c n) -> c n", n=CL).unsqueeze(1).to_broadcast([CH - 1, C, CL])).then_inc(s_d, 16)
                sp.dma_start(d_i[R - C:R, 0:tail], dst[(CH - 1) * CL:E].rearrange("(o n) -> o n", o=1).to_broadcast([C, tail])).then_inc(s_d, 16)

            @block.tensor
            def _(pe):
                pe.wait_ge(s_step, 1)
                for q in range(G4):
                    if q >= 4:
                        pe.wait_ge(s_val, q - 3)
                    for i in range(4 * q, min(CI, 4 * q + 4)):
                        mm = pe.transpose(ps[q % 4][0:R, i % 4, :], by_step[:, i * R:(i + 1) * R], ids[:])
                    mm.then_inc(s_in, 1)
                pe.wait_ge(s_ends, 1)
                for i in range(4):
                    mm = pe.transpose(small[0:1, i * R:(i + 1) * R], ends[:, i:i + 1], ids[0:R, 0:R])
                mm.then_inc(s_row, 1)
                pe.wait_ge(s_back_row, 1)
                for i in range(4):
                    mm = pe.transpose(small[0:R, i:i + 1], row[0:1, i, :], ids[0:1, 0:1])
                mm.then_inc(s_back, 1)
                pe.wait_ge(s_run, 1)
                for q in range(G4):
                    if q >= 4:
                        pe.wait_ge(s_most, q - 3)
                    for i in range(4 * q, min(CI, 4 * q + 4)):
                        mm = pe.transpose(ps[q % 4][:, i % 4, 0:R], val[:, i * P:(i + 1) * P], ids[0:R, 0:R])
                    mm.then_inc(s_out, 1)

            @block.scalar
            def _(act):
                act.activation(by_step.rearrange("p (i c h) -> p i c h", c=CH, h=C),
                               ae[0][:].rearrange("p (c i) h -> p i c h", i=CI), ACT.Copy).then_inc(s_step, 1)
                for q in range(G4):
                    n = min(CI, 4 * q + 4) - 4 * q
                    act.wait_ge(s_in, q + 1)
                    act.activation(val[:, 4 * q * P:(4 * q + n) * P].rearrange("r (a b) -> r a b", b=P), ps[q % 4][0:R, 0:n, :], ACT.Copy).then_inc(s_val, 1)
                for q in range(G4):
                    n = min(CI, 4 * q + 4) - 4 * q
                    act.wait_ge(s_out, q + 1)
                    act.activation(most[:].rearrange("p (c i) h -> p i c h", i=CI)[:, 4 * q:4 * q + n],
                                   ps[q % 4][:, 0:n, 0:R].rearrange("p i (c h) -> p i c h", h=C), ACT.Copy).then_inc(s_most, 1)
                act.wait_ge(s_logit, 1)
                act.activation(ext[:, :, 0:C], ae[0][:], ACT.Exp).then_inc(s_p, 1)

            @block.vector
            def _(dve):
                ch = Chain(dve, s_chain)
                dve.memset(d_i[:], PAD_KEY).then_inc(s_pad, 1)
                ch.link(dve.memset(brk[:], -BIG))
                dve.wait_ge(s_d, 32)
                ch.link(dve.tensor_copy(d_f[:], d_i[:]))
                ch.link(dve.tensor_tensor(brk[:, 1:CL], d_f[:, 1:CL], d_f[:, 0:CL - 1], ALU.not_equal))
                ch.link(dve.tensor_scalar(brk[:, 1:CL], brk[:, 1:CL], -BIG, None, ALU.mult))
                dve.wait_ge(s_val, G4)
                ch.link(dve.tensor_tensor_scan(run[:], brk[:, 0:CL], val[:], 0.0, ALU.add, ALU.max))
                ch.link(dve.tensor_copy(ends[:, 0:1], run[:, CL - 1:CL]))
                ch.link(dve.tensor_tensor_scan(val[:, ::-1], brk[:, 1:CL + 1][:, ::-1], run[:, ::-1], 0.0, ALU.add, ALU.max))
                dve.tensor_copy(ends[:, 1:2], val[:, 0:1])
                dve.tensor_copy(ends[:, 2:3], d_f[:, CL - 1:CL])
                ch.link(dve.tensor_copy(ends[:, 3:4], d_f[:, 0:1]))
                dve.sem_inc(s_ends, 1)
                dve.wait_ge(s_row, 1)
                fend, mbeg, dlast, dfirst, wf, wb = (hc[:, i] for i in range(6))
                for i in range(4):
                    last = dve.tensor_copy(hc[:, i], small[0:1, i * R:(i + 1) * R].rearrange("o (c h) -> o h c", h=C))
                ch.link(last)
                dve.memset(wf[:, :, 0:1], 1.0)
                dve.memset(wb[:, :, CH - 1:CH], 1.0)
                dve.tensor_tensor(wf[:, :, 1:CH], dlast[:, :, 1:CH], dlast[:, :, 0:CH - 1], ALU.not_equal)
                ch.link(dve.tensor_tensor(wb[:, :, 0:CH - 1], dfirst[:, :, 1:CH], dfirst[:, :, 0:CH - 1], ALU.not_equal))
                ch.link(dve.tensor_scalar(hc[:, 4:6], hc[:, 4:6], -BIG, None, ALU.mult))
                one = lambda a: a.rearrange("o h c -> o (h c)")
                ch.link(dve.tensor_tensor_scan(one(fend), one(wf), one(fend), 0.0, ALU.add, ALU.max))
                ch.link(dve.tensor_tensor_scan(one(mbeg)[:, ::-1], one(wb)[:, ::-1], one(mbeg)[:, ::-1], 0.0, ALU.add, ALU.max))
                ch.link(dve.memset(row[:], -BIG))
                r4 = row[:].rearrange("o f (c h) -> o f c h", h=C)
                sw = lambda a: a.rearrange("o h c -> o c h")
                dve.tensor_copy(r4[:, 0, 1:CH], sw(fend)[:, 0:CH - 1])
                dve.tensor_copy(r4[:, 1, 0:CH - 1], sw(mbeg)[:, 1:CH])
                dve.tensor_copy(r4[:, 2, 1:CH], sw(dlast)[:, 0:CH - 1])
                ch.link(dve.tensor_copy(r4[:, 3, 0:CH - 1], sw(dfirst)[:, 1:CH]))
                dve.sem_inc(s_back_row, 1)
                dve.wait_ge(s_back, 1)
                ch.link(dve.tensor_copy(back[:], small[0:R, 0:4]))
                for j in range(2):
                    ch.link(dve.tensor_scalar(run[:], d_f[:], back[:, 2 + j:3 + j], -BIG, ALU.not_equal, ALU.mult))
                    ch.link(dve.scalar_tensor_tensor(val[:], run[:], back[:, j:j + 1], val[:], ALU.add, ALU.max))
                dve.sem_inc(s_run, 1)
                lo = ae[0][:]
                ch.link(dve.tensor_tensor(lo, ae[0][:], ae[1][:], ALU.add))
                ch.link(dve.scalar_tensor_tensor(lo, lo, NEG, lo, ALU.mult, ALU.max))
                dve.wait_ge(s_most, G4)
                dve.tensor_copy(ext[:, :, 2 * C:2 * C + 1], g.is_last[:].unsqueeze(2))
                dve.tensor_copy(ext[:, :, 2 * C + 1:2 * C + 2], g.dst_key[:].unsqueeze(2))
                dve.tensor_tensor(ext[:, :, C:2 * C], most[:], g.is_last[:].unsqueeze(2).to_broadcast([P, ET, C]), ALU.mult)
                ch.link(dve.tensor_tensor(ae[1][:], most[:], ae[1][:], ALU.add))
                ch.link(dve.scalar_tensor_tensor(ae[1][:], ae[1][:], NEG, ae[1][:], ALU.mult, ALU.max))
                ch.link(dve.tensor_tensor(lo, lo, ae[1][:], ALU.subtract))
                dve.sem_inc(s_logit, 1)
    return ext


def aggregate(nc, g, name, table, idx, visits, values, heads, summed, acc):
    vt, minus = visits
    VW = values.shape[2]
    W = D + summed
    with ExitStack() as c:
        tb = lambda n, s, d=F32: c.enter_context(nc.sbuf_tensor(n, s, d, allow_name_mangling=True))
        idx_now = [tb(f"idx_now{u}", [P, 1], I32) for u in range(SLOTS)]
        rows = [tb(f"rows{u}", [P, D]) for u in range(SLOTS)]
        msg = [tb(f"msg{u}", [P, D + VW]) for u in range(SLOTS)]
        hot = [tb(f"hot{u}", [P, P]) for u in range(SLOTS)]
        ps = [c.enter_context(nc.psum_tensor(f"sum{u}", [P, W], F32, allow_name_mangling=True)) for u in range(SLOTS)]
        sem = g.semaphores(c)
        s_go, s_act, s_idx, s_values, s_msg, s_sum, s_acc, s_hot = map(sem, ("s_go", "s_act", "s_idx", "s_values", "s_msg", "s_sum", "s_acc", "s_hot"))
        s_rows = [sem(f"s_rows{u}") for u in range(SLOTS)]
        ROUNDS = V // SLOTS
        eng = mybir.EngineType
        def of_round(which, row, i):
            _, values = nc.values_load_multi_w_load_instructions(
                vt[0:1, row, bass.ds(i * SLOTS, SLOTS)], engines=(which,), min_val=0, max_val=(ET - 1, DUMMY)[row],
                skip_runtime_bounds_check_because="the table's values are clamped where it is made")
            return values
        with nc.Block() as block:
            @block.gpsimd
            def _(pool):
                with pool.Fori(0, ROUNDS) as i:
                    for u in range(SLOTS):
                        pool.wait_ge(s_idx, SLOTS * i + (u + 1))
                        pool.wait_ge(s_msg, SLOTS * i + (u + 1))
                        pool.sem_inc(s_go, 1)
                        pool.indirect_dma_start(out=rows[u][:], out_offset=None, in_=table,
                                                in_offset=bass.IndirectOffsetOnAxis(ap=idx_now[u][:], axis=0)).then_inc(s_rows[u], 16)

            @block.scalar
            def _(act):
                with act.Fori(0, ROUNDS) as i:
                    ks = of_round(eng.Activation, 0, i)
                    for u in range(SLOTS):
                        act.wait_ge(s_msg, SLOTS * i + (u + 1))
                        act.sem_inc(s_act, 1)
                        act.activation(idx_now[u][:], idx[:, bass.ds(ks[u], 1)], ACT.Copy).then_inc(s_idx, 1)
                        act.wait_ge(s_sum, SLOTS * i + (u + 1))
                        act.sem_inc(s_act, 1)
                        act.activation(msg[u][:, D:], values[:, bass.ds(ks[u], 1), :].rearrange("p o x -> p (o x)"), ACT.Copy).then_inc(s_values, 1)

            @block.vector
            def _(dve):
                dve.sem_inc(s_msg, SLOTS)
                dve.sem_inc(s_sum, SLOTS)
                dve.memset(acc[:], 0.0).then_inc(s_acc, 1)
                for u in range(SLOTS - LAG, SLOTS):
                    dve.memset(ps[u][:], 0.0).then_inc(s_acc, 1)
                dve.sem_inc(s_acc, SLOTS - LAG)

                def add(i, u, ts):
                    dve.wait_ge(s_sum, SLOTS * i + (u - LAG + 1 + SLOTS))
                    dve.wait_ge(s_acc, SLOTS * i + (u + 1 + SLOTS))
                    into = acc[:, bass.ds(ts[u], 1), :].rearrange("p o w -> p (o w)")
                    dve.tensor_tensor(into, ps[(u - LAG) % SLOTS][:], into, ALU.add).then_inc(s_acc, 1)

                with dve.Fori(0, ROUNDS) as i:
                    ts = of_round(eng.DVE, 1, i)
                    for u in range(SLOTS):
                        dve.wait_ge(s_values, SLOTS * i + (u + 1))
                        dve.tensor_scalar(hot[u][:], g.iota_row[:], msg[u][:, D + VW - 1:], minus[:, bass.ds(SLOTS * i + u, 1)],
                                          ALU.subtract, ALU.is_equal).then_inc(s_hot, 1)
                        dve.wait_ge(s_rows[u], 16 * i + 16)
                        if heads == 1:
                            dve.tensor_scalar(msg[u][:, 0:D], rows[u][:], msg[u][:, D:D + 1], None, ALU.mult).then_inc(s_msg, 1)
                        else:
                            dve.tensor_tensor(msg[u][:, 0:D].rearrange("p (h f) -> p h f", h=heads), rows[u][:].rearrange("p (h f) -> p h f", h=heads),
                                              msg[u][:, D:D + heads].unsqueeze(2).to_broadcast([P, heads, D // heads]), ALU.mult).then_inc(s_msg, 1)
                        add(i, u, ts)
                ts = of_round(eng.DVE, 1, ROUNDS)
                for u in range(LAG):
                    add(ROUNDS, u, ts)

            @block.tensor
            def _(pe):
                with pe.Fori(0, ROUNDS) as i:
                    for u in range(SLOTS):
                        pe.wait_ge(s_hot, SLOTS * i + (u + 1))
                        pe.wait_ge(s_acc, SLOTS * i + (u + LAG + 2))
                        pe.wait_ge(s_msg, SLOTS * i + (u + 1 + SLOTS))
                        pe.matmul(ps[u][:], hot[u][:], msg[u][:, 0:W], start=True, stop=True).then_inc(s_sum, 1)


def finish_attention(nc, g, acc, h, al, bias, heads, x):
    C = heads
    with ExitStack() as c:
        tb = lambda n, s, d=F32: c.enter_context(nc.sbuf_tensor(n, s, d, allow_name_mangling=True))
        b_row = tb("b_row", [P, D])
        w = tb("w_fin", [P, 7, NT, C])
        sem = g.semaphores(c)
        s_b, s_chain, s_logit, s_exp, s_coef, s_own, s_num = map(sem, ("s_b", "s_chain", "s_logit", "s_exp", "s_coef", "s_own", "s_num"))
        own, near, top, den, c_near, c_own, spare = (w[:, i] for i in range(7))
        heads_of = lambda a: a.rearrange("p t (h f) -> p t h f", h=C)
        over = lambda a: a.unsqueeze(3).to_broadcast([P, NT, C, D // C])
        sums = acc[:, 0:NT, 0:D]
        with nc.Block() as block:
            @block.sync
            def _(sp):
                sp.dma_start(b_row[:], bias.rearrange("(o d) -> o d", o=1).to_broadcast([P, D])).then_inc(s_b, 16)

            @block.vector
            def _(dve):
                ch = Chain(dve, s_chain)
                ch.link(dve.tensor_scalar(spare, acc[:, 0:NT, D + 2 * C:].to_broadcast([P, NT, C]), -1.0, BIG, ALU.add, ALU.mult))
                ch.link(dve.tensor_tensor(near, acc[:, 0:NT, D + C:D + 2 * C], spare, ALU.add))
                ch.link(dve.tensor_tensor(near, near, al[:, :, 1, :], ALU.add))
                ch.link(dve.tensor_tensor(own, al[:, :, 0, :], al[:, :, 1, :], ALU.add))
                ch.link(dve.scalar_tensor_tensor(w[:, 0:2], w[:, 0:2], NEG, w[:, 0:2], ALU.mult, ALU.max))
                ch.link(dve.tensor_tensor(top, own, near, ALU.max))
                ch.link(dve.tensor_tensor(w[:, 0:2], w[:, 0:2], top.unsqueeze(1).to_broadcast([P, 2, NT, C]), ALU.subtract))
                dve.sem_inc(s_logit, 1)
                dve.wait_ge(s_exp, 1)
                ch.link(dve.tensor_tensor(den, acc[:, 0:NT, D:D + C], near, ALU.mult))
                ch.link(dve.tensor_tensor(den, den, own, ALU.add))
                ch.link(dve.tensor_scalar(den, den, 1e-16, None, ALU.add))
                ch.link(dve.reciprocal(spare, den))
                ch.link(dve.tensor_tensor(c_own, own, spare, ALU.mult))
                dve.sem_inc(s_coef, 1)
                ch.link(dve.tensor_tensor(c_near, near, spare, ALU.mult))
                ch.link(dve.tensor_tensor(heads_of(sums), heads_of(sums), over(c_near), ALU.mult))
                if x is not None:
                    ch.link(dve.tensor_tensor(x[:], x[:], sums, ALU.add))
                dve.wait_ge(s_own, 2)
                into = x[:] if x is not None else sums
                dve.tensor_tensor(into, into, h[:], ALU.add)

            @block.scalar
            def _(act):
                act.wait_ge(s_logit, 1)
                act.activation(w[:, 0:2], w[:, 0:2], ACT.Exp).then_inc(s_exp, 1)

            @block.gpsimd
            def _(pool):
                pool.wait_ge(s_coef, 1)
                pool.tensor_tensor(heads_of(h[:]), heads_of(h[:]), over(c_own), ALU.mult).then_inc(s_own, 1)
                pool.wait_ge(s_own, 1)
                pool.wait_ge(s_b, 16)
                pool.tensor_tensor(h[:], h[:], b_row[:].unsqueeze(1).to_broadcast([P, NT, D]), ALU.add).then_inc(s_own, 1)


def by_source(nc, g, hot, ends, zero_dram, ctx):
    sb = lambda n, s, d=F32: ctx.enter_context(nc.sbuf_tensor(n, s, d, allow_name_mangling=True))
    g.spot = sb("spot", [P, ET], I32)
    ZT = 8
    g.list_dram = nc.dram_tensor("list_dram", (EP, 4), F32, kind="Internal").ap()
    with ExitStack() as c:
        tb = lambda n, s, d=F32: c.enter_context(nc.sbuf_tensor(n, s, d, allow_name_mangling=True))
        rank = tb("rank", [P, NT, ET])
        total = tb("total", [P, NT])
        base = tb("base", [P, NT])
        place = tb("place", [P, ET])
        number = tb("number", [P, ET])
        ps = c.enter_context(nc.psum_tensor("base_ps", [P, NT], F32, allow_name_mangling=True))
        sem = g.semaphores(c)
        s_number, s_scan, s_total, s_base, s_chain, s_zero, s_zeroed = map(
            sem, ("s_number", "s_scan", "s_total", "s_base", "s_chain", "s_zero", "s_zeroed"))
        zeros = tb("zeros", [P, ZT, D])
        with nc.Block() as block:
            @block.sync
            def _(sp):
                sp.wait_ge(s_zero, 1)
                for r in range(0, ST, ZT):
                    sp.dma_start(zero_dram[r * P:(r + ZT) * P].rearrange("(p a) d -> p a d", p=P), zeros[:]).then_inc(s_zeroed, 16)
                sp.wait_ge(s_zeroed, 16 * (ST // ZT))

            @block.gpsimd
            def _(pool):
                pool.memset(zeros[:], 0.0).then_inc(s_zero, 1)
                pool.iota(number[:], [[P, ET]], base=0, channel_multiplier=1, allow_small_or_imprecise_dtypes=True).then_inc(s_number, 1)

            @block.tensor
            def _(pe):
                pe.wait_ge(s_total, 1)
                pe.matmul(ps[:], g.before[:], total[:], start=True, stop=True).then_inc(s_base, 1)

            @block.vector
            def _(dve):
                ch = Chain(dve, s_chain)
                for t in range(NT):
                    dve.tensor_tensor_scan(rank[:, t, :], g.ones[:, 0:1].to_broadcast([P, ET]), hot[:, :, t], 0.0,
                                           ALU.mult, ALU.add).then_inc(s_scan, 1)
                dve.wait_ge(s_scan, NT)
                dve.tensor_copy(total[:], rank[:, :, ET - 1]).then_inc(s_total, 1)
                dve.wait_ge(s_base, 1)
                ch.link(dve.tensor_scalar(base[:], ps[:], -1.0, None, ALU.add))
                ch.link(dve.tensor_tensor(base[:, 1:NT], base[:, 1:NT], ends[:, 0:NT - 1], ALU.add))
                ch.link(dve.tensor_tensor(rank[:], rank[:], base[:].unsqueeze(2).to_broadcast([P, NT, ET]), ALU.add))
                ch.link(dve.tensor_tensor(rank[:], rank[:], hot[:].rearrange("p k t -> p t k"), ALU.mult))
                ch.link(dve.tensor_reduce(place[:], rank[:].rearrange("p t k -> p k t"), AX.X, ALU.add))
                dve.wait_ge(s_number, 1)
                ch.link(dve.scalar_tensor_tensor(number[:], g.src_key[:], float(NP), number[:], ALU.is_ge, ALU.mult))
                ch.link(dve.tensor_tensor(g.spot[:], place[:], number[:], ALU.add))


def read_list(nc, g, ctx):
    sb = lambda n, s, d=F32: ctx.enter_context(nc.sbuf_tensor(n, s, d, allow_name_mangling=True))
    idx = sb("l_idx", [P, ET], I32)
    values = sb("l_values", [P, ET, 2])
    with ExitStack() as c:
        rows = c.enter_context(nc.sbuf_tensor("l_rows", [P, RG, P, 4], F32, allow_name_mangling=True))
        ps = c.enter_context(nc.psum_tensor("l_turned", [P, 3, 512], F32, allow_name_mangling=True))
        s_rows, s_turned = map(g.semaphores(c), ("s_rows", "s_turned"))
        with nc.Block() as block:
            @block.sync
            def _(sp):
                o = g.list_dram
                sp.dma_start(rows[:, 0:3], o[0:3 * P * P].rearrange("(g k e) f -> k g e f", k=P, e=P)).then_inc(s_rows, 16)
                sp.dma_start(rows[0:ET - 3 * P, 3], o[3 * P * P:EP].rearrange("(k e) f -> k e f", e=P)).then_inc(s_rows, 16)

            @block.tensor
            def _(pe):
                pe.wait_ge(s_rows, 32)
                for f in range(3):
                    for r in range(RG):
                        k = min(P, ET - r * P)
                        mm = pe.transpose(ps[:, f, r * P:r * P + k], rows[0:k, r, :, f], g.ident[0:k, 0:k])
                mm.then_inc(s_turned, 1)

            @block.vector
            def _(dve):
                dve.wait_ge(s_turned, 1)
                dve.tensor_scalar(idx[:], ps[:, 0, 0:ET], float(N - 1), None, ALU.min)
                dve.tensor_copy(values[:, :, 0], ps[:, 2, 0:ET])
                dve.tensor_copy(values[:, :, 1], ps[:, 1, 0:ET])
    return idx, values


def gate(nc, g, name, turned, gate_w, gate_b, ctx):
    probs = ctx.enter_context(nc.sbuf_tensor(name + "_probs", [P, NT, EXPERTS], F32))
    with ExitStack() as c:
        tb = lambda n, s, d=F32: c.enter_context(nc.sbuf_tensor(n, s, d, allow_name_mangling=True))
        w = tb("gate_w", [P, KC, EXPERTS])
        b = tb("gate_b", [P, EXPERTS])
        top = tb("gate_top", [P, 2, NT])
        ps = c.enter_context(nc.psum_tensor("gate_ps", [P, NT, EXPERTS], F32, allow_name_mangling=True))
        sem = g.semaphores(c)
        s_w, s_mm, s_logit, s_exp, s_chain = map(sem, ("s_w", "s_mm", "s_logit", "s_exp", "s_chain"))
        shape = [P, NT, EXPERTS]
        with nc.Block() as block:
            @block.sync
            def _(sp):
                sp.dma_start(w[:], gate_w.rearrange("(k p) e -> p k e", p=P)).then_inc(s_w, 16)
                sp.dma_start(b[:], gate_b.rearrange("(o e) -> o e", o=1).to_broadcast([P, EXPERTS])).then_inc(s_w, 16)

            @block.tensor
            def _(pe):
                pe.wait_ge(s_w, 32)
                for t in range(NT):
                    for k in range(KC):
                        mm = pe.matmul(ps[:, t, :], turned[:, k, t * P:(t + 1) * P], w[:, k, :], start=(k == 0), stop=(k == KC - 1))
                mm.then_inc(s_mm, 1)

            @block.scalar
            def _(act):
                act.wait_ge(s_logit, 1)
                act.activation(probs[:], probs[:], ACT.Exp).then_inc(s_exp, 1)

            @block.vector
            def _(dve):
                ch = Chain(dve, s_chain)
                dve.wait_ge(s_w, 32)
                dve.wait_ge(s_mm, 1)
                ch.link(dve.tensor_tensor(probs[:], ps[:], b[:].unsqueeze(1).to_broadcast(shape), ALU.add))
                ch.link(dve.tensor_reduce(top[:, 0], probs[:], AX.X, ALU.max))
                ch.link(dve.tensor_tensor(probs[:], probs[:], top[:, 0].unsqueeze(2).to_broadcast(shape), ALU.subtract))
                dve.sem_inc(s_logit, 1)
                dve.wait_ge(s_exp, 1)
                ch.link(dve.tensor_reduce(top[:, 0], probs[:], AX.X, ALU.add))
                ch.link(dve.reciprocal(top[:, 1], top[:, 0]))
                ch.link(dve.tensor_tensor(probs[:], probs[:], top[:, 1].unsqueeze(2).to_broadcast(shape), ALU.mult))
    return probs


def bias_columns(nc, g, b, parts, ctx):
    cols = ctx.enter_context(nc.sbuf_tensor("b1_cols", [P, EXPERTS, parts], F32, allow_name_mangling=True))
    with ExitStack() as c:
        rows = c.enter_context(nc.sbuf_tensor("b1_rows", [EXPERTS * parts, P], F32, allow_name_mangling=True))
        ps = c.enter_context(nc.psum_tensor("b1_ps", [P, EXPERTS * parts], F32, allow_name_mangling=True))
        s_rows, s_turned = map(g.semaphores(c), ("s_rows", "s_turned"))
        with nc.Block() as block:
            @block.sync
            def _(sp):
                sp.dma_start(rows[:], b.rearrange("e (k p) -> (e k) p", p=P)).then_inc(s_rows, 16)

            @block.tensor
            def _(pe):
                pe.wait_ge(s_rows, 16)
                pe.transpose(ps[:], rows[:], g.ident[0:EXPERTS * parts, 0:EXPERTS * parts]).then_inc(s_turned, 1)

            @block.vector
            def _(dve):
                dve.wait_ge(s_turned, 1)
                dve.tensor_copy(cols[:].rearrange("p e k -> p (e k)"), ps[:])
    return cols


def first_largest(dve, ch, g, values, best, hot, work):
    shape = [P, NT, EXPERTS]
    ch.link(dve.tensor_reduce(best, values, AX.X, ALU.max))
    ch.link(dve.tensor_tensor(hot, values, best.unsqueeze(2).to_broadcast(shape), ALU.is_equal))
    ch.link(dve.tensor_tensor(hot, hot, g.falling[:].unsqueeze(1).to_broadcast(shape), ALU.mult))
    ch.link(dve.tensor_reduce(work, hot, AX.X, ALU.max))
    ch.link(dve.tensor_tensor(hot, hot, work.unsqueeze(2).to_broadcast(shape), ALU.is_equal))


def route_top2(nc, g, probs, xn, rows_dram, W1, W2, b2, ctx):
    FC = F1 // P
    sb = lambda n, s, d=F32: ctx.enter_context(nc.sbuf_tensor(n, s, d, allow_name_mangling=True))
    m = Mixture()
    m.take = sb("take2", [P, 2, NT], I32)
    m.factor = sb("factor2", [P, 2, NT])
    m.cw = sb("cw", [P, NT, EXPERTS])
    m.expert_of = sb("expert_of", [1, ST], I32)
    m.w1 = sb("w1_all", [P, EXPERTS, KC, F1])
    m.w2 = sb("w2_all", [P, EXPERTS, FC, D])
    m.b2 = sb("b2_all", [EXPERTS, D])
    with ExitStack() as c:
        tb = lambda n, s, d=F32: c.enter_context(nc.sbuf_tensor(n, s, d, allow_name_mangling=True))
        hot = tb("hot_r2", [P, 2, NT, EXPERTS])
        both = tb("both", [P, NT, EXPERTS])
        number = tb("number2", [P, NT])
        valid = tb("valid2", [P, NT])
        spare = tb("spare2", [P, NT])
        spot = tb("spot2", [P, 2, NT])
        tot = tb("tot2", [P, EXPERTS, NT])
        run = tb("run_r2", [P, EXPERTS, NT])
        rank = tb("rank_r2", [P, NT, EXPERTS])
        mine = tb("mine2", [P, 2, NT, EXPERTS])
        tiles_i = tb("tiles_i", [P, EXPERTS], I32)
        tiles = tb("tiles", [P, 3, EXPERTS])
        slot = tb("slot", [1, ST])
        past = tb("past2", [1, ST, EXPERTS])
        put = tb("put2", [P, 2, NT], I32)
        ps = c.enter_context(nc.psum_tensor("route2_ps", [P, 2, 512], F32, allow_name_mangling=True))
        sem = g.semaphores(c)
        s_number, s_chain, s_hot, s_ranks, s_put, s_sent, s_w = map(sem, ("s_number", "s_chain", "s_hot", "s_ranks", "s_put", "s_sent", "s_w"))
        shape = [P, NT, EXPERTS]
        with nc.Block() as block:
            @block.sync
            def _(sp):
                sp.dma_start(m.w1[:].rearrange("p e k f -> p (e k) f"), W1.rearrange("e (k p) f -> p (e k) f", p=P)).then_inc(s_w, 16)
                sp.dma_start(m.b2[:], b2).then_inc(s_w, 16)
                sp.dma_start(m.w2[:].rearrange("p e k f -> p (e k) f"), W2.rearrange("e (k p) f -> p (e k) f", p=P)).then_inc(s_w, 16)
                sp.wait_ge(s_w, 48)

            @block.gpsimd
            def _(pool):
                pool.iota(number[:], [[P, NT]], base=0, channel_multiplier=1, allow_small_or_imprecise_dtypes=True).then_inc(s_number, 1)
                pool.iota(slot[:], [[1, ST]], base=0, channel_multiplier=0, allow_small_or_imprecise_dtypes=True).then_inc(s_number, 1)
                pool.wait_ge(s_put, 1)
                for t in range(NT):
                    for i in range(2):
                        pool.indirect_dma_start(out=rows_dram, out_offset=bass.IndirectOffsetOnAxis(ap=put[:, i, t:t + 1], axis=0),
                                                in_=xn[:, t, :], in_offset=None).then_inc(s_sent, 16)
                pool.wait_ge(s_sent, 16 * 2 * NT)

            @block.tensor
            def _(pe):
                pe.wait_ge(s_hot, 1)
                rows = both[:].rearrange("p t e -> p (t e)")
                pe.matmul(ps[:, 0, 0:NT * EXPERTS], g.before[:], rows, start=True, stop=True)
                pe.matmul(ps[:, 1, 0:NT * EXPERTS], g.ones[:], rows, start=True, stop=True).then_inc(s_ranks, 1)

            @block.vector
            def _(dve):
                ch = Chain(dve, s_chain)
                first_largest(dve, ch, g, probs[:], m.factor[:, 0], hot[:, 0], spare[:])
                ch.link(dve.tensor_tensor(m.cw[:], probs[:], hot[:, 0], ALU.mult))
                ch.link(dve.scalar_tensor_tensor(probs[:], hot[:, 0], -2.0, probs[:], ALU.mult, ALU.add))
                first_largest(dve, ch, g, probs[:], m.factor[:, 1], hot[:, 1], spare[:])
                ch.link(dve.tensor_tensor(both[:], probs[:], hot[:, 1], ALU.mult))
                ch.link(dve.tensor_tensor(m.cw[:], m.cw[:], both[:], ALU.add))
                dve.wait_ge(s_number, 2)
                ch.link(dve.tensor_scalar(valid[:], number[:], float(N), None, ALU.is_lt))
                for i in range(2):
                    ch.link(dve.tensor_tensor(hot[:, i], hot[:, i], valid[:].unsqueeze(2).to_broadcast(shape), ALU.mult))
                ch.link(dve.tensor_tensor(both[:], hot[:, 0], hot[:, 1], ALU.add))
                dve.sem_inc(s_hot, 1)
                dve.wait_ge(s_ranks, 1)
                ch.link(dve.tensor_copy(tot[:], ps[:, 1, 0:NT * EXPERTS].rearrange("p (t e) -> p e t", e=EXPERTS)))
                for e in range(EXPERTS):
                    last = dve.tensor_tensor_scan(run[:, e, :], g.ones[:, 0:NT], tot[:, e, :], 0.0, ALU.mult, ALU.add)
                ch.link(last)
                need, upto, first = (tiles[:, i, :] for i in range(3))
                ch.link(dve.tensor_scalar(tiles_i[:], run[:, :, NT - 1], float(P - 1), None, ALU.add))
                ch.link(dve.tensor_scalar(tiles_i[:], tiles_i[:], 7, None, ALU.logical_shift_right))
                ch.link(dve.tensor_copy(need, tiles_i[:]))
                ch.link(dve.tensor_tensor_scan(upto, g.ones[:, 0:EXPERTS], need, 0.0, ALU.mult, ALU.add))
                ch.link(dve.tensor_tensor(first, upto, need, ALU.subtract))
                ch.link(dve.tensor_scalar(first, first, float(P), None, ALU.mult))
                ch.link(dve.tensor_tensor(run[:], run[:], tot[:], ALU.subtract))
                ch.link(dve.tensor_tensor(run[:], run[:], first.unsqueeze(2).to_broadcast([P, EXPERTS, NT]), ALU.add))
                ch.link(dve.tensor_tensor(rank[:], ps[:, 0, 0:NT * EXPERTS].rearrange("p (t e) -> p t e", e=EXPERTS),
                                          run[:].rearrange("p e t -> p t e"), ALU.add))
                ch.link(dve.tensor_tensor(mine[:], hot[:], rank[:].unsqueeze(1).to_broadcast([P, 2] + shape[1:]), ALU.mult))
                ch.link(dve.tensor_reduce(spot[:], mine[:], AX.X, ALU.add))
                dve.tensor_copy(m.take[:], spot[:])
                ch.link(dve.tensor_scalar(number[:], number[:], float(ST * P), None, ALU.add))
                for i in range(2):
                    if i == 1:
                        ch.link(dve.tensor_scalar(number[:], number[:], float(P), None, ALU.add))
                    ch.link(dve.tensor_tensor(spot[:, i], spot[:, i], number[:], ALU.subtract))
                    ch.link(dve.tensor_tensor(spot[:, i], spot[:, i], valid[:], ALU.mult))
                    ch.link(dve.tensor_tensor(put[:, i], spot[:, i], number[:], ALU.add))
                dve.sem_inc(s_put, 1)
                ch.link(dve.tensor_tensor(past[:], slot[:].unsqueeze(2).to_broadcast([1, ST, EXPERTS]),
                                          tiles[0:1, 1, :].unsqueeze(1).to_broadcast([1, ST, EXPERTS]), ALU.is_ge))
                ch.link(dve.tensor_reduce(slot[:], past[:], AX.X, ALU.add))
                ch.link(dve.tensor_scalar(m.expert_of[:], slot[:], float(EXPERTS - 1), None, ALU.min))
    return m


class Mixture:
    pass


def expert_tiles(nc, g, m, rows_dram, y_dram, b1):
    FC = F1 // P
    RING_X = 4
    with ExitStack() as c:
        tb = lambda n, s, d=F32: c.enter_context(nc.sbuf_tensor(n, s, d, allow_name_mangling=True))
        b1_all = bias_columns(nc, g, b1, FC, c)
        xin = [tb(f"xin{j}", [P, D]) for j in range(RING_X)]
        xt = [tb(f"xt{j}", [P, KC * P]) for j in range(2)]
        w1_now = [tb(f"w1_now{j}", [P, KC, F1]) for j in range(2)]
        b1_now = [tb(f"b1_now{j}", [P, FC]) for j in range(2)]
        hid = [tb(f"hid{j}", [P, FC, P]) for j in range(2)]
        y = [tb(f"y{j}", [P, D]) for j in range(2)]
        primed = tb("primed", [P, 1])
        bank = lambda n: c.enter_context(nc.psum_tensor(n, [P, 512], F32, allow_name_mangling=True))
        ps_t = [bank(f"ps_t{j}") for j in range(2)]
        ps_h = [bank(f"ps_h{j}") for j in range(2)]
        ps_y = [bank(f"ps_y{j}") for j in range(2)]
        sem = g.semaphores(c)
        s_turn, s_xt, s_now, s_up, s_hid, s_down, s_y = map(sem, ("s_turn", "s_xt", "s_now", "s_up", "s_hid", "s_down", "s_y"))
        s_xin = [sem(f"s_xin{j}") for j in range(RING_X)]
        s_st = [sem(f"s_st{j}") for j in range(2)]
        U = SLOTS
        PER = U // RING_X
        eng = mybir.EngineType
        def experts(which, i):
            _, values = nc.values_load_multi_w_load_instructions(
                m.expert_of[0:1, bass.ds(i * U, U)], engines=(which,), min_val=0, max_val=EXPERTS - 1,
                skip_runtime_bounds_check_because="the table's values are clamped where it is made")
            return values
        with nc.Block() as block:
            @block.sync
            def _(sp):
                with sp.Fori(0, ST // U) as i:
                    for u in range(U):
                        sp.wait_ge(s_turn, U * i + (u + 1))
                        sp.dma_start(xin[u % RING_X][:], rows_dram[bass.ds((U * i + u) * P, P)]).then_inc(s_xin[u % RING_X], 16)

            @block.tensor
            def _(pe):
                pe.sem_inc(s_turn, RING_X)
                pe.sem_inc(s_up, 2)
                pe.sem_inc(s_down, 2)

                def turn(i, u):
                    j = u % 2
                    pe.wait_ge(s_xin[u % RING_X], 16 * PER * i + 16 * (u // RING_X + 1))
                    pe.wait_ge(s_xt, U * i + (u + 1))
                    for k in range(KC):
                        mm = pe.transpose(ps_t[j][:, k * P:(k + 1) * P], xin[u % RING_X][:, k * P:(k + 1) * P], g.ident[:])
                    mm.then_inc(s_turn, 1)

                def up(i, u):
                    j = u % 2
                    pe.wait_ge(s_xt, U * i + (u + 3))
                    pe.wait_ge(s_now, 2 * U * i + 2 * (u + 1))
                    pe.wait_ge(s_hid, FC * U * i + FC * (u + 1))
                    for f in range(FC):
                        for k in range(KC):
                            mm = pe.matmul(ps_h[j][:, f * P:(f + 1) * P], w1_now[j][:, k, f * P:(f + 1) * P],
                                           xt[j][:, k * P:(k + 1) * P], start=(k == 0), stop=(k == KC - 1))
                    mm.then_inc(s_up, 1)

                def down(i, u, e):
                    j = u % 2
                    pe.wait_ge(s_hid, FC * U * i + FC * (u + 3))
                    pe.wait_ge(s_y, U * i + (u + 1))
                    for f in range(FC):
                        mm = pe.matmul(ps_y[j][:, 0:D], hid[j][:, f, :], m.w2[:, bass.ds(e, 1), f, :].rearrange("p o d -> p (o d)"),
                                       start=(f == 0), stop=(f == FC - 1))
                    mm.then_inc(s_down, 1)

                with pe.Fori(0, ST // U) as i:
                    es = experts(eng.PE, i)
                    turn(i, 0)
                    for u in range(U + 1):
                        if u + 1 < U:
                            turn(i, u + 1)
                        if u < U:
                            up(i, u)
                        if u >= 1:
                            down(i, u - 1, es[u - 1])

            @block.scalar
            def _(act):
                act.sem_inc(s_hid, 2 * FC)
                act.activation(primed[:], b1_all[:, 0, 0:1], ACT.Gelu)
                with act.Fori(0, ST // U) as i:
                    for u in range(U + 1):
                        if u < U:
                            act.wait_ge(s_up, U * i + (u + 3))
                            act.wait_ge(s_down, U * i + (u + 1))
                            for f in range(FC):
                                act.activation(hid[u % 2][:, f, :], ps_h[u % 2][:, f * P:(f + 1) * P], ACT.Gelu,
                                               bias=b1_now[u % 2][:, f:f + 1]).then_inc(s_hid, 1)
                        if u >= 1:
                            act.wait_ge(s_y, U * i + (u + 2))
                            act.dma_start(y_dram[bass.ds((U * i + (u - 1)) * P, P)], y[(u - 1) % 2][:]).then_inc(s_st[(u - 1) % 2], 16)
                for j in range(2):
                    act.wait_ge(s_st[j], 16 * (ST // 2 + 1))

            @block.vector
            def _(dve):
                dve.sem_inc(s_xt, 2)
                dve.sem_inc(s_y, 2)
                for j in range(2):
                    dve.sem_inc(s_st[j], 16)

                def inputs(i, u, e):
                    j = u % 2
                    dve.wait_ge(s_up, U * i + (u + 1))
                    dve.tensor_copy(w1_now[j][:], m.w1[:, bass.ds(e, 1)].rearrange("p o k f -> p (o k) f")).then_inc(s_now, 1)
                    dve.wait_ge(s_hid, FC * U * i + FC * (u + 1))
                    dve.tensor_copy(b1_now[j][:], b1_all[:, bass.ds(e, 1), :].rearrange("p o f -> p (o f)")).then_inc(s_now, 1)
                    dve.wait_ge(s_turn, U * i + (u + 1 + RING_X))
                    dve.tensor_copy(xt[j][:], ps_t[j][:, 0:D]).then_inc(s_xt, 1)

                with dve.Fori(0, ST // U) as i:
                    es = experts(eng.DVE, i)
                    inputs(i, 0, es[0])
                    for u in range(U + 1):
                        if u + 1 < U:
                            inputs(i, u + 1, es[u + 1])
                        if u >= 1:
                            dve.wait_ge(s_down, U * i + (u + 2))
                            dve.wait_ge(s_st[(u - 1) % 2], 8 * U * i + 16 * ((u - 1) // 2 + 1))
                            dve.tensor_copy(y[(u - 1) % 2][:], ps_y[(u - 1) % 2][:, 0:D]).then_inc(s_y, 1)


def combine_top2(nc, g, x, m, y_dram):
    RING = 8
    with ExitStack() as c:
        tb = lambda n, s, d=F32: c.enter_context(nc.sbuf_tensor(n, s, d, allow_name_mangling=True))
        rows = [tb(f"rows_m{u}", [P, D]) for u in range(RING)]
        cw_turned = tb("cw_turned", [EXPERTS, NT, P])
        ps = [c.enter_context(nc.psum_tensor(f"ps_b{j}", [P, 512], F32, allow_name_mangling=True)) for j in range(4)]
        sem = g.semaphores(c)
        s_turn, s_turned, s_bias, s_bias_in, s_used = map(sem, ("s_turn", "s_turned", "s_bias", "s_bias_in", "s_used"))
        s_rows = [sem(f"s_rows{u}") for u in range(RING)]
        TG = -(-NT // 4)
        order = [(i, tile) for t in range(NT + 1) for i, tile in ((0, t), (1, t - 1)) if 0 <= tile < NT]
        with nc.Block() as block:
            @block.gpsimd
            def _(pool):
                for n, (i, tile) in enumerate(order):
                    if n >= RING:
                        pool.wait_ge(s_used, n - RING + 1)
                    pool.indirect_dma_start(out=rows[n % RING][:], out_offset=None, in_=y_dram,
                                            in_offset=bass.IndirectOffsetOnAxis(ap=m.take[:, i, tile:tile + 1], axis=0)
                                            ).then_inc(s_rows[n % RING], 16)

            @block.tensor
            def _(pe):
                for q in range(TG):
                    if q >= 4:
                        pe.wait_ge(s_turned, q - 3)
                    for t in range(4 * q, min(NT, 4 * q + 4)):
                        mm = pe.transpose(ps[q % 4][0:EXPERTS, (t % 4) * P:(t % 4 + 1) * P], m.cw[:, t, :], g.ident[:])
                    mm.then_inc(s_turn, 1)
                pe.wait_ge(s_turned, TG)
                for t in range(NT):
                    if t >= 4:
                        pe.wait_ge(s_bias_in, t - 3)
                    pe.matmul(ps[t % 4][:, 0:D], cw_turned[:, t, :], m.b2[:], start=True, stop=True).then_inc(s_bias, 1)

            @block.scalar
            def _(act):
                for q in range(TG):
                    n = min(NT, 4 * q + 4) - 4 * q
                    act.wait_ge(s_turn, q + 1)
                    act.activation(cw_turned[:, 4 * q:4 * q + n, :].rearrange("e t n -> e (t n)"), ps[q % 4][0:EXPERTS, 0:n * P], ACT.Copy).then_inc(s_turned, 1)

            @block.vector
            def _(dve):
                for t in range(NT):
                    dve.wait_ge(s_bias, t + 1)
                    dve.tensor_tensor(x[:, t, :], ps[t % 4][:, 0:D], x[:, t, :], ALU.add).then_inc(s_bias_in, 1)
                dve.wait_ge(s_bias_in, NT)
                for n, (i, tile) in enumerate(order):
                    dve.wait_ge(s_rows[n % RING], 16 * (n // RING + 1))
                    if i == 1:
                        dve.wait_ge(s_used, order.index((0, tile)) + 1)
                    dve.scalar_tensor_tensor(x[:, tile, :], rows[n % RING][:], m.factor[:, i, tile:tile + 1], x[:, tile, :],
                                             ALU.mult, ALU.add).then_inc(s_used, 1)


def add_sums(nc, g, x, acc, bias):
    with ExitStack() as c:
        b_row = c.enter_context(nc.sbuf_tensor("b_row2", [P, D], F32, allow_name_mangling=True))
        s_b, s_sum = map(g.semaphores(c), ("s_b", "s_sum"))
        with nc.Block() as block:
            @block.sync
            def _(sp):
                sp.dma_start(b_row[:], bias.rearrange("(o d) -> o d", o=1).to_broadcast([P, D])).then_inc(s_b, 16)

            @block.gpsimd
            def _(pool):
                pool.wait_ge(s_b, 16)
                pool.tensor_tensor(acc[:, 0:NT, :], acc[:, 0:NT, :], b_row[:].unsqueeze(1).to_broadcast([P, NT, D]), ALU.add).then_inc(s_sum, 1)

            @block.vector
            def _(dve):
                dve.wait_ge(s_sum, 1)
                dve.tensor_tensor(x[:], x[:], acc[:, 0:NT, :], ALU.add)


def route(nc, g, probs, xn, rows_dram, ctx):
    sb = lambda n, s, d=F32: ctx.enter_context(nc.sbuf_tensor(n, s, d, allow_name_mangling=True))
    take = sb("take", [P, NT], I32)
    factor = sb("factor", [P, NT])
    with ExitStack() as c:
        tb = lambda n, s, d=F32: c.enter_context(nc.sbuf_tensor(n, s, d, allow_name_mangling=True))
        hot = tb("hot_r", [P, NT, EXPERTS])
        w = tb("w_route", [P, 8, NT])
        tot = tb("tot", [P, EXPERTS, NT])
        run = tb("run_r", [P, EXPERTS, NT])
        rank = tb("rank_r", [P, NT, EXPERTS])
        put = tb("put", [P, NT], I32)
        ps = c.enter_context(nc.psum_tensor("route_ps", [P, 2, 512], F32, allow_name_mangling=True))
        sem = g.semaphores(c)
        s_number, s_chain, s_hot, s_ranks, s_put, s_sent = map(sem, ("s_number", "s_chain", "s_hot", "s_ranks", "s_put", "s_sent"))
        best, spare, number, valid, place, expert, kept, spot = (w[:, i] for i in range(8))
        shape = [P, NT, EXPERTS]
        with nc.Block() as block:
            @block.gpsimd
            def _(pool):
                pool.iota(number, [[P, NT]], base=0, channel_multiplier=1, allow_small_or_imprecise_dtypes=True).then_inc(s_number, 1)
                pool.wait_ge(s_put, 1)
                for t in range(NT):
                    pool.indirect_dma_start(out=rows_dram, out_offset=bass.IndirectOffsetOnAxis(ap=put[:, t:t + 1], axis=0),
                                            in_=xn[:, t, :], in_offset=None).then_inc(s_sent, 16)
                pool.wait_ge(s_sent, 16 * NT)

            @block.tensor
            def _(pe):
                pe.wait_ge(s_hot, 1)
                rows = hot[:].rearrange("p t e -> p (t e)")
                pe.matmul(ps[:, 0, 0:NT * EXPERTS], g.before[:], rows, start=True, stop=True)
                pe.matmul(ps[:, 1, 0:NT * EXPERTS], g.ones[:], rows, start=True, stop=True).then_inc(s_ranks, 1)

            @block.vector
            def _(dve):
                ch = Chain(dve, s_chain)
                first_largest(dve, ch, g, probs[:], best, hot[:], spare)
                dve.wait_ge(s_number, 1)
                ch.link(dve.tensor_scalar(valid, number, float(N), None, ALU.is_lt))
                ch.link(dve.tensor_tensor(hot[:], hot[:], valid.unsqueeze(2).to_broadcast(shape), ALU.mult))
                dve.sem_inc(s_hot, 1)
                dve.wait_ge(s_ranks, 1)
                ch.link(dve.tensor_copy(tot[:], ps[:, 1, 0:NT * EXPERTS].rearrange("p (t e) -> p e t", e=EXPERTS)))
                for e in range(EXPERTS):
                    last = dve.tensor_tensor_scan(run[:, e, :], g.ones[:, 0:NT], tot[:, e, :], 0.0, ALU.mult, ALU.add)
                ch.link(last)
                ch.link(dve.tensor_tensor(run[:], run[:], tot[:], ALU.subtract))
                ch.link(dve.tensor_tensor(rank[:], ps[:, 0, 0:NT * EXPERTS].rearrange("p (t e) -> p t e", e=EXPERTS),
                                          run[:].rearrange("p e t -> p t e"), ALU.add))
                ch.link(dve.tensor_tensor(rank[:], rank[:], hot[:], ALU.mult))
                ch.link(dve.tensor_reduce(place, rank[:], AX.X, ALU.add))
                ch.link(dve.tensor_tensor(rank[:], hot[:], g.iota25[:, 0:EXPERTS].unsqueeze(1).to_broadcast(shape), ALU.mult))
                ch.link(dve.tensor_reduce(expert, rank[:], AX.X, ALU.add))
                ch.link(dve.tensor_scalar(kept, place, float(CAP), None, ALU.is_lt))
                ch.link(dve.tensor_tensor(kept, kept, valid, ALU.mult))
                ch.link(dve.tensor_tensor(factor[:], best, kept, ALU.mult))
                ch.link(dve.tensor_scalar(expert, expert, float(CAPP), None, ALU.mult))
                ch.link(dve.tensor_scalar(spare, place, float(CAP - 1), None, ALU.min))
                ch.link(dve.tensor_tensor(take[:], spare, expert, ALU.add))
                ch.link(dve.tensor_tensor(spot, place, expert, ALU.add))
                ch.link(dve.tensor_scalar(number, number, float(EXPERTS * CAPP), None, ALU.add))
                ch.link(dve.tensor_tensor(spot, spot, number, ALU.subtract))
                ch.link(dve.tensor_tensor(spot, spot, kept, ALU.mult))
                ch.link(dve.tensor_tensor(put[:], spot, number, ALU.add))
                dve.sem_inc(s_put, 1)
    return take, factor


def expert_layers(nc, g, rows_dram, y_dram, w1, b1, w2, b2):
    FC = F2 // P
    RT = CAPP // P
    with ExitStack() as c:
        tb = lambda n, s, d=F32: c.enter_context(nc.sbuf_tensor(n, s, d, allow_name_mangling=True))
        up_w = [tb(f"up_w{j}", [P, KC, F2]) for j in range(2)]
        down_w = [tb(f"down_w{j}", [P, FC, D]) for j in range(2)]
        b1_all = bias_columns(nc, g, b1, FC, c)
        b2_row = [tb(f"b2_row{j}", [1, D]) for j in range(2)]
        xin = [tb(f"xin{j}", [P, RT, D]) for j in range(2)]
        xt = [tb(f"xt{j}", [P, KC, CAPP]) for j in range(2)]
        hid = [tb(f"hidden{j}", [P, FC, CAPP]) for j in range(2)]
        y = [tb(f"y{j}", [P, RT, D]) for j in range(2)]
        bank = lambda n: c.enter_context(nc.psum_tensor(n, [P, 512], F32, allow_name_mangling=True))
        ps_t = [bank(f"ps_t{k}") for k in range(KC)]
        ps_h = [bank(f"ps_u{k}") for k in range(3)]
        ps_y = [bank(f"ps_v{k}") for k in range(3)]
        sem = g.semaphores(c)
        s_act, s_turn, s_turned, s_h, s_hid, s_y, s_out_y = map(sem, ("s_act", "s_turn", "s_turned", "s_h", "s_hid", "s_y", "s_out_y"))
        s_w = [sem("s_w0"), sem("s_w1")]
        s_st = [sem("s_st0"), sem("s_st1")]
        PAIRS = EXPERTS // 2
        with nc.Block() as block:
            @block.sync
            def _(sp):
                with sp.Fori(0, PAIRS) as i:
                    for j in range(2):
                        e = 2 * i + j
                        sp.wait_ge(s_y, 2 * RT * i)
                        sp.dma_start(xin[j][:], rows_dram[bass.ds(e * CAPP, CAPP)].rearrange("(t p) d -> p t d", p=P)).then_inc(s_w[j], 16)
                        sp.dma_start(up_w[j][:], w1[bass.ds(e, 1)].rearrange("o (k p) f -> p (o k) f", p=P)).then_inc(s_w[j], 16)
                        sp.dma_start(down_w[j][:], w2[bass.ds(e, 1)].rearrange("o (k p) f -> p (o k) f", p=P)).then_inc(s_w[j], 16)
                        sp.dma_start(b2_row[j][:], b2[bass.ds(e, 1)]).then_inc(s_w[j], 16)

            @block.tensor
            def _(pe):
                with pe.Fori(0, PAIRS) as i:
                    for j in range(2):
                        pe.wait_ge(s_w[j], 64 * i + 64)
                        pe.wait_ge(s_turned, 2 * KC * i + KC * j)
                        for k in range(KC):
                            for t in range(RT):
                                mm = pe.transpose(ps_t[k][:, t * P:(t + 1) * P], xin[j][:, t, k * P:(k + 1) * P], g.ident[:])
                            mm.then_inc(s_turn, 1)
                        pe.wait_ge(s_turned, 2 * KC * i + KC * (j + 1))
                        for f in range(FC):
                            n = j * FC + f
                            pe.wait_ge(s_hid, 2 * FC * i + max(0, n - 2))
                            for k in range(KC):
                                mm = pe.matmul(ps_h[f % 3][:], up_w[j][:, k, f * P:(f + 1) * P], xt[j][:, k, :], start=(k == 0), stop=(k == KC - 1))
                            mm.then_inc(s_h, 1)
                        for t in range(RT):
                            m = j * RT + t
                            pe.wait_ge(s_out_y, 2 * RT * i + max(0, m - 2))
                            pe.matmul(ps_y[m % 3][:, 0:D], g.ones[0:1, :], b2_row[j][:], start=True, stop=False)
                            for f in range(FC):
                                if t == 0:
                                    pe.wait_ge(s_hid, 2 * FC * i + (j * FC + f + 1))
                                mm = pe.matmul(ps_y[m % 3][:, 0:D], hid[j][:, f, t * P:(t + 1) * P], down_w[j][:, f, :], start=False, stop=(f == FC - 1))
                            mm.then_inc(s_y, 1)

            @block.scalar
            def _(act):
                with act.Fori(0, PAIRS) as i:
                    for j in range(2):
                        act.wait_ge(s_y, 2 * RT * i)
                        for f in range(FC):
                            act.wait_ge(s_h, 2 * FC * i + (j * FC + f + 1))
                            act.sem_inc(s_act, 1)
                            act.activation(hid[j][:, f, :], ps_h[f % 3][:], ACT.Relu,
                                           bias=b1_all[:, bass.ds(2 * i + j, 1), f:f + 1].rearrange("p o f -> p (o f)")).then_inc(s_hid, 1)
                        act.wait_ge(s_out_y, 2 * RT * i + RT * (j + 1))
                        act.dma_start(y_dram[bass.ds((2 * i + j) * CAPP, CAPP)].rearrange("(t p) d -> p t d", p=P), y[j][:]).then_inc(s_st[j], 16)
                for j in range(2):
                    act.wait_ge(s_st[j], 16 * PAIRS)

            @block.vector
            def _(dve):
                with dve.Fori(0, PAIRS) as i:
                    for j in range(2):
                        dve.wait_ge(s_y, 2 * RT * i)
                        for k in range(KC):
                            dve.wait_ge(s_turn, 2 * KC * i + (KC * j + k + 1))
                            dve.tensor_copy(xt[j][:, k, :], ps_t[k][:]).then_inc(s_turned, 1)
                        dve.wait_ge(s_st[j], 16 * i)
                        for t in range(RT):
                            m = j * RT + t
                            dve.wait_ge(s_y, 2 * RT * i + (m + 1))
                            dve.tensor_copy(y[j][:, t, :], ps_y[m % 3][:, 0:D]).then_inc(s_out_y, 1)


def combine(nc, g, x, y_dram, take, factor, out):
    RING = 8
    TOP = 3.4028234e38
    with ExitStack() as c:
        tb = lambda n, s, d=F32: c.enter_context(nc.sbuf_tensor(n, s, d, allow_name_mangling=True))
        rows = [tb(f"rows_c{u}", [P, D]) for u in range(RING)]
        odd = [tb(f"odd{u}", [P, 3, D], U8) for u in range(2)]
        fill = tb("fill", [P, 3, D])
        sem = g.semaphores(c)
        s_fill, s_chain, s_x, s_out = map(sem, ("s_fill", "s_chain", "s_x", "s_out"))
        s_rows = [sem(f"s_rows{u}") for u in range(RING)]
        with nc.Block() as block:
            @block.gpsimd
            def _(pool):
                for t in range(NT):
                    if t >= RING:
                        pool.wait_ge(s_x, t - RING + 1)
                    pool.indirect_dma_start(out=rows[t % RING][:], out_offset=None, in_=y_dram,
                                            in_offset=bass.IndirectOffsetOnAxis(ap=take[:, t:t + 1], axis=0)).then_inc(s_rows[t % RING], 16)

            @block.vector
            def _(dve):
                ch = Chain(dve, s_chain)
                for i, v in enumerate((0.0, 1e4, -1e4)):
                    dve.memset(fill[:, i, :], v).then_inc(s_fill, 1)
                dve.wait_ge(s_fill, 3)
                for t in range(NT):
                    r, m = rows[t % RING], odd[t % 2]
                    dve.wait_ge(s_rows[t % RING], 16 * (t // RING + 1))
                    ch.link(dve.tensor_scalar(r[:], r[:], factor[:, t:t + 1], None, ALU.mult))
                    dve.tensor_tensor(m[:, 0], r[:], r[:], ALU.not_equal)
                    dve.tensor_scalar(m[:, 1], r[:], TOP, None, ALU.is_gt)
                    ch.link(dve.tensor_scalar(m[:, 2], r[:], -TOP, None, ALU.is_lt))
                    for i in range(3):
                        ch.link(dve.copy_predicated(r[:], m[:, i], fill[:, i, :]))
                    dve.tensor_tensor(x[:, t, :], x[:, t, :], r[:], ALU.add).then_inc(s_x, 1)

            @block.sync
            def _(sp):
                for t in range(NT):
                    n = min(P, N - t * P)
                    sp.wait_ge(s_x, t + 1)
                    sp.dma_start(out[t * P:t * P + n], x[0:n, t, :]).then_inc(s_out, 16)
                sp.wait_ge(s_out, 16 * NT)


def load_nodes(nc, g, x, x_dram):
    with ExitStack() as c:
        s_pad, s_x = map(g.semaphores(c), ("s_pad", "s_x"))
        with nc.Block() as block:
            @block.vector
            def _(dve):
                dve.memset(x[:, NT - 1, :], 0.0).then_inc(s_pad, 1)

            @block.sync
            def _(sp):
                full = (NT - 1) * P
                sp.dma_start(x[:, 0:NT - 1, :], x_dram[0:full].rearrange("(t p) d -> p t d", p=P)).then_inc(s_x, 16)
                sp.wait_ge(s_pad, 1)
                sp.dma_start(x[0:N - full, NT - 1, :], x_dram[full:N]).then_inc(s_x, 16)
                sp.wait_ge(s_x, 32)


def attention_layer(nc, g, name, turned_from, x_in, weights, heads, dst, hots, visits, x_out, send_list, ctx):
    W, a_src, a_dst, bias = weights
    C = heads
    with ExitStack() as left:
        turned = left.enter_context(nc.sbuf_tensor(name + "_turned", [P, KC, NP], F32))
        if turned_from == "norm":
            with nc.sbuf_tensor(name + "_xn", [P, NT, D], F32) as xn:
                normalise(nc, g, x_in, xn, turned)
        else:
            normalise(nc, g, x_in, None, turned)
        if turned_from != "norm":
            ctx.close()
        h, al, table = project(nc, g, name, turned, W, (a_src, a_dst), C, ctx)
    with ExitStack() as left:
        ae = expand(nc, g, name, al, hots, C, send_list, left)
        ext = edge_softmax(nc, g, name, ae, dst, C, ctx)
    acc = ctx.enter_context(nc.sbuf_tensor(name + "_acc", [P, NT + 1, D + 2 * C + 1], F32, side="right"))
    aggregate(nc, g, name, table, g.src_idx, visits, ext, C, 2 * C + 1, acc)
    finish_attention(nc, g, acc, h, al, bias, C, x_out)
    return acc


def build(nc, x, src, dst, edge_weight, L0_gnn_W1, L0_gnn_a_src1, L0_gnn_a_dst1, L0_gnn_b1, L0_gnn_W2, L0_gnn_a_src2,
          L0_gnn_a_dst2, L0_gnn_b2, L0_ffn_gate_w, L0_ffn_gate_b, L0_ffn_W1, L0_ffn_b1, L0_ffn_W2, L0_ffn_b2, L1_gnn_W,
          L1_gnn_b, L1_ffn_gate_w, L1_ffn_gate_b, L1_ffn_w1, L1_ffn_b1, L1_ffn_w2, L1_ffn_b2, out, stop=99, probe=None):
    g = Graph(nc)
    rows_dram = nc.dram_tensor("rows_dram", (ST * P + NP + P, D), F32, kind="Internal").ap()
    y_dram = nc.dram_tensor("y_dram", (ST * P, D), F32, kind="Internal").ap()
    with ExitStack() as keep:
        constants(nc, g, keep)
        xs = keep.enter_context(nc.sbuf_tensor("x_nodes", [P, NT, D], F32))
        load_nodes(nc, g, xs, x)
        graph_tables(nc, g, src, dst, edge_weight, keep)
        to_dst, minus_dst, _ = visit_tables(nc, "by_dst", g, g.dst_key, keep)
        to_src, minus_src, ends = visit_tables(nc, "by_src", g, g.src_key, keep)
        with ExitStack() as graph:
            hot_src = high_parts(nc, "hot_src", g, g.src_key, graph)
            by_source(nc, g, hot_src, ends, rows_dram, graph)
            hot_dst = high_parts(nc, "hot_dst", g, g.dst_key, graph)
            right = ExitStack()
            acc = attention_layer(nc, g, "gat1", "norm", xs, (L0_gnn_W1, L0_gnn_a_src1, L0_gnn_a_dst1, L0_gnn_b1), HEADS,
                                  dst, (hot_src, hot_dst), (to_dst, minus_dst), None, True, right)
            if stop == 1:
                probe(nc, acc[:, 0:NT, 0:D]); right.close(); return
            attention_layer(nc, g, "gat2", "sums", acc[:, 0:NT, 0:D], (L0_gnn_W2, L0_gnn_a_src2, L0_gnn_a_dst2, L0_gnn_b2), 1,
                            dst, (hot_src, hot_dst), (to_dst, minus_dst), xs, False, right)
            right.close()
            if stop == 2:
                probe(nc, xs[:]); return
        with ExitStack() as left:
            xn = left.enter_context(nc.sbuf_tensor("ffn0_xn", [P, NT, D], F32))
            with ExitStack() as inner:
                turned = inner.enter_context(nc.sbuf_tensor("ffn0_turned", [P, KC, NP], F32))
                normalise(nc, g, xs, xn, turned)
                probs = gate(nc, g, "ffn0", turned, L0_ffn_gate_w, L0_ffn_gate_b, inner)
                mix = route_top2(nc, g, probs, xn, rows_dram, L0_ffn_W1, L0_ffn_W2, L0_ffn_b2, inner)
                expert_tiles(nc, g, mix, rows_dram, y_dram, L0_ffn_b1)
                combine_top2(nc, g, xs, mix, y_dram)
        if stop == 3:
            probe(nc, xs[:]); return
        with ExitStack() as left:
            l_idx, l_values = read_list(nc, g, left)
            with ExitStack() as right:
                with ExitStack() as inner:
                    turned = inner.enter_context(nc.sbuf_tensor("gcn_turned", [P, KC, NP], F32))
                    with nc.sbuf_tensor("gcn_xn", [P, NT, D], F32) as xn:
                        normalise(nc, g, xs, xn, turned)
                    _, _, table = project(nc, g, "gcn", turned, L1_gnn_W, None, 1, right)
                acc = right.enter_context(nc.sbuf_tensor("gcn_acc", [P, NT + 1, D], F32, side="right"))
                aggregate(nc, g, "gcn", table, l_idx, (to_src, minus_src), l_values, 1, 0, acc)
                add_sums(nc, g, xs, acc, L1_gnn_b)
        if stop == 4:
            probe(nc, xs[:]); return
        with ExitStack() as left:
            xn = left.enter_context(nc.sbuf_tensor("ffn1_xn", [P, NT, D], F32))
            turned = left.enter_context(nc.sbuf_tensor("ffn1_turned", [P, KC, NP], F32))
            normalise(nc, g, xs, xn, turned)
            probs = gate(nc, g, "ffn1", turned, L1_ffn_gate_w, L1_ffn_gate_b, left)
            take, factor = route(nc, g, probs, xn, rows_dram, left)
            expert_layers(nc, g, rows_dram, y_dram, L1_ffn_w1, L1_ffn_b1, L1_ffn_w2, L1_ffn_b2)
            combine(nc, g, xs, y_dram, take, factor, out)


_INS = ["x", "src", "dst", "edge_weight", "L0_gnn_W1", "L0_gnn_a_src1", "L0_gnn_a_dst1", "L0_gnn_b1", "L0_gnn_W2", "L0_gnn_a_src2",
        "L0_gnn_a_dst2", "L0_gnn_b2", "L0_ffn_gate_w", "L0_ffn_gate_b", "L0_ffn_W1", "L0_ffn_b1", "L0_ffn_W2", "L0_ffn_b2", "L1_gnn_W",
        "L1_gnn_b", "L1_ffn_gate_w", "L1_ffn_gate_b", "L1_ffn_w1", "L1_ffn_b1", "L1_ffn_w2", "L1_ffn_b2"]
_OUTS = [((N, D), "float32")]


def kernel(**inputs):
    import numpy as _np
    import concourse.bacc as _bacc
    from concourse import mybir as _mybir
    from concourse.bass_utils import run_bass_kernel_spmd as _run

    nc = _bacc.Bacc("TRN2", target_bir_lowering=False, num_devices=1)
    arrays, args = {}, []
    for name in _INS:
        a = _np.ascontiguousarray(inputs[name])
        arrays[f"in_{name}_dram"] = a
        args.append(nc.dram_tensor(f"in_{name}_dram", a.shape, _mybir.dt.from_np(a.dtype), kind="ExternalInput").ap())
    for i, (shape, dtype) in enumerate(_OUTS):
        dt = _mybir.dt.from_np(_np.dtype(dtype))
        args.append(nc.dram_tensor(f"out_{i}_dram", shape, dt, kind="ExternalOutput").ap())
    build(nc, *args)
    r = _run(nc, [arrays], core_ids=[0])
    return r.results[0]["out_0_dram"]
```

```python
from contextlib import ExitStack

import numpy as np
import concourse.bass as bass
from concourse import mybir

F32 = mybir.dt.float32
BF16 = mybir.dt.bfloat16
I32 = mybir.dt.int32
U8 = mybir.dt.uint8
ALU = mybir.AluOpType
ACT = mybir.ActivationFunctionType
AX = mybir.AxisListType

P = 128
N, D = 3125, 256
NT = -(-N // P)
NP = NT * P
E = 53125
ET = 416
EP = ET * P
CH, CI = 16, 26
CL = CI * P
SLOTS = 8
VG, VQ = 110, 4
V = VG * VQ
GROUP = 8
LAG = 2
MID = NT // 2
FAR = 2.0 ** 90
assert (NT - 1 - MID) ** 2 <= 256
DUMMY = NT
HEADS, HF = 8, 32
NEG = 0.2
EXPERTS = 8
F1 = 512
F2 = 1024
CAP = int(np.ceil(1.25 * N / EXPERTS))
CAPP = 512
ST = (2 * N - EXPERTS) // P + EXPERTS
BIG = 1e30
PAD_KEY = NP
EPS = 1e-5
KC = D // P
RG = -(-ET // P)
assert ST % SLOTS == 0
assert ET >= -(-E // P) and V >= ET + NT - 1 and V % SLOTS == 0 and CH * CI == ET


class Chain:

    def __init__(self, engine, sem):
        self.engine, self.sem, self.count = engine, sem, 0

    def link(self, instruction):
        self.count += 1
        instruction.then_inc(self.sem, 1)
        self.engine.wait_ge(self.sem, self.count)


def load_rows(sp, dst, src, count, sem):
    full = count // P
    whole = full // P
    n = 0
    if whole:
        sp.dma_start(dst[:, 0:whole, :], src[0:whole * P * P].rearrange("(g k e) -> k g e", k=P, e=P)).then_inc(sem, 16)
        n += 1
    left = full - whole * P
    if left:
        sp.dma_start(dst[0:left, whole, :], src[whole * P * P:full * P].rearrange("(k e) -> k e", e=P)).then_inc(sem, 16)
        n += 1
    rest = count - full * P
    if rest:
        sp.dma_start(dst[left:left + 1, whole, 0:rest], src[full * P:count].rearrange("(k e) -> k e", k=1)).then_inc(sem, 16)
        n += 1
    return n


class Graph:

    def __init__(self, nc):
        self.nc, self.numbers, self.at = nc, list(nc.free_semaphores), 0
        self.sent = 0

    def semaphores(self, c):
        taken = []

        def sem(name):
            number = self.numbers[self.at % len(self.numbers)]
            taken.append(self.nc.alloc_semaphore(f"{name}_{self.at}", num=number))
            self.at += 1
            return taken[-1]

        c.callback(lambda: self.nc.clear_and_free_semaphores(taken))
        return sem


def constants(nc, g, ctx):
    sb = lambda n, s, d=F32: ctx.enter_context(nc.sbuf_tensor(n, s, d, allow_name_mangling=True))
    g.ident = sb("ident", [P, P])
    g.iota_row = sb("iota_row", [P, P])
    g.iota_col = sb("iota_col", [P, 1])
    g.iota25 = sb("iota25", [P, 32])
    g.falling = sb("falling", [P, EXPERTS])
    g.before = sb("before", [P, P])
    g.ones = sb("ones", [P, P])
    with ExitStack() as c:
        s_iota = g.semaphores(c)("s_iota")
        with nc.Block() as block:
            @block.gpsimd
            def _(pool):
                pool.iota(g.iota_row[:], [[1, P]], base=0, channel_multiplier=0, allow_small_or_imprecise_dtypes=True).then_inc(s_iota, 1)
                pool.iota(g.iota_col[:], [[0, 1]], base=0, channel_multiplier=1, allow_small_or_imprecise_dtypes=True).then_inc(s_iota, 1)
                pool.iota(g.iota25[:], [[1, 32]], base=0, channel_multiplier=0, allow_small_or_imprecise_dtypes=True).then_inc(s_iota, 1)

            @block.vector
            def _(dve):
                dve.memset(g.ones[:], 1.0)
                dve.wait_ge(s_iota, 3)
                dve.tensor_scalar(g.falling[:], g.iota25[:, 0:EXPERTS], -1.0, float(EXPERTS), ALU.mult, ALU.add)
                dve.tensor_scalar(g.ident[:], g.iota_row[:], g.iota_col[:, 0:1], None, ALU.is_equal)
                dve.tensor_scalar(g.before[:], g.iota_row[:], g.iota_col[:, 0:1], None, ALU.is_gt)


def graph_tables(nc, g, src, dst, w, x_dram, x, ctx):
    sb = lambda n, s, d=F32: ctx.enter_context(nc.sbuf_tensor(n, s, d, allow_name_mangling=True))
    g.src_key = sb("src_key", [P, ET])
    g.dst_key = sb("dst_key", [P, ET])
    g.weight = sb("weight", [P, ET])
    g.is_last = sb("is_last", [P, ET])
    g.src_idx = sb("src_idx", [P, ET], I32)
    g.parts_dram = nc.dram_tensor("parts_dram", (8, EP), BF16, kind="Internal").ap()
    with ExitStack() as c:
        rows = c.enter_context(nc.sbuf_tensor("rows", [P, 4, RG, P], I32, allow_name_mangling=True))
        rows_f = c.enter_context(nc.sbuf_tensor("rows_f", [P, 4, RG, P], F32, allow_name_mangling=True))
        parts = c.enter_context(nc.sbuf_tensor("parts", [P, 4, RG, P], I32, allow_name_mangling=True))
        parts_bf = c.enter_context(nc.sbuf_tensor("parts_bf", [P, 8, RG, P], BF16, allow_name_mangling=True))
        centred = c.enter_context(nc.sbuf_tensor("centred", [P, 2, RG, P], F32, allow_name_mangling=True))
        turned = c.enter_context(nc.psum_tensor("turned", [P, 4, 512], F32, allow_name_mangling=True))
        sem = g.semaphores(c)
        s_padded, s_rows, s_float, s_turned, s_low, s_out, s_chain, s_x, s_x_pad = map(
            sem, ("s_padded", "s_rows", "s_float", "s_turned", "s_low", "s_out", "s_chain", "s_x", "s_x_pad"))
        loads = [0]
        lists = ((src, E), (dst, E), (dst[1:E], E - 1), (w, E))
        with nc.Block() as block:
            @block.sync
            def _(sp):
                sp.wait_ge(s_padded, 4)
                for i, (a, count) in enumerate(lists):
                    into = rows[:, i] if i < 3 else rows_f[:, 3]
                    loads[0] += load_rows(sp, into, a, count, s_rows)
                full = (NT - 1) * P
                sp.dma_start(x[:, 0:NT - 1, :], x_dram[0:full].rearrange("(t p) d -> p t d", p=P)).then_inc(s_x, 16)
                sp.wait_ge(s_x_pad, 1)
                sp.dma_start(x[0:N - full, NT - 1, :], x_dram[full:N]).then_inc(s_x, 16)
                sp.wait_ge(s_low, 5)
                for q in range(8):
                    o = g.parts_dram[q]
                    sp.dma_start(o[0:3 * P * P].rearrange("(g k e) -> k g e", k=P, e=P), parts_bf[:, q, 0:3, :]).then_inc(s_out, 16)
                    sp.dma_start(o[3 * P * P:EP].rearrange("(k e) -> k e", e=P), parts_bf[0:ET - 3 * P, q, 3, :]).then_inc(s_out, 16)
                sp.wait_ge(s_out, 16 * 16)
                sp.wait_ge(s_x, 32)

            @block.vector
            def _(dve):
                dve.memset(rows[:, 0], PAD_KEY).then_inc(s_padded, 1)
                dve.memset(rows[:, 1], PAD_KEY).then_inc(s_padded, 1)
                dve.memset(rows[:, 2], PAD_KEY + 1).then_inc(s_padded, 1)
                dve.memset(rows_f[:, 3], 0.0).then_inc(s_padded, 1)
                dve.memset(x[:, NT - 1, :], 0.0).then_inc(s_x_pad, 1)
                dve.wait_ge(s_padded, 4)
                dve.wait_ge(s_rows, 16 * loads[0])
                dve.tensor_copy(rows_f[:, 0:3], rows[:, 0:3]).then_inc(s_float, 1)
                dve.tensor_scalar(parts[:, 0:2], rows[:, 0:2], P - 1, None, ALU.bitwise_and).then_inc(s_chain, 1)
                dve.tensor_scalar(parts[:, 2:4], rows[:, 0:2], 7, None, ALU.logical_shift_right).then_inc(s_chain, 1)
                dve.wait_ge(s_chain, 2)
                dve.tensor_copy(parts_bf[:, 0:2], parts[:, 0:2]).then_inc(s_low, 1)
                dve.tensor_scalar(centred[:], parts[:, 2:4], float(NT - 1), float(-MID), ALU.min, ALU.add).then_inc(s_chain, 1)
                dve.wait_ge(s_chain, 3)
                for s in range(2):
                    dve.tensor_tensor(parts_bf[:, 2 + 3 * s], centred[:, s], centred[:, s], ALU.mult).then_inc(s_low, 1)
                dve.tensor_copy(parts_bf[:, 3:7:3], centred[:]).then_inc(s_low, 1)
                dve.memset(parts_bf[:, 4:8:3], 1.0).then_inc(s_low, 1)
                dve.wait_ge(s_turned, 1)
                dve.tensor_copy(g.src_key[:], turned[:, 0, 0:ET])
                dve.tensor_copy(g.dst_key[:], turned[:, 1, 0:ET]).then_inc(s_chain, 1)
                dve.tensor_copy(g.weight[:], turned[:, 3, 0:ET])
                dve.tensor_scalar(g.src_idx[:], turned[:, 0, 0:ET], float(N - 1), None, ALU.min)
                dve.wait_ge(s_chain, 4)
                dve.tensor_tensor(g.is_last[:], turned[:, 2, 0:ET], g.dst_key[:], ALU.not_equal)

            @block.tensor
            def _(pe):
                pe.wait_ge(s_float, 1)
                for i in range(4):
                    for r in range(RG):
                        k = min(P, ET - r * P)
                        mm = pe.transpose(turned[:, i, r * P:r * P + k], rows_f[0:k, i, r, :], g.ident[0:k, 0:k])
                mm.then_inc(s_turned, 1)


def high_parts(nc, name, g, key, ctx):
    hot = ctx.enter_context(nc.sbuf_tensor(name, [P, ET, NT], U8))
    with ExitStack() as c:
        ki = c.enter_context(nc.sbuf_tensor("ki", [P, ET], I32, allow_name_mangling=True))
        hi = c.enter_context(nc.sbuf_tensor("hi", [P, ET], F32, allow_name_mangling=True))
        s = g.semaphores(c)("s_hi")
        with nc.Block() as block:
            @block.vector
            def _(dve):
                ch = Chain(dve, s)
                ch.link(dve.tensor_copy(ki[:], key[:]))
                ch.link(dve.tensor_scalar(ki[:], ki[:], 7, None, ALU.logical_shift_right))
                ch.link(dve.tensor_copy(hi[:], ki[:]))
                dve.tensor_tensor(hot[:], hi[:].unsqueeze(2).to_broadcast([P, ET, NT]),
                                  g.iota25[:, 0:NT].unsqueeze(1).to_broadcast([P, ET, NT]), ALU.is_equal)
    return hot


def visit_tables(nc, g, keys, ctx):
    L = len(keys)
    sb = lambda n, s, d=F32: ctx.enter_context(nc.sbuf_tensor(n, s, d, allow_name_mangling=True))
    table = sb("visit_table", [1, L, 2, V + SLOTS], I32)
    part = sb("visit_part", [P, L, NT])
    minus = sb("visit_minus", [P, L, V])
    ends = sb("visit_ends", [P, L, NT])
    with ExitStack() as c:
        tb = lambda n, s, d=F32: c.enter_context(nc.sbuf_tensor(n, s, d, allow_name_mangling=True))
        junk = tb("junk", [P, 2, ET], BF16)
        work = tb("work", [P, 7, L, NT])
        work_i = tb("work_i", [P, 2, L, NT], I32)
        past = tb("past", [VG, L, VQ, NT])
        prod = tb("prod", [VG, L, VQ, NT])
        vi = tb("vi", [VG, VQ])
        both = tb("both_v", [VG, 2, L, VQ])
        spread = tb("spread", [VG, 2, L, VQ, VG])
        everywhere = c.enter_context(nc.psum_tensor("everywhere", [P, 2, L, 512], F32, allow_name_mangling=True))
        total = c.enter_context(nc.psum_tensor("total", [P, L, NT], F32, allow_name_mangling=True))
        sem = g.semaphores(c)
        s_part, s_total, s_vi, s_chain, s_spread, s_every = map(sem, ("s_part", "s_total", "s_vi", "s_chain", "s_spread", "s_every"))
        with nc.Block() as block:
            @block.gpsimd
            def _(pool):
                pool.iota(vi[:], [[VG, VQ]], base=0, channel_multiplier=1, allow_small_or_imprecise_dtypes=True).then_inc(s_vi, 1)

            @block.tensor
            def _(pe):
                pe.wait_ge(s_part, L * NT)
                pe.matmul(total[:].rearrange("p l t -> p (l t)"), g.ones[:], part[:].rearrange("p l t -> p (l t)"),
                          start=True, stop=True).then_inc(s_total, 1)
                pe.wait_ge(s_spread, 1)
                for i in range(2):
                    for l in range(L):
                        mm = pe.matmul(everywhere[:, i, l, 0:V], g.ones[0:VG, :], spread[:, i, l].rearrange("p q v -> p (q v)"),
                                       start=True, stop=True)
                mm.then_inc(s_every, 1)

            @block.vector
            def _(dve):
                ch = Chain(dve, s_chain)
                for n in range(L * NT):
                    l, t = n // NT, n % NT
                    if n >= 2:
                        dve.wait_ge(s_part, n - 1)
                    dve.tensor_scalar(junk[:, n % 2, :], keys[l][:], float(P * (t + 1)), None, ALU.is_lt, ALU.add,
                                      accum_out=part[:, l, t:t + 1]).then_inc(s_part, 1)
                dve.wait_ge(s_total, 1)
                ch.link(dve.tensor_copy(ends[:], total[:]))
                ch.link(dve.memset(work[:], 0.0))
                start, first, last, nvis, vend, off, step = (work[:, i] for i in range(7))
                ch.link(dve.tensor_copy(start[:, :, 1:NT], ends[:, :, 0:NT - 1]))
                ch.link(dve.tensor_copy(work_i[:, 0], start))
                ch.link(dve.tensor_scalar(work_i[:, 1], ends[:], -1.0, 0.0, ALU.add, ALU.max))
                ch.link(dve.tensor_scalar(work_i[:], work_i[:], 7, None, ALU.logical_shift_right))
                ch.link(dve.tensor_copy(work[:, 1:3], work_i[:]))
                ch.link(dve.tensor_tensor(nvis, last, first, ALU.subtract))
                ch.link(dve.tensor_scalar(nvis, nvis, 1.0, None, ALU.add))
                ch.link(dve.tensor_tensor(off, ends[:], start, ALU.is_gt))
                ch.link(dve.tensor_tensor(nvis, nvis, off, ALU.mult))
                for l in range(L):
                    scan = dve.tensor_tensor_scan(vend[:, l], g.ones[:, 0:NT], nvis[:, l], 0.0, ALU.mult, ALU.add)
                ch.link(scan)
                ch.link(dve.tensor_tensor(off, first, vend, ALU.subtract))
                ch.link(dve.tensor_tensor(off, off, nvis, ALU.add))
                ch.link(dve.tensor_tensor(step[:, :, 0:NT - 1], off[:, :, 1:NT], off[:, :, 0:NT - 1], ALU.subtract))
                dve.wait_ge(s_vi, 1)
                shape = [VG, L, VQ, NT]
                tv, kv = both[:, 0], both[:, 1]
                ch.link(dve.tensor_tensor(past[:], vi[:].unsqueeze(1).unsqueeze(3).to_broadcast(shape),
                                          vend[0:VG].unsqueeze(2).to_broadcast(shape), ALU.is_ge))
                ch.link(dve.tensor_reduce(tv, past[:], AX.X, ALU.add))
                ch.link(dve.tensor_tensor(prod[:], past[:], step[0:VG].unsqueeze(2).to_broadcast(shape), ALU.mult))
                ch.link(dve.tensor_reduce(kv, prod[:], AX.X, ALU.add))
                ch.link(dve.tensor_tensor(kv, kv, vi[:].unsqueeze(1).to_broadcast([VG, L, VQ]), ALU.add))
                for l in range(L):
                    moved = dve.tensor_scalar(kv[:, l], kv[:, l], off[0:VG, l, 0:1], 0.0, ALU.add, ALU.max)
                ch.link(moved)
                for i in range(2):
                    diagonal = dve.tensor_tensor(spread[:, i], both[:, i].unsqueeze(3).to_broadcast([VG, L, VQ, VG]),
                                                 g.ident[0:VG, 0:VG].unsqueeze(1).unsqueeze(1).to_broadcast([VG, L, VQ, VG]), ALU.mult)
                ch.link(diagonal)
                dve.sem_inc(s_spread, 1)
                ch.link(dve.memset(table[:], DUMMY))
                dve.wait_ge(s_every, 1)
                dve.tensor_scalar(table[:, :, 0, 0:V], everywhere[0:1, 1, :, 0:V], float(ET - 1), None, ALU.min)
                dve.tensor_copy(table[:, :, 1, LAG:LAG + V], everywhere[0:1, 0, :, 0:V])
                dve.tensor_scalar(minus[:], everywhere[:, 0, :, 0:V], -float(P), None, ALU.mult)
    return [(table[:, l], minus[:, l], ends[:, l], part[:, l]) for l in range(L)]


class LayerNorm:

    def __init__(self, nc, g, x, out, stats, ctx):
        tb = lambda n, s: ctx.enter_context(nc.sbuf_tensor(n, s, F32, allow_name_mangling=True))
        self.x, self.out, self.taken = x, out, stats is not None
        self.stats = stats if self.taken else tb("stats", [P, NT, 6])
        self.mv = tb("mv", [P, NT, 2])
        self.std = tb("std", [P, NT])
        self.rstd = tb("rstd", [P, NT])
        self.s_var, self.s_std, self.s_norm, self.s_stats, self.s_added = map(
            g.semaphores(ctx), ("s_var", "s_std", "s_norm", "s_stats", "s_added"))

    def variance(self, dve, add=None):
        n = 0
        if not self.taken:
            for t in range(NT + 1):
                if add is not None and t < NT:
                    dve.tensor_tensor(self.x[:, t, :], self.x[:, t, :], add[:, t, :], ALU.add).then_inc(self.s_added, 1)
                if t > 0:
                    if add is not None:
                        dve.wait_ge(self.s_added, t)
                    dve.bn_stats(self.stats[:, t - 1, :], self.x[:, t - 1, :]).then_inc(self.s_stats, 1)
            n = NT
            dve.wait_ge(self.s_stats, n)
        for t in range(NT):
            dve.bn_aggr(self.mv[:, t, :], self.stats[:, t, :]).then_inc(self.s_stats, 1)
        dve.wait_ge(self.s_stats, n + NT)
        dve.tensor_scalar(self.std[:], self.mv[:, :, 1], EPS, None, ALU.add).then_inc(self.s_var, 1)
        self.count = n + NT

    def root(self, act):
        act.wait_ge(self.s_var, 1)
        act.activation(self.std[:], self.std[:], ACT.Sqrt).then_inc(self.s_std, 1)

    def scale(self, dve):
        ch = Chain(dve, self.s_stats)
        ch.count = self.count
        std, rstd = self.std, self.rstd
        dve.wait_ge(self.s_std, 1)
        ch.link(dve.reciprocal(rstd[:], std[:]))
        ch.link(dve.tensor_tensor(std[:], rstd[:], rstd[:], ALU.mult))
        ch.link(dve.scalar_tensor_tensor(std[:], self.mv[:, :, 1], EPS, std[:], ALU.add, ALU.mult))
        ch.link(dve.tensor_scalar(std[:], std[:], -0.5, 1.5, ALU.mult, ALU.add))
        ch.link(dve.tensor_tensor(rstd[:], rstd[:], std[:], ALU.mult))
        for t in range(NT):
            dve.tensor_scalar(self.out[:, t, :], self.x[:, t, :], self.mv[:, t, 0:1], rstd[:, t:t + 1],
                              ALU.subtract, ALU.mult).then_inc(self.s_norm, 1)


def normalise_and_gate(nc, g, x, add, xn, probs, gate_w, gate_b, send_pairs):
    with ExitStack() as c:
        tb = lambda n, s, d=F32: c.enter_context(nc.sbuf_tensor(n, s, d, allow_name_mangling=True))
        ln = LayerNorm(nc, g, x, xn, None, c)
        turned = [tb(f"turned_g{j}", [P, KC * P]) for j in range(4)]
        w = tb("gate_w", [P, KC, EXPERTS])
        b = tb("gate_b", [P, EXPERTS])
        top = tb("gate_top", [P, 2, NT])
        turn = [c.enter_context(nc.psum_tensor(f"turn_g{i}", [P, 512], F32, allow_name_mangling=True)) for i in range(4)]
        ps = c.enter_context(nc.psum_tensor("gate_ps", [P, 512], F32, allow_name_mangling=True))[:, 0:NT * EXPERTS]
        ps = ps.rearrange("p (t e) -> p t e", e=EXPERTS)
        sem = g.semaphores(c)
        s_w, s_turn, s_copied, s_mm, s_logit, s_exp, s_chain = map(sem, ("s_w", "s_turn", "s_copied", "s_mm", "s_logit", "s_exp", "s_chain"))
        shape = [P, NT, EXPERTS]
        send = list_sender(nc, g, c, send_pairs)
        with nc.Block() as block:
            @block.gpsimd
            def _(pool):
                send(pool)

            @block.sync
            def _(sp):
                sp.dma_start(w[:], gate_w.rearrange("(k p) e -> p k e", p=P)).then_inc(s_w, 16)
                sp.dma_start(b[:], gate_b.rearrange("(o e) -> o e", o=1).to_broadcast([P, EXPERTS])).then_inc(s_w, 16)

            @block.tensor
            def _(pe):
                def product(t):
                    pe.wait_ge(s_copied, t + 1)
                    for k in range(KC):
                        mm = pe.matmul(ps[:, t, :], turned[t % 4][:, k * P:(k + 1) * P], w[:, k, :], start=(k == 0), stop=(k == KC - 1))
                    mm.then_inc(s_mm, 1)

                pe.wait_ge(s_w, 32)
                for t in range(NT + 2):
                    if t < NT:
                        pe.wait_ge(ln.s_norm, t + 1)
                        if t >= 4:
                            pe.wait_ge(s_copied, t - 3)
                        for k in range(KC):
                            mm = pe.transpose(turn[t % 4][:, k * P:(k + 1) * P], xn[:, t, k * P:(k + 1) * P], g.ident[:])
                        mm.then_inc(s_turn, 1)
                    if t >= 2:
                        product(t - 2)

            @block.scalar
            def _(act):
                ln.root(act)
                for t in range(NT):
                    act.wait_ge(s_turn, t + 1)
                    if t >= 4:
                        act.wait_ge(s_mm, t - 3)
                    act.activation(turned[t % 4][:], turn[t % 4][:, 0:D], ACT.Copy).then_inc(s_copied, 1)
                act.wait_ge(s_logit, 1)
                act.activation(probs[:], probs[:], ACT.Exp).then_inc(s_exp, 1)

            @block.vector
            def _(dve):
                ln.variance(dve, add)
                ln.scale(dve)
                ch = Chain(dve, s_chain)
                dve.wait_ge(s_w, 32)
                dve.wait_ge(s_mm, NT)
                ch.link(dve.tensor_tensor(probs[:], ps, b[:].unsqueeze(1).to_broadcast(shape), ALU.add))
                ch.link(dve.tensor_reduce(top[:, 0], probs[:], AX.X, ALU.max))
                ch.link(dve.tensor_tensor(probs[:], probs[:], top[:, 0].unsqueeze(2).to_broadcast(shape), ALU.subtract))
                dve.sem_inc(s_logit, 1)
                dve.wait_ge(s_exp, 1)
                ch.link(dve.tensor_reduce(top[:, 0], probs[:], AX.X, ALU.add))
                ch.link(dve.reciprocal(top[:, 1], top[:, 0]))
                ch.link(dve.tensor_tensor(probs[:], probs[:], top[:, 1].unsqueeze(2).to_broadcast(shape), ALU.mult))


def project(nc, g, name, x_in, norm, stats, W, attention, heads, seg, send_pairs, side, ctx):
    C = heads if attention else 0
    h = ctx.enter_context(nc.sbuf_tensor(name + "_h", [P, NT, D], F32, side=side))
    al = ctx.enter_context(nc.sbuf_tensor(name + "_al", [P, NT, 2, max(C, 1)], F32, side=side))
    table = nc.dram_tensor(name + "_table_dram", (NP, D), F32, kind="Internal").ap()
    al_dram = nc.dram_tensor(name + "_al_dram", (NP, C), F32, kind="Internal").ap() if C > 1 else None
    with ExitStack() as c:
        tb = lambda n, s, d=F32: c.enter_context(nc.sbuf_tensor(n, s, d, allow_name_mangling=True))
        xn = tb("xn", [P, NT, D]) if norm else x_in
        ln = LayerNorm(nc, g, x_in, xn, stats, c) if norm else None
        turned = [tb(f"turned{j}", [P, KC * P]) for j in range(4)]
        wcat = tb("wcat", [P, KC, D + 2 * C])
        wraw = tb("wraw", [P, KC, D])
        avec = tb("avec", [P, 2, D])
        prod = tb("prod_wa", [P, 2, KC, D])
        turn = [c.enter_context(nc.psum_tensor(f"turn{i}", [P, 512], F32, allow_name_mangling=True)) for i in range(4)]
        ps = [c.enter_context(nc.psum_tensor(f"proj{i}", [P, 512], F32, allow_name_mangling=True)) for i in range(4)]
        sem = g.semaphores(c)
        s_w, s_chain, s_wcat, s_turn, s_copied, s_mm, s_h, s_out = map(sem, ("s_w", "s_chain", "s_wcat", "s_turn", "s_copied", "s_mm", "s_h", "s_out"))
        if seg:
            seg.open(c)
        CHUNK = 5
        PER = 2 if C else 1
        send = list_sender(nc, g, c, send_pairs)
        with nc.Block() as block:
            @block.gpsimd
            def _(pool):
                send(pool)

            @block.sync
            def _(sp):
                flat_w = W.rearrange("(k p) h f -> p k (h f)", p=P) if len(W.shape) == 3 else W.rearrange("(k p) n -> p k n", p=P)
                sp.dma_start(wraw[:], flat_w).then_inc(s_w, 16)
                if seg:
                    seg.load(sp)
                for i, a in enumerate(attention or ()):
                    sp.dma_start(avec[:, i, :], a.rearrange("(o h) f -> o (h f)", o=1).to_broadcast([P, D])).then_inc(s_w, 16)
                for j in range(0, NT, CHUNK):
                    sp.wait_ge(s_h, PER * (j + CHUNK))
                    sp.dma_start(table[j * P:(j + CHUNK) * P].rearrange("(t p) d -> p t d", p=P), h[:, j:j + CHUNK, :]).then_inc(s_out, 16)
                if C > 1:
                    sp.dma_start(al_dram.rearrange("(t p) c -> p t c", p=P), al[:, :, 0, :]).then_inc(s_out, 16)
                sp.wait_ge(s_out, 16 * (NT // CHUNK + (C > 1)))

            @block.vector
            def _(dve):
                ch = Chain(dve, s_chain)
                if seg:
                    seg.pad(dve)
                if norm:
                    ln.variance(dve)
                dve.wait_ge(s_w, 48 if C else 16)
                dve.tensor_copy(wcat[:, :, 0:D], wraw[:]).then_inc(s_wcat, 1)
                for i in range(2 if C else 0):
                    ch.link(dve.tensor_tensor(prod[:, i], wraw[:], avec[:, i, :].unsqueeze(1).to_broadcast([P, KC, D]), ALU.mult))
                    for k in range(KC):
                        dve.tensor_reduce(wcat[:, k, D + i * C:D + (i + 1) * C],
                                          prod[:, i, k, :].rearrange("p (h f) -> p h f", h=C), AX.X, ALU.add).then_inc(s_wcat, 1)
                if norm:
                    ln.scale(dve)
                if seg:
                    seg.build(dve)

            @block.tensor
            def _(pe):
                def transpose(t):
                    if norm:
                        pe.wait_ge(ln.s_norm, t + 1)
                    if t >= 4:
                        pe.wait_ge(s_copied, t - 3)
                    for k in range(KC):
                        mm = pe.transpose(turn[t % 4][:, k * P:(k + 1) * P], xn[:, t, k * P:(k + 1) * P], g.ident[:])
                    mm.then_inc(s_turn, 1)

                def product(t):
                    pe.wait_ge(s_copied, t + 1)
                    if t >= 4:
                        pe.wait_ge(s_h, PER * (t - 3))
                    for k in range(KC):
                        mm = pe.matmul(ps[t % 4][:, 0:D + 2 * C], turned[t % 4][:, k * P:(k + 1) * P], wcat[:, k, :], start=(k == 0), stop=(k == KC - 1))
                    mm.then_inc(s_mm, 1)

                transpose(0)
                transpose(1)
                pe.wait_ge(s_wcat, 1 + 2 * KC if C else 1)
                for t in range(NT):
                    if t + 2 < NT:
                        transpose(t + 2)
                    product(t)

            @block.scalar
            def _(act):
                def copy(t):
                    act.wait_ge(s_turn, t + 1)
                    if t >= 4:
                        act.wait_ge(s_mm, t - 3)
                    act.activation(turned[t % 4][:], turn[t % 4][:, 0:D], ACT.Copy).then_inc(s_copied, 1)

                if norm:
                    ln.root(act)
                copy(0)
                copy(1)
                for t in range(NT):
                    if t + 2 < NT:
                        copy(t + 2)
                    act.wait_ge(s_mm, t + 1)
                    if C:
                        act.activation(al[:, t].rearrange("p s c -> p (s c)"), ps[t % 4][:, D:D + 2 * C], ACT.Copy).then_inc(s_h, 1)
                    act.activation(h[:, t, :], ps[t % 4][:, 0:D], ACT.Copy).then_inc(s_h, 1)
    return h, al, table, al_dram


def list_sender(nc, g, c, pairs):
    first, g.sent = g.sent, g.sent + pairs
    if not pairs:
        return lambda pool: None
    sem = g.semaphores(c)
    tb = lambda n, s, d=F32: c.enter_context(nc.sbuf_tensor(n, s, d, allow_name_mangling=True))
    spot_now = [tb(f"spot_now{j}", [P, GROUP], I32) for j in range(2)]
    load_now = [tb(f"load_now{j}", [P, GROUP, 4]) for j in range(2)]
    s_staged, s_send = map(sem, ("s_staged", "s_send"))
    s_sent = [sem("s_sent0"), sem("s_sent1")]

    def send(pool):
        for j in range(2):
            pool.memset(load_now[j][:], 0.0).then_inc(s_staged, 1)
        pool.wait_ge(s_staged, 2)

        def pair(i, peeled):
            for j in range(2):
                if not peeled:
                    pool.wait_ge(s_sent[j], 16 * GROUP * i)
                tiles = bass.ds((2 * first + j) * GROUP + 2 * GROUP * i, GROUP)
                pool.tensor_copy(spot_now[j][:], g.spot[:, tiles]).then_inc(s_staged, 1)
                for f, values in enumerate((g.dst_key, g.src_key, g.weight)):
                    pool.tensor_copy(load_now[j][:, :, f], values[:, tiles]).then_inc(s_staged, 1)
                pool.wait_ge(s_staged, 8 * i + (4 * j + 6))
                pool.sem_inc(s_send, 1)
                for u in range(GROUP):
                    pool.indirect_dma_start(out=g.list_dram, out_offset=bass.IndirectOffsetOnAxis(ap=spot_now[j][:, u:u + 1], axis=0),
                                            in_=load_now[j][:, u, :], in_offset=None).then_inc(s_sent[j], 16)

        pair(0, True)
        if pairs > 1:
            with pool.Fori(1, pairs) as i:
                pair(i, False)
        for j in range(2):
            pool.wait_ge(s_sent[j], 16 * GROUP * pairs)
    return send


class Segments:

    def __init__(self, nc, g, dst, heads, ctx):
        self.nc, self.g, self.dst, self.C, self.R = nc, g, dst, heads, CH * heads
        self.room = ctx.enter_context(nc.sbuf_tensor("dst_room", [P, CL], F32, allow_name_mangling=True))
        self.dst_f = self.room[0:self.R, :]
        self.brk = ctx.enter_context(nc.sbuf_tensor("brk", [self.R, CL + 1], F32, allow_name_mangling=True))

    def open(self, c):
        self.raw = c.enter_context(self.nc.sbuf_tensor("dst_raw", [self.R, CL], I32, allow_name_mangling=True))
        self.s_pad, self.s_raw, self.s_step = map(self.g.semaphores(c), ("s_pad", "s_raw", "s_step"))

    def load(self, sp):
        R, C, tail = self.R, self.C, E - (CH - 1) * CL
        sp.wait_ge(self.s_pad, 1)
        sp.dma_start(self.raw[0:R - C, :], self.dst[0:(CH - 1) * CL].rearrange("(c n) -> c n", n=CL).unsqueeze(1)
                     .to_broadcast([CH - 1, C, CL])).then_inc(self.s_raw, 16)
        sp.dma_start(self.raw[R - C:R, 0:tail], self.dst[(CH - 1) * CL:E].rearrange("(o n) -> o n", o=1).to_broadcast([C, tail])).then_inc(self.s_raw, 16)

    def pad(self, dve):
        dve.memset(self.raw[:], PAD_KEY).then_inc(self.s_pad, 1)

    def build(self, dve):
        ch = Chain(dve, self.s_step)
        dve.memset(self.brk[:], -BIG).then_inc(self.s_step, 1)
        dve.wait_ge(self.s_raw, 32)
        dve.tensor_copy(self.dst_f, self.raw[:]).then_inc(self.s_step, 1)
        ch.count = 2
        dve.wait_ge(self.s_step, 2)
        inner = self.brk[:, 1:CL]
        ch.link(dve.tensor_tensor(inner, self.dst_f[:, 1:CL], self.dst_f[:, 0:CL - 1], ALU.not_equal))
        dve.tensor_scalar(inner, inner, -BIG, None, ALU.mult).then_inc(self.s_step, 1)


def expand(nc, g, name, al, al_dram, heads, send_pairs, ctx):
    C = heads
    BT = 16
    TB = 2 if C > 1 else BT
    G = 8 if C > 1 else 0
    BY_PE = (BT - G, BT)
    NB0 = BY_PE[0] // TB
    NB = NB0 + BY_PE[1] // TB
    RING = 8 if C > 1 else 4
    ae = [ctx.enter_context(nc.sbuf_tensor(f"{name}_ae{s}", [P, ET, C], F32)) for s in range(2)]
    with ExitStack() as c:
        tb = lambda n, s, d=F32: c.enter_context(nc.sbuf_tensor(n, s, d, allow_name_mangling=True))
        rest = tb("rest", [P, 2, C, NT])
        part = [tb(f"part{j}", [P, 2, C, NT], BF16) for j in range(3)]
        lo_rows = [[tb(f"lo_rows{s}{j}", [P, BY_PE[s] * P], BF16) for j in range(2)] for s in range(2)]
        hot_lo = [[tb(f"hot_lo{s}{j}", [P, BY_PE[s] * P], BF16) for j in range(2)] for s in range(2)]
        tile_rows = [[tb(f"tile_rows{s}{j}", [3, BY_PE[s] * P], BF16) for j in range(2)] for s in range(2)]
        row_is = tb("row_is", [3, 3])
        quad = tb("quad", [3, 3, NT])
        quad_bf = tb("quad_bf", [3, C, NT], BF16)
        ps = [c.enter_context(nc.psum_tensor(f"picked{r}", [P, TB, C, NT], F32, allow_name_mangling=True)) for r in range(RING)]
        sem = g.semaphores(c)
        s_chain, s_parts, s_hot, s_bank, s_picked = map(sem, ("s_chain", "s_parts", "s_hot", "s_bank", "s_picked"))
        s_lo = [[sem(f"s_lo{s}{j}") for j in range(2)] for s in range(2)]
        BLOCKS = ET // BT
        side = lambda b: int(b >= NB0)
        send = list_sender(nc, g, c, send_pairs)
        if G:
            idx_now = [tb(f"idx_now{j}", [P, G], I32) for j in range(2)]
            got = [tb(f"got{j}", [P, G, C]) for j in range(2)]
            s_idx, s_go, s_act, s_placed = map(sem, ("s_idx", "s_go", "s_act", "s_placed"))
            s_got = [sem("s_got0"), sem("s_got1")]
        with nc.Block() as block:
            @block.gpsimd
            def _(pool):
                if G:
                    with pool.Fori(0, BLOCKS // 2) as i:
                        for j in range(2):
                            pool.wait_ge(s_idx, 2 * i + (j + 1))
                            pool.wait_ge(s_placed, 2 * i + (j + 1))
                            pool.sem_inc(s_go, 1)
                            for u in range(G):
                                pool.indirect_dma_start(out=got[j][:, u, :], out_offset=None, in_=al_dram,
                                                        in_offset=bass.IndirectOffsetOnAxis(ap=idx_now[j][:, u:u + 1], axis=0)).then_inc(s_got[j], 16)
                send(pool)

            @block.scalar
            def _(act):
                if not G:
                    return
                act.sem_inc(s_placed, 2)

                def indices(i, j):
                    act.sem_inc(s_act, 1)
                    act.activation(idx_now[j][:], g.src_idx[:, bass.ds((2 * i + j) * BT + BT - G, G)], ACT.Copy).then_inc(s_idx, 1)

                def place(i, j):
                    act.wait_ge(s_got[j], 16 * G * i + 16 * G)
                    act.sem_inc(s_act, 1)
                    act.activation(ae[0][:, bass.ds((2 * i + j) * BT + BT - G, G), :], got[j][:], ACT.Copy).then_inc(s_placed, 1)

                indices(0, 0)
                with act.Fori(0, BLOCKS // 2 - 1) as i:
                    indices(i, 1)
                    place(i, 0)
                    indices(i + 1, 0)
                    place(i, 1)
                indices(BLOCKS // 2 - 1, 1)
                place(BLOCKS // 2 - 1, 0)
                place(BLOCKS // 2 - 1, 1)

            @block.sync
            def _(sp):
                with sp.Fori(0, BLOCKS // 2) as i:
                    for j in range(2):
                        for s in range(2):
                            sp.wait_ge(s_bank, 2 * NB * i + (NB * j + (NB0, NB)[s]))
                            edges = bass.ds((2 * i + j) * (BT * P), BY_PE[s] * P)
                            sp.dma_start(lo_rows[s][j][:], g.parts_dram[s:s + 1, edges].to_broadcast([P, BY_PE[s] * P])).then_inc(s_lo[s][j], 16)
                            sp.dma_start(tile_rows[s][j][:], g.parts_dram[2 + 3 * s:5 + 3 * s, edges]).then_inc(s_lo[s][j], 16)

            @block.vector
            def _(dve):
                ch = Chain(dve, s_chain)
                ch.link(dve.tensor_copy(rest[:], al[:].rearrange("p t s c -> p s c t")))
                for j in range(3):
                    ch.link(dve.tensor_copy(part[j][:], rest[:]))
                    if j < 2:
                        ch.link(dve.tensor_tensor(rest[:], rest[:], part[j][:], ALU.subtract))
                t, twice, square = quad[:, 0, :], quad[:, 1, :], quad[:, 2, :]
                ch.link(dve.tensor_scalar(row_is[:], g.iota25[0:3, 0:3], g.iota_col[0:3, 0:1], None, ALU.is_equal))
                ch.link(dve.tensor_scalar(t, g.iota25[0:3, 0:NT], float(-MID), None, ALU.add))
                ch.link(dve.tensor_tensor(square, t, t, ALU.mult))
                ch.link(dve.tensor_scalar(twice, t, row_is[:, 1:2], 2.0, ALU.mult, ALU.mult))
                ch.link(dve.tensor_scalar(square, square, row_is[:, 2:3], None, ALU.mult))
                ch.link(dve.tensor_tensor(t, twice, square, ALU.subtract))
                ch.link(dve.tensor_scalar(t, t, row_is[:, 0:1], FAR, ALU.subtract, ALU.mult))
                ch.link(dve.tensor_copy(quad_bf[:], t.unsqueeze(1).to_broadcast([3, C, NT])))
                dve.sem_inc(s_parts, 1)
                dve.sem_inc(s_bank, 2 * NB)
                dve.sem_inc(s_picked, RING)

                def compare(i, j):
                    for s in range(2):
                        dve.wait_ge(s_lo[s][j], 32 * i + 32)
                        dve.wait_ge(s_bank, 2 * NB * i + (NB * j + (NB0, NB)[s]))
                        dve.tensor_scalar(hot_lo[s][j][:], lo_rows[s][j][:], g.iota_col[:, 0:1], None, ALU.is_equal).then_inc(s_hot, 1)

                def select(i, j):
                    for b in range(NB):
                        at = NB * j + b
                        dve.wait_ge(s_bank, 2 * NB * i + (at + 1 + 2 * NB))
                        dve.tensor_reduce(ae[side(b)][:, bass.ds((2 * i + j) * BT + (b - NB0 * side(b)) * TB, TB), :], ps[at % RING][:],
                                          AX.X, ALU.max).then_inc(s_picked, 1)

                compare(0, 0)
                with dve.Fori(0, BLOCKS // 2 - 1) as i:
                    compare(i, 1)
                    select(i, 0)
                    compare(i + 1, 0)
                    select(i, 1)
                compare(BLOCKS // 2 - 1, 1)
                select(BLOCKS // 2 - 1, 0)
                select(BLOCKS // 2 - 1, 1)

            @block.tensor
            def _(pe):
                pe.wait_ge(s_parts, 1)
                with pe.Fori(0, BLOCKS // 2) as i:
                    for at in range(2 * NB):
                        j, b, r = at // NB, at % NB, at % RING
                        s = side(b)
                        if b in (0, NB0):
                            pe.wait_ge(s_hot, 4 * i + (2 * j + s + 1))
                        pe.wait_ge(s_picked, 2 * NB * i + (at + 1))
                        for k in range(TB):
                            tile = (b - NB0 * s) * TB + k
                            into = ps[r][:, k].rearrange("p c t -> p (c t)")
                            edges = slice(tile * P, (tile + 1) * P)
                            pe.matmul(into, tile_rows[s][j][:, edges], quad_bf[:].rearrange("p c t -> p (c t)"), start=True, stop=False)
                            for n in range(3):
                                mm = pe.matmul(into, hot_lo[s][j][:, edges], part[n][:, s].rearrange("p c t -> p (c t)"),
                                               start=False, stop=(n == 2))
                        mm.then_inc(s_bank, 1)
    return ae


def edge_softmax(nc, g, name, ae, seg, build_seg, heads, send_pairs, ctx):
    C = heads
    R = CH * C
    ext = ctx.enter_context(nc.sbuf_tensor(name + "_ext", [P, ET, 2 * C + 2], F32, side="right"))
    with ExitStack() as c:
        tb = lambda n, s, d=F32: c.enter_context(nc.sbuf_tensor(n, s, d, allow_name_mangling=True))
        run = tb("run", [R, CL])
        d_f, brk = seg.dst_f, seg.brk
        if build_seg:
            seg.open(c)
        val = tb("val", [R, CL])
        most = seg.room[:, 0:ET * C].rearrange("p (k c) -> p k c", c=C)
        ends = tb("ends_c", [R, 4])
        row = tb("row", [1, 4, R])
        hc = tb("hc", [1, 6, C, CH])
        back = tb("back", [R, 4])
        ps = [c.enter_context(nc.psum_tensor(f"sx{r}", [P, 4, P], F32, allow_name_mangling=True)) for r in range(4)]
        small = c.enter_context(nc.psum_tensor("small", [P, 512], F32, allow_name_mangling=True))
        sem = g.semaphores(c)
        s_in, s_val, s_ends, s_row, s_back_row, s_back, s_run, s_out, s_most, s_logit, s_p, s_chain = map(sem, (
            "s_in", "s_val", "s_ends", "s_row", "s_back_row", "s_back", "s_run", "s_out", "s_most", "s_logit", "s_p", "s_chain"))
        s_step = sem("s_step")
        by_step = ext[:].rearrange("p k x -> p (k x)")[:, 0:ET * C]
        G4 = -(-CI // 4)
        ids = g.ident
        send = list_sender(nc, g, c, send_pairs)
        with nc.Block() as block:
            @block.gpsimd
            def _(pool):
                send(pool)

            @block.sync
            def _(sp):
                if build_seg:
                    seg.load(sp)

            @block.tensor
            def _(pe):
                pe.wait_ge(s_step, 1)
                for q in range(G4):
                    if q >= 4:
                        pe.wait_ge(s_val, q - 3)
                    for i in range(4 * q, min(CI, 4 * q + 4)):
                        mm = pe.transpose(ps[q % 4][0:R, i % 4, :], by_step[:, i * R:(i + 1) * R], ids[:])
                    mm.then_inc(s_in, 1)
                pe.wait_ge(s_ends, 1)
                for i in range(4):
                    mm = pe.transpose(small[0:1, i * R:(i + 1) * R], ends[:, i:i + 1], ids[0:R, 0:R])
                mm.then_inc(s_row, 1)
                pe.wait_ge(s_back_row, 1)
                for i in range(4):
                    mm = pe.transpose(small[0:R, i:i + 1], row[0:1, i, :], ids[0:1, 0:1])
                mm.then_inc(s_back, 1)
                pe.wait_ge(s_run, 1)
                for q in range(G4):
                    if q >= 4:
                        pe.wait_ge(s_most, q - 3)
                    for i in range(4 * q, min(CI, 4 * q + 4)):
                        mm = pe.transpose(ps[q % 4][:, i % 4, 0:R], val[:, i * P:(i + 1) * P], ids[0:R, 0:R])
                    mm.then_inc(s_out, 1)

            @block.scalar
            def _(act):
                act.activation(by_step.rearrange("p (i c h) -> p i c h", c=CH, h=C),
                               ae[0][:].rearrange("p (c i) h -> p i c h", i=CI), ACT.Copy).then_inc(s_step, 1)
                for q in range(G4):
                    n = min(CI, 4 * q + 4) - 4 * q
                    act.wait_ge(s_in, q + 1)
                    act.activation(val[:, 4 * q * P:(4 * q + n) * P].rearrange("r (a b) -> r a b", b=P), ps[q % 4][0:R, 0:n, :], ACT.Copy).then_inc(s_val, 1)
                for q in range(G4):
                    n = min(CI, 4 * q + 4) - 4 * q
                    act.wait_ge(s_out, q + 1)
                    act.activation(most[:].rearrange("p (c i) h -> p i c h", i=CI)[:, 4 * q:4 * q + n],
                                   ps[q % 4][:, 0:n, 0:R].rearrange("p i (c h) -> p i c h", h=C), ACT.Copy).then_inc(s_most, 1)
                act.wait_ge(s_logit, 1)
                act.activation(ext[:, :, 0:C], ae[0][:], ACT.Exp).then_inc(s_p, 1)

            @block.vector
            def _(dve):
                ch = Chain(dve, s_chain)
                if build_seg:
                    seg.pad(dve)
                    seg.build(dve)
                    dve.wait_ge(seg.s_step, 4)
                dve.wait_ge(s_val, G4)
                ch.link(dve.tensor_tensor_scan(run[:], brk[:, 0:CL], val[:], 0.0, ALU.add, ALU.max))
                ch.link(dve.tensor_copy(ends[:, 0:1], run[:, CL - 1:CL]))
                ch.link(dve.tensor_tensor_scan(val[:, ::-1], brk[:, 1:CL + 1][:, ::-1], run[:, ::-1], 0.0, ALU.add, ALU.max))
                dve.tensor_copy(ends[:, 1:2], val[:, 0:1])
                dve.tensor_copy(ends[:, 2:3], d_f[:, CL - 1:CL])
                ch.link(dve.tensor_copy(ends[:, 3:4], d_f[:, 0:1]))
                dve.sem_inc(s_ends, 1)
                dve.wait_ge(s_row, 1)
                fend, mbeg, dlast, dfirst, wf, wb = (hc[:, i] for i in range(6))
                for i in range(4):
                    last = dve.tensor_copy(hc[:, i], small[0:1, i * R:(i + 1) * R].rearrange("o (c h) -> o h c", h=C))
                ch.link(last)
                dve.memset(wf[:, :, 0:1], 1.0)
                dve.memset(wb[:, :, CH - 1:CH], 1.0)
                dve.tensor_tensor(wf[:, :, 1:CH], dlast[:, :, 1:CH], dlast[:, :, 0:CH - 1], ALU.not_equal)
                ch.link(dve.tensor_tensor(wb[:, :, 0:CH - 1], dfirst[:, :, 1:CH], dfirst[:, :, 0:CH - 1], ALU.not_equal))
                ch.link(dve.tensor_scalar(hc[:, 4:6], hc[:, 4:6], -BIG, None, ALU.mult))
                one = lambda a: a.rearrange("o h c -> o (h c)")
                ch.link(dve.tensor_tensor_scan(one(fend), one(wf), one(fend), 0.0, ALU.add, ALU.max))
                ch.link(dve.tensor_tensor_scan(one(mbeg)[:, ::-1], one(wb)[:, ::-1], one(mbeg)[:, ::-1], 0.0, ALU.add, ALU.max))
                ch.link(dve.memset(row[:], -BIG))
                r4 = row[:].rearrange("o f (c h) -> o f c h", h=C)
                sw = lambda a: a.rearrange("o h c -> o c h")
                dve.tensor_copy(r4[:, 0, 1:CH], sw(fend)[:, 0:CH - 1])
                dve.tensor_copy(r4[:, 1, 0:CH - 1], sw(mbeg)[:, 1:CH])
                dve.tensor_copy(r4[:, 2, 1:CH], sw(dlast)[:, 0:CH - 1])
                ch.link(dve.tensor_copy(r4[:, 3, 0:CH - 1], sw(dfirst)[:, 1:CH]))
                dve.sem_inc(s_back_row, 1)
                dve.wait_ge(s_back, 1)
                ch.link(dve.tensor_copy(back[:], small[0:R, 0:4]))
                for j in range(2):
                    ch.link(dve.tensor_scalar(run[:], d_f[:], back[:, 2 + j:3 + j], -BIG, ALU.not_equal, ALU.mult))
                    ch.link(dve.scalar_tensor_tensor(val[:], run[:], back[:, j:j + 1], val[:], ALU.add, ALU.max))
                dve.sem_inc(s_run, 1)
                lo = ae[0][:]
                ch.link(dve.tensor_tensor(lo, ae[0][:], ae[1][:], ALU.add))
                ch.link(dve.scalar_tensor_tensor(lo, lo, NEG, lo, ALU.mult, ALU.max))
                dve.wait_ge(s_most, G4)
                dve.tensor_copy(ext[:, :, 2 * C:2 * C + 1], g.is_last[:].unsqueeze(2))
                dve.tensor_copy(ext[:, :, 2 * C + 1:2 * C + 2], g.dst_key[:].unsqueeze(2))
                dve.tensor_tensor(ext[:, :, C:2 * C], most[:], g.is_last[:].unsqueeze(2).to_broadcast([P, ET, C]), ALU.mult)
                ch.link(dve.tensor_tensor(ae[1][:], most[:], ae[1][:], ALU.add))
                ch.link(dve.scalar_tensor_tensor(ae[1][:], ae[1][:], NEG, ae[1][:], ALU.mult, ALU.max))
                ch.link(dve.tensor_tensor(lo, lo, ae[1][:], ALU.subtract))
                dve.sem_inc(s_logit, 1)
    return ext


def aggregate(nc, g, name, table, idx, visits, values, heads, summed, bias, acc):
    vt, minus = visits
    VW = values.shape[2]
    W = D + summed
    with ExitStack() as c:
        tb = lambda n, s, d=F32: c.enter_context(nc.sbuf_tensor(n, s, d, allow_name_mangling=True))
        idx_now = [tb(f"idx_now{u}", [P, 1], I32) for u in range(SLOTS)]
        rows = [tb(f"rows{u}", [P, D]) for u in range(SLOTS)]
        msg = [tb(f"msg{u}", [P, D + VW]) for u in range(SLOTS)]
        hot = [tb(f"hot{u}", [P, P]) for u in range(SLOTS)]
        ps = [c.enter_context(nc.psum_tensor(f"sum{u}", [P, W], F32, allow_name_mangling=True)) for u in range(SLOTS)]
        sem = g.semaphores(c)
        s_go, s_act, s_idx, s_values, s_msg, s_sum, s_acc, s_hot = map(sem, ("s_go", "s_act", "s_idx", "s_values", "s_msg", "s_sum", "s_acc", "s_hot"))
        s_rows = [sem(f"s_rows{u}") for u in range(SLOTS)]
        if bias is not None:
            b_row = tb("b_row2", [P, D])
            s_bias = sem("s_bias")
        ROUNDS = V // SLOTS
        eng = mybir.EngineType
        def of_round(which, row, i):
            _, values = nc.values_load_multi_w_load_instructions(
                vt[0:1, row, bass.ds(i * SLOTS, SLOTS)], engines=(which,), min_val=0, max_val=(ET - 1, DUMMY)[row],
                skip_runtime_bounds_check_because="the table's values are clamped where it is made")
            return values
        with nc.Block() as block:
            @block.sync
            def _(sp):
                if bias is not None:
                    sp.dma_start(b_row[:], bias.rearrange("(o d) -> o d", o=1).to_broadcast([P, D])).then_inc(s_bias, 16)

            @block.gpsimd
            def _(pool):
                with pool.Fori(0, ROUNDS) as i:
                    for u in range(SLOTS):
                        pool.wait_ge(s_idx, SLOTS * i + (u + 1))
                        pool.wait_ge(s_msg, SLOTS * i + (u + 1))
                        pool.sem_inc(s_go, 1)
                        pool.indirect_dma_start(out=rows[u][:], out_offset=None, in_=table,
                                                in_offset=bass.IndirectOffsetOnAxis(ap=idx_now[u][:], axis=0)).then_inc(s_rows[u], 16)

            @block.scalar
            def _(act):
                with act.Fori(0, ROUNDS) as i:
                    ks = of_round(eng.Activation, 0, i)
                    for u in range(SLOTS):
                        act.wait_ge(s_msg, SLOTS * i + (u + 1))
                        act.sem_inc(s_act, 1)
                        act.activation(idx_now[u][:], idx[:, bass.ds(ks[u], 1)], ACT.Copy).then_inc(s_idx, 1)
                        act.wait_ge(s_sum, SLOTS * i + (u + 1))
                        act.sem_inc(s_act, 1)
                        act.activation(msg[u][:, D:], values[:, bass.ds(ks[u], 1), :].rearrange("p o x -> p (o x)"), ACT.Copy).then_inc(s_values, 1)

            @block.vector
            def _(dve):
                dve.sem_inc(s_msg, SLOTS)
                dve.sem_inc(s_sum, SLOTS)
                if bias is None:
                    dve.memset(acc[:], 0.0).then_inc(s_acc, 1)
                else:
                    dve.wait_ge(s_bias, 16)
                    dve.tensor_copy(acc[:], b_row[:].unsqueeze(1).to_broadcast([P, NT + 1, D])).then_inc(s_acc, 1)
                for u in range(SLOTS - LAG, SLOTS):
                    dve.memset(ps[u][:], 0.0).then_inc(s_acc, 1)
                dve.sem_inc(s_acc, SLOTS - LAG)

                def add(i, u, ts):
                    dve.wait_ge(s_sum, SLOTS * i + (u - LAG + 1 + SLOTS))
                    dve.wait_ge(s_acc, SLOTS * i + (u + 1 + SLOTS))
                    into = acc[:, bass.ds(ts[u], 1), :].rearrange("p o w -> p (o w)")
                    dve.tensor_tensor(into, ps[(u - LAG) % SLOTS][:], into, ALU.add).then_inc(s_acc, 1)

                with dve.Fori(0, ROUNDS) as i:
                    ts = of_round(eng.DVE, 1, i)
                    for u in range(SLOTS):
                        dve.wait_ge(s_values, SLOTS * i + (u + 1))
                        dve.tensor_scalar(hot[u][:], g.iota_row[:], msg[u][:, D + VW - 1:], minus[:, bass.ds(SLOTS * i + u, 1)],
                                          ALU.subtract, ALU.is_equal).then_inc(s_hot, 1)
                        dve.wait_ge(s_rows[u], 16 * i + 16)
                        if heads == 1:
                            dve.tensor_scalar(msg[u][:, 0:D], rows[u][:], msg[u][:, D:D + 1], None, ALU.mult).then_inc(s_msg, 1)
                        else:
                            dve.tensor_tensor(msg[u][:, 0:D].rearrange("p (h f) -> p h f", h=heads), rows[u][:].rearrange("p (h f) -> p h f", h=heads),
                                              msg[u][:, D:D + heads].unsqueeze(2).to_broadcast([P, heads, D // heads]), ALU.mult).then_inc(s_msg, 1)
                        add(i, u, ts)
                ts = of_round(eng.DVE, 1, ROUNDS)
                for u in range(LAG):
                    add(ROUNDS, u, ts)

            @block.tensor
            def _(pe):
                with pe.Fori(0, ROUNDS) as i:
                    for u in range(SLOTS):
                        pe.wait_ge(s_hot, SLOTS * i + (u + 1))
                        pe.wait_ge(s_acc, SLOTS * i + (u + LAG + 2))
                        pe.wait_ge(s_msg, SLOTS * i + (u + 1 + SLOTS))
                        pe.matmul(ps[u][:], hot[u][:], msg[u][:, 0:W], start=True, stop=True).then_inc(s_sum, 1)


def finish_attention(nc, g, acc, h, al, bias, heads, x):
    C = heads
    with ExitStack() as c:
        tb = lambda n, s, d=F32: c.enter_context(nc.sbuf_tensor(n, s, d, allow_name_mangling=True))
        b_row = tb("b_row", [P, D])
        w = tb("w_fin", [P, 7, NT, C])
        sem = g.semaphores(c)
        s_b, s_chain, s_logit, s_exp, s_coef, s_own, s_biased = map(sem, ("s_b", "s_chain", "s_logit", "s_exp", "s_coef", "s_own", "s_biased"))
        own, near, top, den, c_near, c_own, spare = (w[:, i] for i in range(7))
        heads_of = lambda a: a.rearrange("p t (h f) -> p t h f", h=C)
        over = lambda a: a.unsqueeze(3).to_broadcast([P, NT, C, D // C])
        sums = acc[:, 0:NT, 0:D]
        with nc.Block() as block:
            @block.sync
            def _(sp):
                sp.dma_start(b_row[:], bias.rearrange("(o d) -> o d", o=1).to_broadcast([P, D])).then_inc(s_b, 16)

            @block.vector
            def _(dve):
                ch = Chain(dve, s_chain)
                ch.link(dve.tensor_scalar(spare, acc[:, 0:NT, D + 2 * C:].to_broadcast([P, NT, C]), -1.0, BIG, ALU.add, ALU.mult))
                ch.link(dve.tensor_tensor(near, acc[:, 0:NT, D + C:D + 2 * C], spare, ALU.add))
                ch.link(dve.tensor_tensor(near, near, al[:, :, 1, :], ALU.add))
                ch.link(dve.tensor_tensor(own, al[:, :, 0, :], al[:, :, 1, :], ALU.add))
                ch.link(dve.scalar_tensor_tensor(w[:, 0:2], w[:, 0:2], NEG, w[:, 0:2], ALU.mult, ALU.max))
                ch.link(dve.tensor_tensor(top, own, near, ALU.max))
                ch.link(dve.tensor_tensor(w[:, 0:2], w[:, 0:2], top.unsqueeze(1).to_broadcast([P, 2, NT, C]), ALU.subtract))
                dve.sem_inc(s_logit, 1)
                dve.wait_ge(s_exp, 1)
                ch.link(dve.tensor_tensor(den, acc[:, 0:NT, D:D + C], near, ALU.mult))
                ch.link(dve.tensor_tensor(den, den, own, ALU.add))
                ch.link(dve.tensor_scalar(den, den, 1e-16, None, ALU.add))
                ch.link(dve.reciprocal(spare, den))
                ch.link(dve.tensor_tensor(c_own, own, spare, ALU.mult))
                dve.sem_inc(s_coef, 1)
                ch.link(dve.tensor_tensor(c_near, near, spare, ALU.mult))
                ch.link(dve.tensor_tensor(heads_of(sums), heads_of(sums), over(c_near), ALU.mult))
                if x is None:
                    dve.wait_ge(s_b, 16)
                    ch.link(dve.tensor_tensor(sums, sums, b_row[:].unsqueeze(1).to_broadcast([P, NT, D]), ALU.add))
                dve.wait_ge(s_own, NT if C == 1 else 1)
                ch.link(dve.tensor_tensor(sums, sums, h[:], ALU.add))
                if x is not None:
                    dve.wait_ge(s_biased, 1)
                    dve.tensor_tensor(x[:], x[:], sums, ALU.add)

            @block.scalar
            def _(act):
                act.wait_ge(s_logit, 1)
                act.activation(w[:, 0:2], w[:, 0:2], ACT.Exp).then_inc(s_exp, 1)
                if C == 1:
                    act.wait_ge(s_coef, 1)
                    for t in range(NT):
                        act.activation(h[:, t, :], h[:, t, :], ACT.Copy, scale=c_own[:, t, :]).then_inc(s_own, 1)

            @block.gpsimd
            def _(pool):
                if x is not None:
                    pool.wait_ge(s_b, 16)
                    pool.tensor_tensor(x[:], x[:], b_row[:].unsqueeze(1).to_broadcast([P, NT, D]), ALU.add).then_inc(s_biased, 1)
                if C > 1:
                    pool.wait_ge(s_coef, 1)
                    pool.tensor_tensor(heads_of(h[:]), heads_of(h[:]), over(c_own), ALU.mult).then_inc(s_own, 1)


def by_source(nc, g, hot, ends, part, zero_dram):
    ZT = 8
    g.list_dram = nc.dram_tensor("list_dram", (EP, 4), F32, kind="Internal").ap()
    with ExitStack() as c:
        tb = lambda n, s, d=F32: c.enter_context(nc.sbuf_tensor(n, s, d, allow_name_mangling=True))
        rank = tb("rank", [P, NT, ET])
        total = tb("total", [P, NT])
        base = tb("base", [P, NT])
        place = tb("place", [P, ET])
        number = tb("number", [P, ET])
        ps = c.enter_context(nc.psum_tensor("base_ps", [P, NT], F32, allow_name_mangling=True))
        sem = g.semaphores(c)
        s_number, s_scan, s_total, s_base, s_chain, s_zero, s_zeroed = map(
            sem, ("s_number", "s_scan", "s_total", "s_base", "s_chain", "s_zero", "s_zeroed"))
        zeros = tb("zeros", [P, ZT, D])
        with nc.Block() as block:
            @block.sync
            def _(sp):
                sp.wait_ge(s_zero, 1)
                for r in range(0, ST, ZT):
                    sp.dma_start(zero_dram[r * P:(r + ZT) * P].rearrange("(p a) d -> p a d", p=P), zeros[:]).then_inc(s_zeroed, 16)
                sp.wait_ge(s_zeroed, 16 * (ST // ZT))

            @block.gpsimd
            def _(pool):
                pool.memset(zeros[:], 0.0).then_inc(s_zero, 1)
                pool.iota(number[:], [[P, ET]], base=0, channel_multiplier=1, allow_small_or_imprecise_dtypes=True).then_inc(s_number, 1)

            @block.tensor
            def _(pe):
                pe.wait_ge(s_total, 1)
                pe.matmul(ps[:], g.before[:], total[:], start=True, stop=True).then_inc(s_base, 1)

            @block.vector
            def _(dve):
                ch = Chain(dve, s_chain)
                dve.tensor_copy(total[:, 0:1], part[:, 0:1])
                ch.link(dve.tensor_tensor(total[:, 1:NT], part[:, 1:NT], part[:, 0:NT - 1], ALU.subtract))
                dve.sem_inc(s_total, 1)
                dve.wait_ge(s_base, 1)
                ch.link(dve.tensor_scalar(base[:], ps[:], -1.0, None, ALU.add))
                ch.link(dve.tensor_tensor(base[:, 1:NT], base[:, 1:NT], ends[:, 0:NT - 1], ALU.add))
                for t in range(NT):
                    dve.tensor_tensor_scan(rank[:, t, :], g.ones[:, 0:1].to_broadcast([P, ET]), hot[:, :, t], base[:, t:t + 1],
                                           ALU.mult, ALU.add).then_inc(s_scan, 1)
                dve.wait_ge(s_scan, NT)
                ch.link(dve.tensor_tensor(rank[:], rank[:], hot[:].rearrange("p k t -> p t k"), ALU.mult))
                ch.link(dve.tensor_reduce(place[:], rank[:].rearrange("p t k -> p k t"), AX.X, ALU.add))
                dve.wait_ge(s_number, 1)
                ch.link(dve.scalar_tensor_tensor(number[:], g.src_key[:], float(NP), number[:], ALU.is_ge, ALU.mult))
                ch.link(dve.tensor_tensor(g.spot[:], place[:], number[:], ALU.add))


def read_list(nc, g, ctx):
    sb = lambda n, s, d=F32: ctx.enter_context(nc.sbuf_tensor(n, s, d, allow_name_mangling=True))
    idx = sb("l_idx", [P, ET], I32)
    values = sb("l_values", [P, ET, 2])
    with ExitStack() as c:
        rows = c.enter_context(nc.sbuf_tensor("l_rows", [P, RG, P, 4], F32, allow_name_mangling=True))
        ps = c.enter_context(nc.psum_tensor("l_turned", [P, 3, 512], F32, allow_name_mangling=True))
        s_rows, s_turned = map(g.semaphores(c), ("s_rows", "s_turned"))
        with nc.Block() as block:
            @block.sync
            def _(sp):
                o = g.list_dram
                sp.dma_start(rows[:, 0:3], o[0:3 * P * P].rearrange("(g k e) f -> k g e f", k=P, e=P)).then_inc(s_rows, 16)
                sp.dma_start(rows[0:ET - 3 * P, 3], o[3 * P * P:EP].rearrange("(k e) f -> k e f", e=P)).then_inc(s_rows, 16)

            @block.tensor
            def _(pe):
                pe.wait_ge(s_rows, 32)
                for f in range(3):
                    for r in range(RG):
                        k = min(P, ET - r * P)
                        mm = pe.transpose(ps[:, f, r * P:r * P + k], rows[0:k, r, :, f], g.ident[0:k, 0:k])
                mm.then_inc(s_turned, 1)

            @block.vector
            def _(dve):
                dve.wait_ge(s_turned, 1)
                dve.tensor_scalar(idx[:], ps[:, 0, 0:ET], float(N - 1), None, ALU.min)
                dve.tensor_copy(values[:, :, 0], ps[:, 2, 0:ET])
                dve.tensor_copy(values[:, :, 1], ps[:, 1, 0:ET])
    return idx, values


def bias_columns(nc, g, b, parts, ctx):
    cols = ctx.enter_context(nc.sbuf_tensor("b1_cols", [P, EXPERTS, parts], F32, allow_name_mangling=True))
    with ExitStack() as c:
        rows = c.enter_context(nc.sbuf_tensor("b1_rows", [EXPERTS * parts, P], F32, allow_name_mangling=True))
        ps = c.enter_context(nc.psum_tensor("b1_ps", [P, EXPERTS * parts], F32, allow_name_mangling=True))
        s_rows, s_turned = map(g.semaphores(c), ("s_rows", "s_turned"))
        with nc.Block() as block:
            @block.sync
            def _(sp):
                sp.dma_start(rows[:], b.rearrange("e (k p) -> (e k) p", p=P)).then_inc(s_rows, 16)

            @block.tensor
            def _(pe):
                pe.wait_ge(s_rows, 16)
                pe.transpose(ps[:], rows[:], g.ident[0:EXPERTS * parts, 0:EXPERTS * parts]).then_inc(s_turned, 1)

            @block.vector
            def _(dve):
                dve.wait_ge(s_turned, 1)
                dve.tensor_copy(cols[:].rearrange("p e k -> p (e k)"), ps[:])
    return cols


def first_largest(dve, ch, g, values, best, hot, work):
    shape = [P, NT, EXPERTS]
    ch.link(dve.tensor_reduce(best, values, AX.X, ALU.max))
    ch.link(dve.tensor_tensor(hot, values, best.unsqueeze(2).to_broadcast(shape), ALU.is_equal))
    ch.link(dve.tensor_tensor(hot, hot, g.falling[:].unsqueeze(1).to_broadcast(shape), ALU.mult))
    ch.link(dve.tensor_reduce(work, hot, AX.X, ALU.max))
    ch.link(dve.tensor_tensor(hot, hot, work.unsqueeze(2).to_broadcast(shape), ALU.is_equal))


def route_top2(nc, g, probs, xn, rows_dram, W1, W2, b2, ctx):
    FC = F1 // P
    sb = lambda n, s, d=F32: ctx.enter_context(nc.sbuf_tensor(n, s, d, allow_name_mangling=True))
    m = Mixture()
    m.take = sb("take2", [P, 2, NT], I32)
    m.factor = sb("factor2", [P, 2, NT])
    m.cw = sb("cw", [P, NT, EXPERTS])
    m.expert_of = sb("expert_of", [1, ST], I32)
    m.w1 = sb("w1_all", [P, EXPERTS, KC, F1])
    m.w2 = sb("w2_all", [P, EXPERTS, FC, D])
    m.b2 = sb("b2_all", [EXPERTS, D])
    with ExitStack() as c:
        tb = lambda n, s, d=F32: c.enter_context(nc.sbuf_tensor(n, s, d, allow_name_mangling=True))
        hot = tb("hot_r2", [P, 2, NT, EXPERTS])
        both = tb("both", [P, NT, EXPERTS])
        number = tb("number2", [P, NT])
        valid = tb("valid2", [P, NT])
        spare = tb("spare2", [P, NT])
        spot = tb("spot2", [P, 2, NT])
        tot = tb("tot2", [P, EXPERTS, NT])
        run = tb("run_r2", [P, EXPERTS, NT])
        rank = tb("rank_r2", [P, NT, EXPERTS])
        mine = tb("mine2", [P, 2, NT, EXPERTS])
        tiles_i = tb("tiles_i", [P, EXPERTS], I32)
        tiles = tb("tiles", [P, 3, EXPERTS])
        slot = tb("slot", [1, ST])
        past = tb("past2", [1, ST, EXPERTS])
        put = tb("put2", [P, 2, NT], I32)
        ps = c.enter_context(nc.psum_tensor("route2_ps", [P, 2, 512], F32, allow_name_mangling=True))
        sem = g.semaphores(c)
        s_number, s_chain, s_hot, s_ranks, s_put, s_sent, s_w = map(sem, ("s_number", "s_chain", "s_hot", "s_ranks", "s_put", "s_sent", "s_w"))
        shape = [P, NT, EXPERTS]
        with nc.Block() as block:
            @block.sync
            def _(sp):
                sp.dma_start(m.w1[:].rearrange("p e k f -> p (e k) f"), W1.rearrange("e (k p) f -> p (e k) f", p=P)).then_inc(s_w, 16)
                sp.dma_start(m.b2[:], b2).then_inc(s_w, 16)
                sp.dma_start(m.w2[:].rearrange("p e k f -> p (e k) f"), W2.rearrange("e (k p) f -> p (e k) f", p=P)).then_inc(s_w, 16)
                sp.wait_ge(s_w, 48)

            @block.gpsimd
            def _(pool):
                pool.iota(number[:], [[P, NT]], base=0, channel_multiplier=1, allow_small_or_imprecise_dtypes=True).then_inc(s_number, 1)
                pool.iota(slot[:], [[1, ST]], base=0, channel_multiplier=0, allow_small_or_imprecise_dtypes=True).then_inc(s_number, 1)
                pool.wait_ge(s_put, 1)
                for t in range(NT):
                    for i in range(2):
                        pool.indirect_dma_start(out=rows_dram, out_offset=bass.IndirectOffsetOnAxis(ap=put[:, i, t:t + 1], axis=0),
                                                in_=xn[:, t, :], in_offset=None).then_inc(s_sent, 16)
                pool.wait_ge(s_sent, 16 * 2 * NT)

            @block.tensor
            def _(pe):
                pe.wait_ge(s_hot, 1)
                rows = both[:].rearrange("p t e -> p (t e)")
                pe.matmul(ps[:, 0, 0:NT * EXPERTS], g.before[:], rows, start=True, stop=True)
                pe.matmul(ps[:, 1, 0:NT * EXPERTS], g.ones[:], rows, start=True, stop=True).then_inc(s_ranks, 1)

            @block.vector
            def _(dve):
                ch = Chain(dve, s_chain)
                first_largest(dve, ch, g, probs[:], m.factor[:, 0], hot[:, 0], spare[:])
                ch.link(dve.tensor_tensor(m.cw[:], probs[:], hot[:, 0], ALU.mult))
                ch.link(dve.scalar_tensor_tensor(probs[:], hot[:, 0], -2.0, probs[:], ALU.mult, ALU.add))
                first_largest(dve, ch, g, probs[:], m.factor[:, 1], hot[:, 1], spare[:])
                ch.link(dve.tensor_tensor(both[:], probs[:], hot[:, 1], ALU.mult))
                ch.link(dve.tensor_tensor(m.cw[:], m.cw[:], both[:], ALU.add))
                dve.wait_ge(s_number, 2)
                ch.link(dve.tensor_scalar(valid[:], number[:], float(N), None, ALU.is_lt))
                for i in range(2):
                    ch.link(dve.tensor_tensor(hot[:, i], hot[:, i], valid[:].unsqueeze(2).to_broadcast(shape), ALU.mult))
                ch.link(dve.tensor_tensor(both[:], hot[:, 0], hot[:, 1], ALU.add))
                dve.sem_inc(s_hot, 1)
                dve.wait_ge(s_ranks, 1)
                ch.link(dve.tensor_copy(tot[:], ps[:, 1, 0:NT * EXPERTS].rearrange("p (t e) -> p e t", e=EXPERTS)))
                for e in range(EXPERTS):
                    last = dve.tensor_tensor_scan(run[:, e, :], g.ones[:, 0:NT], tot[:, e, :], 0.0, ALU.mult, ALU.add)
                ch.link(last)
                need, upto, first = (tiles[:, i, :] for i in range(3))
                ch.link(dve.tensor_scalar(tiles_i[:], run[:, :, NT - 1], float(P - 1), None, ALU.add))
                ch.link(dve.tensor_scalar(tiles_i[:], tiles_i[:], 7, None, ALU.logical_shift_right))
                ch.link(dve.tensor_copy(need, tiles_i[:]))
                ch.link(dve.tensor_tensor_scan(upto, g.ones[:, 0:EXPERTS], need, 0.0, ALU.mult, ALU.add))
                ch.link(dve.tensor_tensor(first, upto, need, ALU.subtract))
                ch.link(dve.tensor_scalar(first, first, float(P), None, ALU.mult))
                ch.link(dve.tensor_tensor(run[:], run[:], tot[:], ALU.subtract))
                ch.link(dve.tensor_tensor(run[:], run[:], first.unsqueeze(2).to_broadcast([P, EXPERTS, NT]), ALU.add))
                ch.link(dve.tensor_tensor(rank[:], ps[:, 0, 0:NT * EXPERTS].rearrange("p (t e) -> p t e", e=EXPERTS),
                                          run[:].rearrange("p e t -> p t e"), ALU.add))
                ch.link(dve.tensor_tensor(mine[:], hot[:], rank[:].unsqueeze(1).to_broadcast([P, 2] + shape[1:]), ALU.mult))
                ch.link(dve.tensor_reduce(spot[:], mine[:], AX.X, ALU.add))
                dve.tensor_copy(m.take[:], spot[:])
                ch.link(dve.tensor_scalar(number[:], number[:], float(ST * P), None, ALU.add))
                for i in range(2):
                    if i == 1:
                        ch.link(dve.tensor_scalar(number[:], number[:], float(P), None, ALU.add))
                    ch.link(dve.tensor_tensor(spot[:, i], spot[:, i], number[:], ALU.subtract))
                    ch.link(dve.tensor_tensor(spot[:, i], spot[:, i], valid[:], ALU.mult))
                    ch.link(dve.tensor_tensor(put[:, i], spot[:, i], number[:], ALU.add))
                dve.sem_inc(s_put, 1)
                ch.link(dve.tensor_tensor(past[:], slot[:].unsqueeze(2).to_broadcast([1, ST, EXPERTS]),
                                          tiles[0:1, 1, :].unsqueeze(1).to_broadcast([1, ST, EXPERTS]), ALU.is_ge))
                ch.link(dve.tensor_reduce(slot[:], past[:], AX.X, ALU.add))
                ch.link(dve.tensor_scalar(m.expert_of[:], slot[:], float(EXPERTS - 1), None, ALU.min))
    return m


class Mixture:
    pass


def expert_tiles(nc, g, m, rows_dram, y_dram, b1, send_pairs):
    FC = F1 // P
    RING_X = 4
    with ExitStack() as c:
        tb = lambda n, s, d=F32: c.enter_context(nc.sbuf_tensor(n, s, d, allow_name_mangling=True))
        b1_all = bias_columns(nc, g, b1, FC, c)
        xin = [tb(f"xin{j}", [P, D]) for j in range(RING_X)]
        xt = [tb(f"xt{j}", [P, KC * P]) for j in range(2)]
        w1_now = [tb(f"w1_now{j}", [P, KC, F1]) for j in range(2)]
        b1_now = [tb(f"b1_now{j}", [P, FC]) for j in range(2)]
        hid = [tb(f"hid{j}", [P, FC, P]) for j in range(2)]
        y = [tb(f"y{j}", [P, D]) for j in range(2)]
        primed = tb("primed", [P, 1])
        bank = lambda n: c.enter_context(nc.psum_tensor(n, [P, 512], F32, allow_name_mangling=True))
        ps_t = [bank(f"ps_t{j}") for j in range(2)]
        ps_h = [bank(f"ps_h{j}") for j in range(2)]
        ps_y = [bank(f"ps_y{j}") for j in range(2)]
        sem = g.semaphores(c)
        s_turn, s_xt, s_now, s_up, s_hid, s_down, s_y = map(sem, ("s_turn", "s_xt", "s_now", "s_up", "s_hid", "s_down", "s_y"))
        s_xin = [sem(f"s_xin{j}") for j in range(RING_X)]
        s_st = [sem(f"s_st{j}") for j in range(2)]
        U = SLOTS
        PER = U // RING_X
        eng = mybir.EngineType
        def experts(which, i):
            _, values = nc.values_load_multi_w_load_instructions(
                m.expert_of[0:1, bass.ds(i * U, U)], engines=(which,), min_val=0, max_val=EXPERTS - 1,
                skip_runtime_bounds_check_because="the table's values are clamped where it is made")
            return values
        send = list_sender(nc, g, c, send_pairs)
        with nc.Block() as block:
            @block.gpsimd
            def _(pool):
                send(pool)

            @block.sync
            def _(sp):
                with sp.Fori(0, ST // U) as i:
                    for u in range(U):
                        sp.wait_ge(s_turn, U * i + (u + 1))
                        sp.dma_start(xin[u % RING_X][:], rows_dram[bass.ds((U * i + u) * P, P)]).then_inc(s_xin[u % RING_X], 16)

            @block.tensor
            def _(pe):
                pe.sem_inc(s_turn, RING_X)
                pe.sem_inc(s_up, 2)
                pe.sem_inc(s_down, 2)

                def turn(i, u):
                    j = u % 2
                    pe.wait_ge(s_xin[u % RING_X], 16 * PER * i + 16 * (u // RING_X + 1))
                    pe.wait_ge(s_xt, U * i + (u + 1))
                    for k in range(KC):
                        mm = pe.transpose(ps_t[j][:, k * P:(k + 1) * P], xin[u % RING_X][:, k * P:(k + 1) * P], g.ident[:])
                    mm.then_inc(s_turn, 1)

                def up(i, u):
                    j = u % 2
                    pe.wait_ge(s_xt, U * i + (u + 3))
                    pe.wait_ge(s_now, 2 * U * i + 2 * (u + 1))
                    pe.wait_ge(s_hid, FC * U * i + FC * (u + 1))
                    for f in range(FC):
                        for k in range(KC):
                            mm = pe.matmul(ps_h[j][:, f * P:(f + 1) * P], w1_now[j][:, k, f * P:(f + 1) * P],
                                           xt[j][:, k * P:(k + 1) * P], start=(k == 0), stop=(k == KC - 1))
                    mm.then_inc(s_up, 1)

                def down(i, u, e):
                    j = u % 2
                    pe.wait_ge(s_hid, FC * U * i + FC * (u + 3))
                    pe.wait_ge(s_y, U * i + (u + 1))
                    for f in range(FC):
                        mm = pe.matmul(ps_y[j][:, 0:D], hid[j][:, f, :], m.w2[:, bass.ds(e, 1), f, :].rearrange("p o d -> p (o d)"),
                                       start=(f == 0), stop=(f == FC - 1))
                    mm.then_inc(s_down, 1)

                with pe.Fori(0, ST // U) as i:
                    es = experts(eng.PE, i)
                    turn(i, 0)
                    for u in range(U + 1):
                        if u + 1 < U:
                            turn(i, u + 1)
                        if u < U:
                            up(i, u)
                        if u >= 1:
                            down(i, u - 1, es[u - 1])

            @block.scalar
            def _(act):
                act.sem_inc(s_hid, 2 * FC)
                act.activation(primed[:], b1_all[:, 0, 0:1], ACT.Gelu)
                with act.Fori(0, ST // U) as i:
                    for u in range(U + 1):
                        if u < U:
                            act.wait_ge(s_up, U * i + (u + 3))
                            act.wait_ge(s_down, U * i + (u + 1))
                            for f in range(FC):
                                act.activation(hid[u % 2][:, f, :], ps_h[u % 2][:, f * P:(f + 1) * P], ACT.Gelu,
                                               bias=b1_now[u % 2][:, f:f + 1]).then_inc(s_hid, 1)
                        if u >= 1:
                            act.wait_ge(s_y, U * i + (u + 2))
                            act.dma_start(y_dram[bass.ds((U * i + (u - 1)) * P, P)], y[(u - 1) % 2][:]).then_inc(s_st[(u - 1) % 2], 16)
                for j in range(2):
                    act.wait_ge(s_st[j], 16 * (ST // 2 + 1))

            @block.vector
            def _(dve):
                dve.sem_inc(s_xt, 2)
                dve.sem_inc(s_y, 2)
                for j in range(2):
                    dve.sem_inc(s_st[j], 16)

                def inputs(i, u, e):
                    j = u % 2
                    dve.wait_ge(s_up, U * i + (u + 1))
                    dve.tensor_copy(w1_now[j][:], m.w1[:, bass.ds(e, 1)].rearrange("p o k f -> p (o k) f")).then_inc(s_now, 1)
                    dve.wait_ge(s_hid, FC * U * i + FC * (u + 1))
                    dve.tensor_copy(b1_now[j][:], b1_all[:, bass.ds(e, 1), :].rearrange("p o f -> p (o f)")).then_inc(s_now, 1)
                    dve.wait_ge(s_turn, U * i + (u + 1 + RING_X))
                    dve.tensor_copy(xt[j][:], ps_t[j][:, 0:D]).then_inc(s_xt, 1)

                with dve.Fori(0, ST // U) as i:
                    es = experts(eng.DVE, i)
                    inputs(i, 0, es[0])
                    for u in range(U + 1):
                        if u + 1 < U:
                            inputs(i, u + 1, es[u + 1])
                        if u >= 1:
                            dve.wait_ge(s_down, U * i + (u + 2))
                            dve.wait_ge(s_st[(u - 1) % 2], 8 * U * i + 16 * ((u - 1) // 2 + 1))
                            dve.tensor_copy(y[(u - 1) % 2][:], ps_y[(u - 1) % 2][:, 0:D]).then_inc(s_y, 1)


def combine_top2(nc, g, x, m, y_dram, stats):
    RING = 8
    with ExitStack() as c:
        tb = lambda n, s, d=F32: c.enter_context(nc.sbuf_tensor(n, s, d, allow_name_mangling=True))
        rows = [tb(f"rows_m{u}", [P, D]) for u in range(RING)]
        cw_turned = tb("cw_turned", [EXPERTS, NT, P])
        ps = [c.enter_context(nc.psum_tensor(f"ps_b{j}", [P, 512], F32, allow_name_mangling=True)) for j in range(4)]
        sem = g.semaphores(c)
        s_turn, s_turned, s_bias, s_bias_in, s_used = map(sem, ("s_turn", "s_turned", "s_bias", "s_bias_in", "s_used"))
        s_rows = [sem(f"s_rows{u}") for u in range(RING)]
        TG = -(-NT // 4)
        order = [(i, tile) for t in range(NT + 1) for i, tile in ((0, t), (1, t - 1)) if 0 <= tile < NT]
        with nc.Block() as block:
            @block.gpsimd
            def _(pool):
                for n, (i, tile) in enumerate(order):
                    if n >= RING:
                        pool.wait_ge(s_used, n - RING + 1)
                    pool.indirect_dma_start(out=rows[n % RING][:], out_offset=None, in_=y_dram,
                                            in_offset=bass.IndirectOffsetOnAxis(ap=m.take[:, i, tile:tile + 1], axis=0)
                                            ).then_inc(s_rows[n % RING], 16)

            @block.tensor
            def _(pe):
                for q in range(TG):
                    if q >= 4:
                        pe.wait_ge(s_turned, q - 3)
                    for t in range(4 * q, min(NT, 4 * q + 4)):
                        mm = pe.transpose(ps[q % 4][0:EXPERTS, (t % 4) * P:(t % 4 + 1) * P], m.cw[:, t, :], g.ident[:])
                    mm.then_inc(s_turn, 1)
                pe.wait_ge(s_turned, TG)
                for t in range(NT):
                    if t >= 4:
                        pe.wait_ge(s_bias_in, t - 3)
                    pe.matmul(ps[t % 4][:, 0:D], cw_turned[:, t, :], m.b2[:], start=True, stop=True).then_inc(s_bias, 1)

            @block.scalar
            def _(act):
                for q in range(TG):
                    n = min(NT, 4 * q + 4) - 4 * q
                    act.wait_ge(s_turn, q + 1)
                    act.activation(cw_turned[:, 4 * q:4 * q + n, :].rearrange("e t n -> e (t n)"), ps[q % 4][0:EXPERTS, 0:n * P], ACT.Copy).then_inc(s_turned, 1)

            @block.vector
            def _(dve):
                for t in range(NT):
                    dve.wait_ge(s_bias, t + 1)
                    dve.tensor_tensor(x[:, t, :], ps[t % 4][:, 0:D], x[:, t, :], ALU.add).then_inc(s_bias_in, 1)
                dve.wait_ge(s_bias_in, NT)
                for n, (i, tile) in enumerate(order):
                    dve.wait_ge(s_rows[n % RING], 16 * (n // RING + 1))
                    if i == 1:
                        dve.wait_ge(s_used, order.index((0, tile)) + 1)
                    dve.scalar_tensor_tensor(x[:, tile, :], rows[n % RING][:], m.factor[:, i, tile:tile + 1], x[:, tile, :],
                                             ALU.mult, ALU.add).then_inc(s_used, 1)
                    for done in [tile - 1] * (i == 1 and tile > 0) + [tile] * (n == 2 * NT - 1):
                        dve.wait_ge(s_used, order.index((1, done)) + 1)
                        dve.bn_stats(stats[:, done, :], x[:, done, :])


def route(nc, g, probs, xn, rows_dram, weights, ctx):
    sb = lambda n, s, d=F32: ctx.enter_context(nc.sbuf_tensor(n, s, d, allow_name_mangling=True))
    take = sb("take", [P, NT], I32)
    factor = sb("factor", [P, NT])
    with ExitStack() as c:
        tb = lambda n, s, d=F32: c.enter_context(nc.sbuf_tensor(n, s, d, allow_name_mangling=True))
        hot = tb("hot_r", [P, NT, EXPERTS])
        w = tb("w_route", [P, 8, NT])
        tot = tb("tot", [P, EXPERTS, NT])
        run = tb("run_r", [P, EXPERTS, NT])
        rank = tb("rank_r", [P, NT, EXPERTS])
        put = tb("put", [P, NT], I32)
        ps = c.enter_context(nc.psum_tensor("route_ps", [P, 2, 512], F32, allow_name_mangling=True))
        sem = g.semaphores(c)
        s_number, s_chain, s_hot, s_ranks, s_put, s_sent = map(sem, ("s_number", "s_chain", "s_hot", "s_ranks", "s_put", "s_sent"))
        best, spare, number, valid, place, expert, kept, spot = (w[:, i] for i in range(8))
        shape = [P, NT, EXPERTS]
        with nc.Block() as block:
            @block.sync
            def _(sp):
                for j in range(2):
                    weights.load(sp, j, j)

            @block.gpsimd
            def _(pool):
                pool.iota(number, [[P, NT]], base=0, channel_multiplier=1, allow_small_or_imprecise_dtypes=True).then_inc(s_number, 1)
                pool.wait_ge(s_put, 1)
                for t in range(NT):
                    pool.indirect_dma_start(out=rows_dram, out_offset=bass.IndirectOffsetOnAxis(ap=put[:, t:t + 1], axis=0),
                                            in_=xn[:, t, :], in_offset=None).then_inc(s_sent, 16)
                pool.wait_ge(s_sent, 16 * NT)

            @block.tensor
            def _(pe):
                pe.wait_ge(s_hot, 1)
                rows = hot[:].rearrange("p t e -> p (t e)")
                pe.matmul(ps[:, 0, 0:NT * EXPERTS], g.before[:], rows, start=True, stop=True)
                pe.matmul(ps[:, 1, 0:NT * EXPERTS], g.ones[:], rows, start=True, stop=True).then_inc(s_ranks, 1)

            @block.vector
            def _(dve):
                ch = Chain(dve, s_chain)
                first_largest(dve, ch, g, probs[:], best, hot[:], spare)
                dve.wait_ge(s_number, 1)
                ch.link(dve.tensor_scalar(valid, number, float(N), None, ALU.is_lt))
                ch.link(dve.tensor_tensor(hot[:], hot[:], valid.unsqueeze(2).to_broadcast(shape), ALU.mult))
                dve.sem_inc(s_hot, 1)
                dve.wait_ge(s_ranks, 1)
                ch.link(dve.tensor_copy(tot[:], ps[:, 1, 0:NT * EXPERTS].rearrange("p (t e) -> p e t", e=EXPERTS)))
                for e in range(EXPERTS):
                    last = dve.tensor_tensor_scan(run[:, e, :], g.ones[:, 0:NT], tot[:, e, :], 0.0, ALU.mult, ALU.add)
                ch.link(last)
                ch.link(dve.tensor_tensor(run[:], run[:], tot[:], ALU.subtract))
                ch.link(dve.tensor_tensor(rank[:], ps[:, 0, 0:NT * EXPERTS].rearrange("p (t e) -> p t e", e=EXPERTS),
                                          run[:].rearrange("p e t -> p t e"), ALU.add))
                ch.link(dve.tensor_tensor(rank[:], rank[:], hot[:], ALU.mult))
                ch.link(dve.tensor_reduce(place, rank[:], AX.X, ALU.add))
                ch.link(dve.tensor_tensor(rank[:], hot[:], g.iota25[:, 0:EXPERTS].unsqueeze(1).to_broadcast(shape), ALU.mult))
                ch.link(dve.tensor_reduce(expert, rank[:], AX.X, ALU.add))
                ch.link(dve.tensor_scalar(kept, place, float(CAP), None, ALU.is_lt))
                ch.link(dve.tensor_tensor(kept, kept, valid, ALU.mult))
                ch.link(dve.tensor_tensor(factor[:], best, kept, ALU.mult))
                ch.link(dve.tensor_scalar(expert, expert, float(CAPP), None, ALU.mult))
                ch.link(dve.tensor_scalar(spare, place, float(CAP - 1), None, ALU.min))
                ch.link(dve.tensor_tensor(take[:], spare, expert, ALU.add))
                ch.link(dve.tensor_tensor(spot, place, expert, ALU.add))
                ch.link(dve.tensor_scalar(number, number, float(EXPERTS * CAPP), None, ALU.add))
                ch.link(dve.tensor_tensor(spot, spot, number, ALU.subtract))
                ch.link(dve.tensor_tensor(spot, spot, kept, ALU.mult))
                ch.link(dve.tensor_tensor(put[:], spot, number, ALU.add))
                dve.sem_inc(s_put, 1)
    return take, factor


class ExpertWeights:

    def __init__(self, nc, g, w1, w2, b2, ctx):
        tb = lambda n, s: ctx.enter_context(nc.sbuf_tensor(n, s, F32, allow_name_mangling=True))
        self.w1, self.w2, self.b2 = w1, w2, b2
        self.up = [tb(f"up_w{j}", [P, KC, F2]) for j in range(2)]
        self.down = [tb(f"down_w{j}", [P, F2 // P, D]) for j in range(2)]
        self.bias = [tb(f"b2_row{j}", [P, D]) for j in range(2)]
        sem = g.semaphores(ctx)
        self.s_loaded = [sem("s_weights0"), sem("s_weights1")]

    def load(self, sp, e, j):
        sp.dma_start(self.up[j][:], self.w1[bass.ds(e, 1)].rearrange("o (k p) f -> p (o k) f", p=P)).then_inc(self.s_loaded[j], 16)
        sp.dma_start(self.down[j][:], self.w2[bass.ds(e, 1)].rearrange("o (k p) f -> p (o k) f", p=P)).then_inc(self.s_loaded[j], 16)
        sp.dma_start(self.bias[j][:], self.b2[bass.ds(e, 1)].to_broadcast([P, D])).then_inc(self.s_loaded[j], 16)


def expert_layers(nc, g, weights, rows_dram, y_dram, b1):
    FC = F2 // P
    RT = CAPP // P
    with ExitStack() as c:
        tb = lambda n, s, d=F32: c.enter_context(nc.sbuf_tensor(n, s, d, allow_name_mangling=True))
        b1_all = bias_columns(nc, g, b1, FC, c)
        xin = [tb(f"xin{j}", [P, RT, D]) for j in range(2)]
        xt = [tb(f"xt{j}", [P, KC, CAPP]) for j in range(2)]
        hid = [tb(f"hidden{j}", [P, FC, CAPP]) for j in range(2)]
        y = [tb(f"y{j}", [P, RT, D]) for j in range(2)]
        bank = lambda n: c.enter_context(nc.psum_tensor(n, [P, 512], F32, allow_name_mangling=True))
        ps_t = [bank(f"ps_t{k}") for k in range(KC)]
        ps_h = [bank(f"ps_u{k}") for k in range(4)]
        ps_y = [bank(f"ps_v{k}") for k in range(2)]
        sem = g.semaphores(c)
        s_act, s_turn, s_turned, s_up, s_hid, s_y, s_out_y = map(sem, ("s_act", "s_turn", "s_turned", "s_up", "s_hid", "s_y", "s_out_y"))
        s_xin = [sem("s_xin0"), sem("s_xin1")]
        s_st = [sem("s_st0"), sem("s_st1")]
        PAIRS = EXPERTS // 2
        with nc.Block() as block:
            @block.sync
            def _(sp):
                def rows(i, j):
                    sp.wait_ge(s_turn, 2 * KC * i + KC * (j + 1))
                    sp.dma_start(xin[j][:], rows_dram[bass.ds((2 * i + j) * CAPP, CAPP)].rearrange("(t p) d -> p t d", p=P)).then_inc(s_xin[j], 16)

                for j in range(2):
                    rows(0, j)
                with sp.Fori(1, PAIRS) as i:
                    for j in range(2):
                        rows(i, j)
                        sp.wait_ge(s_out_y, 2 * RT * i + (RT * (j - 1) + 2))
                        weights.load(sp, 2 * i + j, j)

            @block.tensor
            def _(pe):
                pe.sem_inc(s_turn, 2 * KC)
                pe.sem_inc(s_y, 2 * RT)

                def turn(i, j):
                    pe.wait_ge(s_xin[j], 16 * i + 16)
                    pe.wait_ge(s_turned, 2 * KC * i + KC * (j + 1))
                    for k in range(KC):
                        for t in range(RT):
                            mm = pe.transpose(ps_t[k][:, t * P:(t + 1) * P], xin[j][:, t, k * P:(k + 1) * P], g.ident[:])
                        mm.then_inc(s_turn, 1)

                def up(i, j):
                    pe.wait_ge(weights.s_loaded[j], 48 * i + 48)
                    pe.wait_ge(s_turned, 2 * KC * i + KC * (j + 2))
                    for f in range(FC):
                        pe.wait_ge(s_hid, 2 * FC * i + (FC * j + f + 1))
                        for k in range(KC):
                            mm = pe.matmul(ps_h[f % 4][:], weights.up[j][:, k, f * P:(f + 1) * P], xt[j][:, k, :], start=(k == 0), stop=(k == KC - 1))
                        mm.then_inc(s_up, 1)

                def down(i, j):
                    for t in range(RT):
                        pe.wait_ge(s_out_y, 2 * RT * i + (RT * j + t + 1))
                        for f in range(FC):
                            if t == 0:
                                pe.wait_ge(s_hid, 2 * FC * i + (FC * j + f + 5))
                            mm = pe.matmul(ps_y[t % 2][:, 0:D], hid[j][:, f, t * P:(t + 1) * P], weights.down[j][:, f, :], start=(f == 0), stop=(f == FC - 1))
                        mm.then_inc(s_y, 1)

                def experts(i, last):
                    up(i, 0)
                    turn(i, 1)
                    down(i, 0)
                    up(i, 1)
                    if not last:
                        turn(i + 1, 0)
                    down(i, 1)

                turn(0, 0)
                with pe.Fori(0, PAIRS - 1) as i:
                    experts(i, False)
                experts(PAIRS - 1, True)

            @block.scalar
            def _(act):
                act.sem_inc(s_hid, 4)
                with act.Fori(0, PAIRS) as i:
                    for j in range(2):
                        act.wait_ge(s_y, 2 * RT * i + RT * (j + 1))
                        for f in range(FC):
                            act.wait_ge(s_up, 2 * FC * i + (FC * j + f + 1))
                            act.sem_inc(s_act, 1)
                            act.activation(hid[j][:, f, :], ps_h[f % 4][:], ACT.Relu,
                                           bias=b1_all[:, bass.ds(2 * i + j, 1), f:f + 1].rearrange("p o f -> p (o f)")).then_inc(s_hid, 1)
                        act.wait_ge(s_out_y, 2 * RT * i + (RT * (j + 1) + 2))
                        act.dma_start(y_dram[bass.ds((2 * i + j) * CAPP, CAPP)].rearrange("(t p) d -> p t d", p=P), y[j][:]).then_inc(s_st[j], 16)
                for j in range(2):
                    act.wait_ge(s_st[j], 16 * (PAIRS + 1))

            @block.vector
            def _(dve):
                dve.sem_inc(s_turned, KC)
                dve.sem_inc(s_out_y, 2)
                for j in range(2):
                    dve.sem_inc(s_st[j], 16)

                def rows(i, j):
                    dve.wait_ge(s_y, 2 * RT * i + RT * (j + 1))
                    for k in range(KC):
                        dve.wait_ge(s_turn, 2 * KC * i + (KC * (j + 2) + k + 1))
                        dve.tensor_copy(xt[j][:, k, :], ps_t[k][:]).then_inc(s_turned, 1)

                def output(i, j):
                    dve.wait_ge(s_st[j], 16 * i + 16)
                    for t in range(RT):
                        dve.wait_ge(s_y, 2 * RT * i + (RT * (j + 2) + t + 1))
                        dve.tensor_tensor(y[j][:, t, :], ps_y[t % 2][:, 0:D], weights.bias[j][:], ALU.add).then_inc(s_out_y, 1)

                rows(0, 0)
                with dve.Fori(0, PAIRS - 1) as i:
                    rows(i, 1)
                    output(i, 0)
                    rows(i + 1, 0)
                    output(i, 1)
                rows(PAIRS - 1, 1)
                output(PAIRS - 1, 0)
                output(PAIRS - 1, 1)


def combine(nc, g, x, y_dram, take, factor, out):
    BT = 5
    TOP = 3.4028234e38
    with ExitStack() as c:
        tb = lambda n, s, d=F32: c.enter_context(nc.sbuf_tensor(n, s, d, allow_name_mangling=True))
        rows = [tb(f"rows_c{j}", [P, BT, D]) for j in range(2)]
        add = [tb(f"add_c{j}", [P, BT, D]) for j in range(2)]
        over = tb("over", [P, BT, D])
        finite = tb("finite", [P, BT, D], U8)
        sem = g.semaphores(c)
        s_scaled, s_chain, s_added = map(sem, ("s_scaled", "s_chain", "s_added"))
        s_out = [sem("s_out0"), sem("s_out1")]
        s_rows = [sem("s_rows0"), sem("s_rows1")]
        with nc.Block() as block:
            @block.gpsimd
            def _(pool):
                for t in range(NT):
                    b = t // BT
                    if t % BT == 0 and b >= 2:
                        pool.wait_ge(s_added, b - 1)
                    pool.indirect_dma_start(out=rows[b % 2][:, t % BT, :], out_offset=None, in_=y_dram,
                                            in_offset=bass.IndirectOffsetOnAxis(ap=take[:, t:t + 1], axis=0)).then_inc(s_rows[b % 2], 16)

            @block.scalar
            def _(act):
                for t in range(NT):
                    b, r = t // BT, rows[t // BT % 2][:, t % BT, :]
                    if t % BT == 0:
                        act.wait_ge(s_rows[b % 2], 16 * BT * (b // 2 + 1))
                    act.activation(r, r, ACT.Copy, scale=factor[:, t:t + 1]).then_inc(s_scaled, 1)

            @block.vector
            def _(dve):
                ch = Chain(dve, s_chain)
                for b in range(NT // BT):
                    r, a, mine = rows[b % 2], add[b % 2], x[:, b * BT:(b + 1) * BT, :]
                    if b >= 2:
                        dve.wait_ge(s_out[b % 2], 16 * (b // 2))
                    dve.wait_ge(s_scaled, BT * (b + 1))
                    dve.tensor_scalar(finite[:], r[:], 0.0, 0.0, ALU.mult, ALU.is_equal)
                    ch.link(dve.tensor_scalar(over[:], r[:], TOP, None, ALU.is_gt))
                    ch.link(dve.scalar_tensor_tensor(over[:], r[:], -TOP, over[:], ALU.is_lt, ALU.subtract))
                    dve.scalar_tensor_tensor(a[:], over[:], -1e4, mine, ALU.mult, ALU.add)
                    ch.link(dve.tensor_tensor(r[:], r[:], mine, ALU.add))
                    ch.link(dve.copy_predicated(a[:], finite[:], r[:]))
                    dve.sem_inc(s_added, 1)

            @block.sync
            def _(sp):
                for b in range(NT // BT):
                    sp.wait_ge(s_added, b + 1)
                    last = b == NT // BT - 1
                    n = BT - 1 if last else BT
                    r = b * BT * P
                    sp.dma_start(out[r:r + n * P].rearrange("(t p) d -> p t d", p=P), add[b % 2][:, 0:n, :]).then_inc(s_out[b % 2], 16)
                    if last:
                        sp.dma_start(out[r + n * P:N], add[b % 2][0:N - r - n * P, n, :]).then_inc(s_out[b % 2], 16)
                for j in range(2):
                    sp.wait_ge(s_out[j], 16 * len(range(j, NT // BT, 2)) + 16 * ((NT // BT - 1) % 2 == j))


def attention_layer(nc, g, name, norm, x_in, weights, heads, dst, visits, x_out, pairs, ctx):
    W, a_src, a_dst, bias = weights
    C = heads
    with ExitStack() as layer:
        seg = Segments(nc, g, dst, C, layer)
        if norm:
            h, al, table, al_dram = project(nc, g, name, x_in, True, None, W, (a_src, a_dst), C, seg, pairs[0], "right", ctx)
        else:
            h, al, table, al_dram = project(nc, g, name, x_in, False, None, W, (a_src, a_dst), C, None, pairs[0], "left", layer)
            ctx.close()
        with ExitStack() as left:
            ae = expand(nc, g, name, al, al_dram, C, pairs[1], left)
            ext = edge_softmax(nc, g, name, ae, seg, not norm, C, pairs[2], ctx)
        acc = ctx.enter_context(nc.sbuf_tensor(name + "_acc", [P, NT + 1, D + 2 * C + 1], F32, side="right"))
        aggregate(nc, g, name, table, g.src_idx, visits, ext, C, 2 * C + 1, None, acc)
        finish_attention(nc, g, acc, h, al, bias, C, x_out)
    return acc


def build(nc, x, src, dst, edge_weight, L0_gnn_W1, L0_gnn_a_src1, L0_gnn_a_dst1, L0_gnn_b1, L0_gnn_W2, L0_gnn_a_src2,
          L0_gnn_a_dst2, L0_gnn_b2, L0_ffn_gate_w, L0_ffn_gate_b, L0_ffn_W1, L0_ffn_b1, L0_ffn_W2, L0_ffn_b2, L1_gnn_W,
          L1_gnn_b, L1_ffn_gate_w, L1_ffn_gate_b, L1_ffn_w1, L1_ffn_b1, L1_ffn_w2, L1_ffn_b2, out):
    g = Graph(nc)
    rows_dram = nc.dram_tensor("rows_dram", (ST * P + NP + P, D), F32, kind="Internal").ap()
    y_dram = nc.dram_tensor("y_dram", (ST * P, D), F32, kind="Internal").ap()
    with ExitStack() as keep:
        constants(nc, g, keep)
        xs = keep.enter_context(nc.sbuf_tensor("x_nodes", [P, NT, D], F32))
        graph_tables(nc, g, src, dst, edge_weight, x, xs, keep)
        (to_dst, minus_dst, _, _), (to_src, minus_src, ends, part) = visit_tables(nc, g, (g.dst_key, g.src_key), keep)
        stats = keep.enter_context(nc.sbuf_tensor("stats_gcn", [P, NT, 6], F32))
        g.spot = keep.enter_context(nc.sbuf_tensor("spot", [P, ET], I32))
        with ExitStack() as before:
            hot_src = high_parts(nc, "hot_src", g, g.src_key, before)
            by_source(nc, g, hot_src, ends, part, rows_dram)
        with ExitStack() as right:
            acc = attention_layer(nc, g, "gat1", True, xs, (L0_gnn_W1, L0_gnn_a_src1, L0_gnn_a_dst1, L0_gnn_b1), HEADS,
                                  dst, (to_dst, minus_dst), None, (2, 0, 2), right)
            attention_layer(nc, g, "gat2", False, acc[:, 0:NT, 0:D], (L0_gnn_W2, L0_gnn_a_src2, L0_gnn_a_dst2, L0_gnn_b2), 1,
                            dst, (to_dst, minus_dst), xs, (1, 5, 2), right)
        with ExitStack() as left:
            xn = left.enter_context(nc.sbuf_tensor("ffn0_xn", [P, NT, D], F32))
            probs = left.enter_context(nc.sbuf_tensor("ffn0_probs", [P, NT, EXPERTS], F32))
            normalise_and_gate(nc, g, xs, None, xn, probs, L0_ffn_gate_w, L0_ffn_gate_b, 1)
            mix = route_top2(nc, g, probs, xn, rows_dram, L0_ffn_W1, L0_ffn_W2, L0_ffn_b2, left)
            expert_tiles(nc, g, mix, rows_dram, y_dram, L0_ffn_b1, ET // (2 * GROUP) - g.sent)
            combine_top2(nc, g, xs, mix, y_dram, stats)
        with ExitStack() as left:
            xn = left.enter_context(nc.sbuf_tensor("ffn1_xn", [P, NT, D], F32))
            probs = left.enter_context(nc.sbuf_tensor("ffn1_probs", [P, NT, EXPERTS], F32))
            with ExitStack() as gcn:
                l_idx, l_values = read_list(nc, g, gcn)
                _, _, table, _ = project(nc, g, "gcn", xs, True, stats, L1_gnn_W, None, 1, None, 0, "right", gcn)
                acc = gcn.enter_context(nc.sbuf_tensor("gcn_acc", [P, NT + 1, D], F32, side="right"))
                aggregate(nc, g, "gcn", table, l_idx, (to_src, minus_src), l_values, 1, 0, L1_gnn_b, acc)
                normalise_and_gate(nc, g, xs, acc, xn, probs, L1_ffn_gate_w, L1_ffn_gate_b, 0)
            weights = ExpertWeights(nc, g, L1_ffn_w1, L1_ffn_w2, L1_ffn_b2, left)
            take, factor = route(nc, g, probs, xn, rows_dram, weights, left)
            expert_layers(nc, g, weights, rows_dram, y_dram, L1_ffn_b1)
            combine(nc, g, xs, y_dram, take, factor, out)


_INS = ["x", "src", "dst", "edge_weight", "L0_gnn_W1", "L0_gnn_a_src1", "L0_gnn_a_dst1", "L0_gnn_b1", "L0_gnn_W2", "L0_gnn_a_src2",
        "L0_gnn_a_dst2", "L0_gnn_b2", "L0_ffn_gate_w", "L0_ffn_gate_b", "L0_ffn_W1", "L0_ffn_b1", "L0_ffn_W2", "L0_ffn_b2", "L1_gnn_W",
        "L1_gnn_b", "L1_ffn_gate_w", "L1_ffn_gate_b", "L1_ffn_w1", "L1_ffn_b1", "L1_ffn_w2", "L1_ffn_b2"]
_OUTS = [((N, D), "float32")]


def kernel(**inputs):
    import numpy as _np
    import concourse.bacc as _bacc
    from concourse import mybir as _mybir
    from concourse.bass_utils import run_bass_kernel_spmd as _run

    nc = _bacc.Bacc("TRN2", target_bir_lowering=False, num_devices=1)
    arrays, args = {}, []
    for name in _INS:
        a = _np.ascontiguousarray(inputs[name])
        arrays[f"in_{name}_dram"] = a
        args.append(nc.dram_tensor(f"in_{name}_dram", a.shape, _mybir.dt.from_np(a.dtype), kind="ExternalInput").ap())
    for i, (shape, dtype) in enumerate(_OUTS):
        dt = _mybir.dt.from_np(_np.dtype(dtype))
        args.append(nc.dram_tensor(f"out_{i}_dram", shape, dt, kind="ExternalOutput").ap())
    build(nc, *args)
    r = _run(nc, [arrays], core_ids=[0])
    return r.results[0]["out_0_dram"]
```
